# Optimizing a Trainium2 kernel written in Bass

```python
import numpy as np
import jax
import jax.numpy as jnp

def _softmax(x, axis=-1):
    return jax.nn.softmax(x, axis=axis)

def _gelu(x):
    return jax.nn.gelu(x, approximate=True)

def _silu(x):
    return jax.nn.silu(x)

def _sigmoid(x):
    return jax.nn.sigmoid(x)

def _layernorm(x, axis=-1, eps=1e-05):
    m = jnp.mean(x, axis=axis, keepdims=True)
    v = jnp.var(x, axis=axis, keepdims=True)
    return (x - m) / jnp.sqrt(v + eps)

def _scatter_add(tgt, idx, src, axis=0):
    return tgt.at[idx].add(src)

def _segment_sum(src, seg, n):
    return jax.ops.segment_sum(src, seg, n)
kernel_name = 'mk_hybrid_d1_jaxref_r4_aa28af'

def setup_inputs(seed: int=0):
    np.random.seed(seed)
    _w = jnp.asarray

    def _L0_attn_a_setup():
        import jax, jax.numpy as jnp
        import numpy as np
        B, L, D = (2, 512, 256)
        H, P = (16, 3)
        HD = D // H
        DH = D // 2
        key = jax.random.key(seed)
        ks = jax.random.split(key, 18)
        s = 0.02
        inp = {'x': jax.random.normal(ks[0], (B, L, D), jnp.float32), 'wq': jax.random.normal(ks[1], (D, D), jnp.float32) * s, 'bq': jnp.zeros((D,), jnp.float32), 'wk': jax.random.normal(ks[2], (D, D), jnp.float32) * s, 'bk': jnp.zeros((D,), jnp.float32), 'wv': jax.random.normal(ks[3], (D, D), jnp.float32) * s, 'bv': jnp.zeros((D,), jnp.float32), 'wo': jax.random.normal(ks[4], (D, D), jnp.float32) * s, 'bo': jnp.zeros((D,), jnp.float32), 'pw1': jax.random.normal(ks[5], (P, DH, D), jnp.float32) * s, 'pb1': jnp.zeros((P, DH), jnp.float32), 'pw2': jax.random.normal(ks[6], (P, H, DH), jnp.float32) * s, 'pb2': jnp.zeros((P, H), jnp.float32), 'sw1': jax.random.normal(ks[7], (DH, D), jnp.float32) * s, 'sb1': jnp.zeros((DH,), jnp.float32), 'sw2': jax.random.normal(ks[8], (P, DH), jnp.float32) * s, 'sb2': jnp.zeros((P,), jnp.float32)}
        return inp
    _L0_attn_a_in = _L0_attn_a_setup()

    def _L0_attn_b_setup():
        import jax, jax.numpy as jnp
        import numpy as np
        NUM_HEADS = 16
        HIDDEN = 256
        HEAD = HIDDEN // NUM_HEADS
        key = jax.random.key(seed)
        k1, k2 = jax.random.split(key)
        embeddings = jax.random.normal(k1, (4, 512, HIDDEN), dtype=jnp.float32)
        w_qkv = jax.random.normal(k2, (HIDDEN, 3 * HIDDEN), dtype=jnp.float32) * (1.0 / np.sqrt(HIDDEN))
        return {'embeddings': embeddings, 'w_qkv': w_qkv}
    _L0_attn_b_in = _L0_attn_b_setup()

    def _L0_ffn_setup():
        import jax, jax.numpy as jnp
        import numpy as np
        CAPACITY_FACTOR = 0.5
        key = jax.random.key(seed)
        ks = jax.random.split(key, 5)
        B, S, D, F = (4, 1024, 256, 1024)
        scale_in = 1.0 / np.sqrt(D)
        scale_ff = 1.0 / np.sqrt(F)
        return {'hidden_states': jax.random.normal(ks[0], (B, S, D), dtype=jnp.float32), 'w_router': jax.random.normal(ks[1], (D,), dtype=jnp.float32) * scale_in, 'W1': jax.random.normal(ks[2], (D, F), dtype=jnp.float32) * scale_in, 'b1': jnp.zeros((F,), dtype=jnp.float32), 'W2': jax.random.normal(ks[3], (F, D), dtype=jnp.float32) * scale_ff, 'b2': jnp.zeros((D,), dtype=jnp.float32)}
    _L0_ffn_in = _L0_ffn_setup()
    _d = {'L0_attn_a_x': _L0_attn_a_in['x'], 'L0_attn_a_wq': _L0_attn_a_in['wq'], 'L0_attn_a_bq': _L0_attn_a_in['bq'], 'L0_attn_a_wk': _L0_attn_a_in['wk'], 'L0_attn_a_bk': _L0_attn_a_in['bk'], 'L0_attn_a_wv': _L0_attn_a_in['wv'], 'L0_attn_a_bv': _L0_attn_a_in['bv'], 'L0_attn_a_wo': _L0_attn_a_in['wo'], 'L0_attn_a_bo': _L0_attn_a_in['bo'], 'L0_attn_a_pw1': _L0_attn_a_in['pw1'], 'L0_attn_a_pb1': _L0_attn_a_in['pb1'], 'L0_attn_a_pw2': _L0_attn_a_in['pw2'], 'L0_attn_a_pb2': _L0_attn_a_in['pb2'], 'L0_attn_a_sw1': _L0_attn_a_in['sw1'], 'L0_attn_a_sb1': _L0_attn_a_in['sb1'], 'L0_attn_a_sw2': _L0_attn_a_in['sw2'], 'L0_attn_a_sb2': _L0_attn_a_in['sb2'], 'L0_attn_b_w_qkv': _L0_attn_b_in['w_qkv'], 'L0_ffn_w_router': _L0_ffn_in['w_router'], 'L0_ffn_W1': _L0_ffn_in['W1'], 'L0_ffn_b1': _L0_ffn_in['b1'], 'L0_ffn_W2': _L0_ffn_in['W2'], 'L0_ffn_b2': _L0_ffn_in['b2']}
    _x0 = _d['L0_attn_a_x']
    _d['L0_attn_a_x'] = jax.random.normal(jax.random.fold_in(jax.random.key(seed), 1), (8, 1024, 256), dtype=_x0.dtype)
    del _x0
    return _d

def reference(L0_attn_a_x, L0_attn_a_wq, L0_attn_a_bq, L0_attn_a_wk, L0_attn_a_bk, L0_attn_a_wv, L0_attn_a_bv, L0_attn_a_wo, L0_attn_a_bo, L0_attn_a_pw1, L0_attn_a_pb1, L0_attn_a_pw2, L0_attn_a_pb2, L0_attn_a_sw1, L0_attn_a_sb1, L0_attn_a_sw2, L0_attn_a_sb2, L0_attn_b_w_qkv, L0_ffn_w_router, L0_ffn_W1, L0_ffn_b1, L0_ffn_W2, L0_ffn_b2):

    def _L0_attn_a_ref(x, wq, bq, wk, bk, wv, bv, wo, bo, pw1, pb1, pw2, pb2, sw1, sb1, sw2, sb2):
        import jax, jax.numpy as jnp
        import numpy as np
        B, L, D = (2, 512, 256)
        H, P = (16, 3)
        HD = D // H
        DH = D // 2
        b, l, d = x.shape
        h = pw2.shape[1]
        hd = d // h
        scale = jnp.sqrt(jnp.asarray(hd, x.dtype))
        Q = (x @ wq.T + bq).reshape(b, l, h, hd).transpose(0, 2, 1, 3)
        K = (x @ wk.T + bk).reshape(b, l, h, hd).transpose(0, 2, 1, 3)
        V = (x @ wv.T + bv).reshape(b, l, h, hd).transpose(0, 2, 1, 3)
        scores = jnp.einsum('bhqd,bhkd->bhqk', Q, K) / scale
        causal = jnp.triu(jnp.ones((l, l), bool), 1)
        scores = jnp.where(causal[None, None], jnp.asarray(-1000000000.0, x.dtype), scores)
        xm = x.mean(axis=1)
        policy_w = jax.nn.softmax(jax.nn.gelu(xm @ sw1.T + sb1, approximate=False) @ sw2.T + sb2, axis=-1)
        hid = jax.nn.gelu(jnp.einsum('bd,pcd->bpc', xm, pw1) + pb1, approximate=False)
        gates = jax.nn.softmax(jnp.einsum('bpc,phc->bph', hid, pw2) + pb2, axis=-1)
        head_gates = jnp.einsum('bp,bph->bh', policy_w, gates)
        scores = scores * head_gates[:, :, None, None]
        attn = jax.nn.softmax(scores, axis=-1)
        out = jnp.einsum('bhqk,bhkd->bhqd', attn, V)
        out = out.transpose(0, 2, 1, 3).reshape(b, l, d)
        return out @ wo.T + bo

    def _L0_attn_b_ref(embeddings, w_qkv):
        import jax, jax.numpy as jnp
        import numpy as np
        NUM_HEADS = 16
        HIDDEN = 256
        HEAD = HIDDEN // NUM_HEADS
        b, s, h = embeddings.shape
        result = embeddings @ w_qkv
        result = result.reshape(b, s, 3, NUM_HEADS, HEAD)
        q = jnp.transpose(result[:, :, 0], (0, 2, 1, 3))
        k = jnp.transpose(result[:, :, 1], (0, 2, 1, 3))
        v = jnp.transpose(result[:, :, 2], (0, 2, 1, 3))
        scores = jnp.einsum('bnqd,bnkd->bnqk', q, k) / jnp.sqrt(jnp.float32(h))
        probs = jax.nn.softmax(scores, axis=-1)
        ctx = jnp.einsum('bnqk,bnkd->bnqd', probs, v)
        out = jnp.transpose(ctx, (0, 2, 1, 3)).reshape(b, s, h)
        return out

    def _L0_ffn_ref(hidden_states, w_router, W1, b1, W2, b2):
        import jax, jax.numpy as jnp
        import numpy as np
        CAPACITY_FACTOR = 0.5
        'Mixture-of-Depths block: route top-k tokens through an FFN inner block,\n            scatter back with sigmoid router weights; bypassed tokens pass through.'
        B, S, D = hidden_states.shape
        k = int(S * CAPACITY_FACTOR)
        scores = jnp.einsum('bsd,d->bs', hidden_states, w_router)
        top_scores, top_idx = jax.lax.top_k(scores, k)
        weights = jax.nn.sigmoid(top_scores)
        selected = jnp.take_along_axis(hidden_states, top_idx[:, :, None], axis=1)
        h = jax.nn.gelu(jnp.einsum('bkd,df->bkf', selected, W1) + b1)
        processed = jnp.einsum('bkf,fd->bkd', h, W2) + b2
        update = weights[:, :, None] * processed

        def scatter_one(xb, ib, ub):
            return xb.at[ib].add(ub)
        output = jax.vmap(scatter_one)(hidden_states, top_idx, update)
        return output
    x = L0_attn_a_x
    x = x + _L0_attn_a_ref(_layernorm(x, axis=-1), L0_attn_a_wq, L0_attn_a_bq, L0_attn_a_wk, L0_attn_a_bk, L0_attn_a_wv, L0_attn_a_bv, L0_attn_a_wo, L0_attn_a_bo, L0_attn_a_pw1, L0_attn_a_pb1, L0_attn_a_pw2, L0_attn_a_pb2, L0_attn_a_sw1, L0_attn_a_sb1, L0_attn_a_sw2, L0_attn_a_sb2)
    x = x + _L0_ffn_ref(_layernorm(x, axis=-1), L0_ffn_w_router, L0_ffn_W1, L0_ffn_b1, L0_ffn_W2, L0_ffn_b2)
    x = x + _L0_attn_b_ref(_layernorm(x, axis=-1), L0_attn_b_w_qkv)
    x = x + _L0_ffn_ref(_layernorm(x, axis=-1), L0_ffn_w_router, L0_ffn_W1, L0_ffn_b1, L0_ffn_W2, L0_ffn_b2)
    return x

_drawn_inputs = setup_inputs


def setup_inputs(seed=0):
    import zlib

    import numpy as np

    out = dict(_drawn_inputs(seed))
    spreads = {'L0_attn_a_bq': (0.0, 2.0),
     'L0_attn_a_bk': (0.0, 2.0),
     'L0_attn_a_bv': (0.0, 0.1),
     'L0_attn_a_bo': (0.0, 0.1),
     'L0_attn_a_pb1': (0.0, 0.8),
     'L0_attn_a_pb2': (0.0, 2.0),
     'L0_attn_a_sb1': (0.0, 2.0),
     'L0_attn_a_sb2': (0.0, 2.0),
     'L0_ffn_b1': (0.0, 0.316),
     'L0_ffn_b2': (0.0, 0.1)}
    factors = {'L0_attn_a_wq': 8.0,
     'L0_attn_a_wk': 8.0,
     'L0_attn_a_wv': 5.346,
     'L0_attn_a_pw1': 63.329,
     'L0_attn_a_pw2': 8.0,
     'L0_attn_a_sw1': 200.0,
     'L0_attn_a_sw2': 24.544}
    for name, (base, spread) in spreads.items():
        noise = np.random.default_rng([zlib.crc32(name.encode()), seed]).standard_normal(out[name].shape)
        drawn = base * np.exp(spread * noise) if base else spread * noise
        out[name] = jnp.asarray(drawn.astype(out[name].dtype))
    for name, factor in factors.items():
        out[name] = (out[name] * factor).astype(out[name].dtype)
    return out
```

```python
from contextlib import ExitStack

import concourse.bass as bass
from concourse import mybir

P = 128
F32 = mybir.dt.float32
BF16 = mybir.dt.bfloat16
ALU = mybir.AluOpType
ACT = mybir.ActivationFunctionType
AX_X = mybir.AxisListType.X

B, L, D = 8, 1024, 256
H, HD = 16, 16
T = L // P
KD = D // P
HALF = L // 2
TH = T // 2
NE, DH = 3, 128
F = 1024
FT = F // P
KEEP = L // 2
EPS = 1e-5
MASKED = -1.0e9
BLOCKED = -1.0e30
HP = 8
QH = 4
NPAIR = B * H // HP
SLOT = 32
ONE = HD
PARTS = 3
PRODUCTS = [(0, 0), (0, 1), (1, 0), (1, 1), (0, 2), (2, 0)]
KS = HD * len(PRODUCTS)


class Links:

    def __init__(self, eng, sem, base=0):
        self.eng, self.sem, self.base, self.n = eng, sem, base, 0

    def __call__(self, ins):
        self.n += 1
        ins.then_inc(self.sem, 1)
        self.eng.wait_ge(self.sem, self.base + self.n)


def wait_past(eng, sem, value):
    if not (isinstance(value, int) and value == 0):
        eng.wait_ge(sem, value)


def peel_first(eng, count, each):
    each(0)
    with eng.Fori(1, count) as b:
        each(b)


def norm_phase(nc, sem, C, tag, x_in=None, gates=None):
    xs = C.xs
    x_here, linked, stats, rstd, h_ready, filled, ht_ready, stored, ht_sent, bo_added = (
        sem(tag + n) for n in ("x_here", "linked", "stats", "rstd", "h_ready", "filled", "ht_ready",
                               "stored", "ht_sent", "bo_added"))
    with ExitStack() as ctx:
        def sb(name, shape, dt=F32):
            return ctx.enter_context(nc.sbuf_tensor(tag + name, shape, dt))
        h = sb("h", [P, T, D])
        st = sb("st", [P, T, 6])
        var = sb("var", [P, T])
        msum = sb("msum", [P, T])
        r0 = sb("r0", [P, T])
        lnv = sb("lnv", [P, T])
        t1 = sb("t1", [P, T])
        rs = sb("rs", [P, T])
        nmr = sb("nmr", [P, T])
        hts = sb("hts", [P, 2, KD, L])
        psT = ctx.enter_context(nc.psum_tensor(tag + "psT", [P, KD, L], F32))
        block = ctx.enter_context(nc.Block())

        @block.sync
        def _(sp):
            if x_in is not None:
                for b in range(B):
                    sp.dma_start(xs[:, b * T:(b + 1) * T, :],
                                 x_in[b].rearrange("(t p) d -> p t d", p=P)).then_inc(x_here, 16)
                    sp.wait_ge(x_here, b * 16 + 16)
            sp.sem_inc(ht_sent, 16)
            for b in range(B):
                sp.wait_ge(ht_ready, b * 2 + 2)
                sp.dma_start(C.ht_dram[b], hts[:, b % 2]).then_inc(ht_sent, 16)
                sp.wait_ge(ht_sent, b * 16 + 32)

        @block.vector
        def _(dve):
            def each(b):
                link = Links(dve, linked, b * 7)
                if x_in is not None:
                    dve.wait_ge(x_here, b * 16 + 16)
                for t in range(T):
                    ins = nc.vector.bn_stats(st[:, t, :], xs[:, b * T + t, :])
                link(ins)
                nc.vector.tensor_tensor(msum[:], st[:, :, 1], st[:, :, 4], ALU.add)
                nc.vector.tensor_tensor(t1[:], st[:, :, 1], st[:, :, 4], ALU.subtract)
                link(nc.vector.tensor_tensor(var[:], st[:, :, 2], st[:, :, 5], ALU.add))
                link(nc.vector.scalar_tensor_tensor(t1[:], t1[:], 0.25, t1[:], ALU.mult, ALU.mult))
                nc.vector.scalar_tensor_tensor(var[:], var[:], 1.0 / D, t1[:], ALU.mult, ALU.add).then_inc(stats, 1)
                dve.wait_ge(rstd, b + 1)
                dve.wait_ge(stats, b + 1)
                link(nc.vector.scalar_tensor_tensor(t1[:], r0[:], -0.5, r0[:], ALU.mult, ALU.mult))
                link(nc.vector.scalar_tensor_tensor(t1[:], var[:], EPS, t1[:], ALU.add, ALU.mult))
                link(nc.vector.scalar_tensor_tensor(rs[:], t1[:], 1.5, r0[:], ALU.add, ALU.mult))
                link(nc.vector.scalar_tensor_tensor(nmr[:], msum[:], -0.5, rs[:], ALU.mult, ALU.mult))
                wait_past(dve, filled, b * 4)
                for t in range(T):
                    nc.vector.tensor_scalar(h[:, t, :], xs[:, b * T + t, :], rs[:, t:t + 1], nmr[:, t:t + 1],
                                            ALU.mult, ALU.add).then_inc(h_ready, 1)
            peel_first(dve, B, each)

        @block.scalar
        def _(act):
            def each(b):
                act.wait_ge(stats, b + 1)
                nc.scalar.activation(lnv[:], var[:], ACT.Ln, bias=C.eps[:]).then_inc(stored, 1)
                act.wait_ge(stored, b + 1)
                nc.scalar.activation(r0[:], lnv[:], ACT.Exp, scale=-0.5).then_inc(rstd, 1)
                wait_past(act, ht_sent, b * 16)
                for k in range(KD):
                    act.wait_ge(filled, b * 4 + 2 * k + 2)
                    accum = None if gates is None else gates.xsum[:, k, bass.ts(b, 1)]
                    nc.scalar.activation(hts[:, b % 2, k, :], psT[:, k, :], ACT.Identity,
                                         accum_out=accum).then_inc(ht_ready, 1)
            peel_first(act, B, each)

        @block.tensor
        def _(pe):
            def each(b):
                for k in range(KD):
                    for half in range(2):
                        pe.wait_ge(h_ready, b * T + (half + 1) * TH)
                        if half == 0:
                            wait_past(pe, ht_ready, b * 2)
                        for i in range(TH):
                            t = half * TH + i
                            mm = nc.tensor.transpose(psT[:, k, t * P:(t + 1) * P], h[:, t, k * P:(k + 1) * P],
                                                     C.ident[:])
                        mm.then_inc(filled, 1)
            peel_first(pe, B, each)

        if x_in is not None:
            @block.gpsimd
            def _(pool):
                def each(b):
                    pool.wait_ge(h_ready, b * T + T)
                    nc.gpsimd.tensor_tensor(xs[:, bass.ts(b, T), :], xs[:, bass.ts(b, T), :],
                                            C.bo[:].unsqueeze(1).broadcast_to([P, T, D]),
                                            ALU.add).then_inc(bo_added, 1)
                peel_first(pool, B, each)


def constants_phase(nc, sem, C, dram):
    loaded, made, step = sem("c_loaded"), sem("c_made"), sem("c_step")
    with nc.Block() as block:
        @block.sync
        def _(sp):
            loads = [
                (C.bo[:], dram["bo"].partition_broadcast(P)),
                (C.woT[:], dram["woT"].rearrange("(m p) n -> p m n", p=P)),
                (C.bv[:], dram["bv"].partition_broadcast(P)),
                (C.wr[:], dram["wr"].partition_broadcast(P)),
                (C.b2[:], dram["b2"].partition_broadcast(P)),
                (C.b1[:], dram["b1"].rearrange("(f p) -> p f", p=P)),
            ]
            for dst, src in loads:
                sp.dma_start(dst, src, allow_slow_non_contiguous=True).then_inc(loaded, 16)
            sp.wait_ge(loaded, 16 * len(loads))

        @block.vector
        def _(dve):
            nc.vector.memset(C.eps[:], EPS).then_inc(made, 1)
            nc.vector.memset(C.ones[:], 1.0).then_inc(made, 1)
            nc.vector.memset(C.zerosb[:], 0.0).then_inc(made, 1)

        @block.gpsimd
        def _(pool):
            pool.wait_ge(made, 3)
            def keep(out, in_, op, fill, pattern, base, ch):
                return nc.gpsimd.affine_select(out=out, in_=in_, compare_op=op, fill=fill, base=base,
                                               pattern=pattern, channel_multiplier=ch)
            keep(C.ident[:], C.ones[:], ALU.is_equal, 0.0, [[-1, P]], 0, 1).then_inc(step, 1)
            pool.wait_ge(step, 1)
            nc.gpsimd.tensor_copy(C.identb[:], C.ident[:]).then_inc(step, 1)
            keep(C.tri[:], C.ones[:], ALU.is_gt, 0.0, [[-1, P]], 0, 1).then_inc(step, 1)
            keep(C.block_qk[:], C.zerosb[:], ALU.is_ge, BLOCKED, [[-1, P]], 0, 1).then_inc(step, 1)
            keep(C.block_kq[:], C.zerosb[:], ALU.is_ge, BLOCKED, [[1, P]], 0, -1).then_inc(step, 1)
            keep(C.lastrow[:], C.ones[:, 0:T], ALU.not_equal, 3.0e29, [[P, T]], 1 - L, 1).then_inc(step, 1)


def gates_phase(nc, sem, C, G, dram):
    loaded, mm_done, act_done, linked, g_out, g_in, ready = (
        sem("g_" + n) for n in ("loaded", "mm", "act", "linked", "out", "in", "ready"))
    NG = NE + 1
    with ExitStack() as ctx:
        def sb(name, shape, dt=F32):
            return ctx.enter_context(nc.sbuf_tensor("g_" + name, shape, dt))
        w1 = sb("w1", [P, KD, NG, DH])
        bias1 = sb("bias1", [P, NG])
        w2 = sb("w2", [P, NE * H + NE])
        bias2 = sb("bias2", [B, NE * H + NE])
        hid = sb("hid", [P, NG, B])
        lg = sb("lg", [B, NE * H + NE])
        mx = sb("mx", [B, NG])
        ex = sb("ex", [B, NE * H + NE])
        sm = sb("sm", [B, NG])
        hg = sb("hg", [B, H])
        bqc = sb("bqc", [P, KD])
        bkc = sb("bkc", [P, KD])
        ps1 = ctx.enter_context(nc.psum_tensor("g_ps1", [P, NG, B], F32))
        ps2 = ctx.enter_context(nc.psum_tensor("g_ps2", [P, NE * H + NE], F32))
        block = ctx.enter_context(nc.Block())
        experts = lambda t: t[:, 0:NE * H].rearrange("b (e h) -> b e h", e=NE)
        policy = lambda t: t[:, NE * H:NE * H + NE]

        @block.sync
        def _(sp):
            loads = [(w1[:], dram["gw1"].rearrange("(k p) g c -> p k g c", p=P)),
                     (bias1[:], dram["gb1"].rearrange("g c -> c g")),
                     (w2[:], dram["gw2"]), (bias2[:], dram["gb2"].partition_broadcast(B)),
                     (bqc[:], dram["bq"].rearrange("(m p) -> p m", p=P)),
                     (bkc[:], dram["bk"].rearrange("(m p) -> p m", p=P))]
            for dst, src in loads:
                sp.dma_start(dst, src, allow_slow_non_contiguous=True).then_inc(loaded, 16)
            sp.wait_ge(loaded, 16 * len(loads))
            sp.wait_ge(linked, G_LINKS)
            sp.dma_start(C.g_dram, hg[:]).then_inc(g_out, 16)
            sp.wait_ge(g_out, 16)
            sp.dma_start(G.gneg[:], C.g_dram.rearrange("b h -> (b h)").partition_broadcast(P)).then_inc(g_in, 16)
            for hh in range(HP):
                src = C.g_dram.rearrange("b (m h) -> h (b m)", m=KD)[hh]
                sp.dma_start(G.qscale[hh * HD:(hh + 1) * HD, :], src.partition_broadcast(HD),
                             allow_slow_non_contiguous=True).then_inc(g_in, 16)
            sp.wait_ge(g_in, 16 * (HP + 1))

        @block.tensor
        def _(pe):
            pe.wait_ge(loaded, 16 * 6)
            for g in range(NG):
                for k in range(KD):
                    mm = nc.tensor.matmul(ps1[:, g, :], w1[:, k, g, :], G.xsum[:, k, :],
                                          start=(k == 0), stop=(k == KD - 1))
            mm.then_inc(mm_done, 1)
            pe.wait_ge(act_done, NG)
            for e in range(NE):
                nc.tensor.matmul(ps2[0:B, e * H:(e + 1) * H], hid[:, e, :], w2[:, e * H:(e + 1) * H],
                                 start=True, stop=True)
            nc.tensor.matmul(policy(ps2[0:B]), hid[:, NE, :], policy(w2), start=True, stop=True).then_inc(mm_done, 1)

        @block.scalar
        def _(act):
            act.wait_ge(loaded, 16 * 6)
            act.wait_ge(mm_done, 1)
            for g in range(NG):
                nc.scalar.activation(hid[:, g, :], ps1[:, g, :], ACT.Gelu, bias=bias1[:, g:g + 1],
                                     scale=1.0 / L).then_inc(act_done, 1)
            act.wait_ge(linked, 3)
            nc.scalar.activation(ex[:], lg[:], ACT.Exp).then_inc(act_done, 1)

        @block.vector
        def _(dve):
            link = Links(dve, linked)
            dve.wait_ge(mm_done, 2)
            link(nc.vector.tensor_tensor(lg[:], ps2[0:B, :], bias2[:], ALU.add))
            nc.vector.tensor_reduce(mx[:, 0:NE], experts(lg), AX_X, ALU.max)
            link(nc.vector.tensor_reduce(mx[:, NE:NG], policy(lg), AX_X, ALU.max))
            nc.vector.tensor_tensor(experts(lg), experts(lg), mx[:, 0:NE].unsqueeze(2).broadcast_to([B, NE, H]),
                                    ALU.subtract)
            link(nc.vector.tensor_scalar(policy(lg), policy(lg), mx[:, NE:NG], None, ALU.subtract))
            dve.wait_ge(act_done, NG + 1)
            nc.vector.tensor_reduce(sm[:, 0:NE], experts(ex), AX_X, ALU.add)
            link(nc.vector.tensor_reduce(sm[:, NE:NG], policy(ex), AX_X, ALU.add))
            link(nc.vector.reciprocal(sm[:], sm[:]))
            link(nc.vector.tensor_scalar(policy(ex), policy(ex), sm[:, NE:NG], None, ALU.mult))
            link(nc.vector.tensor_tensor(sm[:, 0:NE], sm[:, 0:NE], policy(ex), ALU.mult))
            link(nc.vector.tensor_scalar(hg[:], ex[:, 0:H], sm[:, 0:1], None, ALU.mult))
            for e in range(1, NE):
                link(nc.vector.scalar_tensor_tensor(hg[:], ex[:, e * H:(e + 1) * H], sm[:, e:e + 1], hg[:],
                                                    ALU.mult, ALU.add))
            assert link.n == G_LINKS
            dve.wait_ge(g_in, 16 * (HP + 1))
            link(nc.vector.tensor_scalar(G.qscale[:], G.qscale[:], 0.25, None, ALU.mult))
            per_pair = lambda t: t[:].rearrange("p (b m) -> p b m", m=KD)
            over_b = lambda t: t[:].unsqueeze(1).broadcast_to([P, B, KD])
            nc.vector.tensor_tensor(per_pair(G.qbias), per_pair(G.qscale), over_b(bqc), ALU.mult)
            nc.vector.tensor_copy(per_pair(G.kbias), over_b(bkc))
            nc.vector.tensor_scalar(G.gneg[:], G.gneg[:], MASKED, None, ALU.mult).then_inc(ready, 1)


G_LINKS = 10



def key_tiles(causal, j):
    return TH if causal and j % 2 == 0 else T


def halfstep(causal, j, first, last):
    smax_j = j + 2
    ev = []
    if not (last and j == 3):
        ev.append(("step", "combine", (j + 1) % 4, "dve"))
        if causal:
            ev.append(("step", "weight", (j + 1) % 4, "act"))
        ev.append(("bank", "shift", (j + 1) % 4, "dve"))
    before, after = [], []
    if not (last and j >= 2):
        for h in range(QH):
            for i in range(TH):
                pieces = 1 if causal and smax_j % 2 == 0 else 2
                before += [("bank", "smax", (smax_j % 4, h, i, c), "dve") for c in range(pieces)]
    extra = []
    if not (first and j == 0):
        if causal:
            extra.append(("bank", "masked", (j - 1) % 4, "dve"))
        extra.append(("bank", "ctx", (j - 1) % 4, "dve"))
    if not last and j == 0:
        for qk in range(2):
            extra += [("bank", "project", (qk, 0), "act"), ("bank", "project", (qk, 1), "act"),
                      ("step", "split", qk, "dve")]
    if not last and j == 1:
        extra += [("bank", "values", 0, "dve"), ("bank", "values", 1, "dve")]
    if causal and (j == 3 or (j == 0 and not first)):
        half = 0 if j == 3 else 1
        extra += [("bank", "turn", half, "act"), ("bank", "out", (half, 0), "dve"), ("bank", "out", (half, 1), "dve")]
    n, m = len(before), len(extra)
    at = {min(n, 4 + (n - 4) * i // m) if n else 0: [] for i in range(m)} if m else {}
    for i, e in enumerate(extra):
        at[min(n, 4 + (n - 4) * i // m) if n else 0].append(e)
    for i in range(n + 1):
        ev += at.get(i, [])
        if i < n:
            ev.append(before[i])
    units = [(kt, hp) for kt in range(key_tiles(causal, j)) for hp in range(2)]
    order, done = [], 0
    for u, (kt, hp) in enumerate(units):
        order.append(("unit", kt, hp))
        if hp == 1 and kt > 0:
            order.append(("values_in", kt - 1))
        upto = len(ev) * (u + 1) // len(units)
        order += ev[done:upto]
        done = upto
    order.append(("values_in", key_tiles(causal, j) - 1))
    order.append(("step", "evacuate", j, "act"))
    return order


class Plan:

    def __init__(self, causal):
        self.causal = causal
        proj = [("bank", "project", (qk, h), "act") if h < 2 else ("step", "split", qk, "dve")
                for qk in range(2) for h in range(3)]
        vals = [("bank", "values", 0, "dve"), ("bank", "values", 1, "dve")]
        smax = [("bank", "smax", (j, h, i, c), "dve") for j in range(2) for h in range(QH) for i in range(TH)
                for c in range(1 if causal and j == 0 else 2)]
        shift = [("step", "combine", 0, "dve")] + ([("step", "weight", 0, "act")] if causal else []) + [
            ("bank", "shift", 0, "dve")]
        self.parts = {"start": [proj + vals + smax + shift]}
        for name, first, last in (("first", True, False), ("loop", False, False), ("last", False, True)):
            self.parts[name] = [halfstep(causal, j, first, last) for j in range(4)]
        tail = [("bank", "masked", 3, "dve")] if causal else []
        tail.append(("bank", "ctx", 3, "dve"))
        if causal:
            tail += [("bank", "turn", 1, "act"), ("bank", "out", (1, 0), "dve"), ("bank", "out", (1, 1), "dve")]
        self.parts["end"] = [tail]
        self.flat = {k: [x for seq in v for x in seq] for k, v in self.parts.items()}
        assert self.count("loop", "bank") % 2 == 0

    @staticmethod
    def matches(x, what):
        if what == "bank":
            return x[0] == "bank"
        if what.endswith(" bank"):
            return x[0] == "bank" and x[3] == what.split()[0]
        if what in ("unit", "values_in"):
            return x[0] == what
        return x[0] in ("bank", "step") and x[1] == what

    def count(self, part, what, upto=None):
        return sum(self.matches(x, what) for x in self.flat[part][:upto])

    def base(self, part, u, what):
        n = 0 if part == "start" else self.count("start", what)
        if part in ("loop", "last", "end"):
            n += self.count("first", what)
        per = self.count("loop", what)
        if part == "loop":
            return (u - 1) * per + n
        if part in ("last", "end"):
            n += (NPAIR - 2) * per
        if part == "end":
            n += self.count("last", what)
        return n

    def bank_of(self, part, pos):
        n = self.count("start", "bank") * (part != "start") + self.count("first", "bank") * (
            part in ("loop", "last", "end")) + self.count("last", "bank") * (part == "end")
        return (n + self.count(part, "bank", pos)) % 2

    def bank_free(self, part, pos, u):
        seen = [i for i in range(pos) if self.flat[part][i][0] == "bank"]
        if len(seen) >= 2:
            i = seen[-2]
            who = self.flat[part][i][3]
            return who, self.base(part, u, who + " bank") + self.count(part, who + " bank", i + 1)
        if part == "start":
            return None
        before = [x for x in self.flat[{"first": "start", "loop": "loop", "last": "loop", "end": "last"}[part]]
                  if x[0] == "bank"]
        who = before[len(seen) - 2][3]
        later = sum(x[3] == who for x in before[len(seen) - 2:][1:])
        return who, self.base(part, u, who + " bank") - later


def attention_phase(nc, sem, C, G, dram, causal):
    tag = "a_" if causal else "b_"
    plan = Plan(causal)
    xs = C.xs
    names = ["loaded", "filled", "dve_read", "act_read", "st_filled", "exp_done", "pv_done", "evacuated", "maxima",
             "parts_ready", "shift_in", "split_hi", "split_mid", "rest_1", "split_lo", "scratch_out", "stack_in",
             "v_ready", "ones_ready", "linked", "pool_linked", "weights", "added", "ctx_ready", "vsum_ready",
             "ctok_ready", "shift_ones", "sp_passed", "pool_passed"]
    S = {n: sem(tag + n) for n in names}
    wpair = dram["wpairA" if causal else "wpairB"]
    with ExitStack() as ctx:
        def sb(name, shape, dt=F32):
            return ctx.enter_context(nc.sbuf_tensor(tag + name, shape, dt))
        ht = sb("ht", [P, KD, L])
        w = sb("w", [P, 3, KD, P])
        q32 = sb("q32", [P, 2, L])
        parts = sb("parts", [P, 2, PARTS, L], BF16)
        qst = sb("qst", [KS + PARTS, 3, 2, QH, HALF], BF16)
        kst = sb("kst", [KS + PARTS, 3, QH, L], BF16)
        pt = sb("pt", [P, 2, QH, HALF])
        vnew = sb("vnew", [P, T, P])
        v = sb("v", [P, 2, T, QH, SLOT])
        ctxs = sb("ctxs", [P, 2, HALF])
        tmp = sb("tmp", [P, 2, TH, QH, HD])
        rden = sb("rden", [P, TH, QH])
        part_max = sb("part_max", [P, 2, QH, TH, 2])
        mx = sb("mx", [P, QH, TH])
        nmax = sb("nmax", [P, 2, QH, TH])
        mrest = sb("mrest", [QH * TH, P])
        mparts = sb("mparts", [QH * TH, 2, PARTS, P], BF16)
        if causal:
            vsum = sb("vsum", [P, 2, T, QH, SLOT])
            cneg = sb("cneg", [P, QH, TH])
            wlog = sb("wlog", [P, 4, QH, TH])
            wexp = sb("wexp", [P, 4, QH, TH])
            num = sb("num", [P, TH, QH, HD + 1])
            wsum = sb("wsum", [P, TH, QH, HD + 1])
            ctok = sb("ctok", [P, 2, TH, P])
            cts = sb("cts", [P, HALF])
        ps_s = ctx.enter_context(nc.psum_tensor(tag + "ps_s", [P, 2, 2, HALF], F32))
        ps_c = ctx.enter_context(nc.psum_tensor(tag + "ps_c", [P, 2, HALF], F32))
        ps_m = ctx.enter_context(nc.psum_tensor(tag + "ps_m", [P, 2, HALF], F32))
        q_dram = nc.dram_tensor(tag + "q_scratch", (NPAIR, PARTS, 2, 2, P // 2, HALF), BF16, kind="Internal").ap()
        k_dram = nc.dram_tensor(tag + "k_scratch", (NPAIR, PARTS, P, L), BF16, kind="Internal").ap()
        block = ctx.enter_context(nc.Block())

        WRITES = 2 * PARTS + 1
        NU, NV = plan.count("loop", "unit"), plan.count("loop", "values_in")
        assert NU == 2 * NV

        def units_upto(u, j):
            return u * NU + 2 * sum(key_tiles(causal, i) for i in range(j + 1))

        def first_col(j, kt):
            return max(0, kt * P - (j % 2) * HALF) if causal else 0

        def over_parts(eng, each):
            each("start", 0)
            each("first", 0)
            with eng.Fori(1, NPAIR - 1) as u:
                each("loop", u)
            each("last", NPAIR - 1)
            each("end", NPAIR)

        def quad_buffer(part, u, j_abs):
            q = u * 2 + j_abs // 2
            return q % 3

        def items(part):
            pos = 0
            for seq in plan.parts[part]:
                for x in seq:
                    yield pos, x
                    pos += 1

        def j_of(part, pos):
            n = 0
            for j, seq in enumerate(plan.parts[part]):
                n += len(seq)
                if pos < n:
                    return j

        def upto_projection(u):
            if isinstance(u, int) and u == 1:
                pos = max(i for i, x in enumerate(plan.flat["start"]) if x[1] == "values")
                return plan.count("start", "bank", pos + 1)
            part = "first" if isinstance(u, int) and u == 2 else "loop"
            pos = max(i for i, x in enumerate(plan.flat[part]) if x[1] == "values")
            return plan.base(part, u - 2, "bank") + plan.count(part, "bank", pos + 1)

        @block.sync
        def _(sp):
            def until(s, value):
                sp.wait_ge(s, value)
                if not isinstance(value, int):
                    sp.sem_inc(S["sp_passed"], 1)

            def params(u):
                if not (isinstance(u, int) and u == 0):
                    until(S["filled"], upto_projection(u))
                sp.dma_start(ht[:], C.ht_dram[u // 2]).then_inc(S["loaded"], 16)
                sp.dma_start(w[:], wpair[u % 2]).then_inc(S["loaded"], 16)
                until(S["loaded"], u * 32 + 32)

            def write_parts(u):
                until(S["split_lo"], u * 2 + 1)
                for n in range(2):
                    for c in range(PARTS):
                        sp.dma_start(q_dram[u, c, n].rearrange("f p q -> p f q"),
                                     parts[n * 64:(n + 1) * 64, 0, c, :].rearrange("p (f q) -> p f q", f=2)
                                     ).then_inc(S["scratch_out"], 16)
                until(S["split_lo"], u * 2 + 2)
                sp.dma_start(k_dram[u].rearrange("c p q -> p c q"), parts[:, 1]).then_inc(S["scratch_out"], 16)
                until(S["scratch_out"], (u + 1) * WRITES * 16)

            def load_stack(u, n):
                q = u * 2 + n
                buf = q % 3
                for r, (cq, ck) in enumerate(PRODUCTS):
                    rows = slice(r * HD, (r + 1) * HD)
                    sp.dma_start(qst[rows, buf].rearrange("d f h q -> d (f h) q"),
                                 q_dram[u, cq, n].rearrange("f (h d) q -> d (f h) q", h=QH)).then_inc(
                        S["stack_in"], 16)
                    sp.dma_start(kst[rows, buf], k_dram[u, ck, n * 64:(n + 1) * 64, :].rearrange(
                        "(h d) q -> d h q", h=QH)).then_inc(S["stack_in"], 16)
                until(S["stack_in"], (q + 1) * 2 * 16 * len(PRODUCTS))

            def shift_rows(u, j):
                g = u * 4 + j
                until(S["parts_ready"], g + 1)
                for c in range(PARTS):
                    dst = qst[KS + c:KS + c + 1, (u * 2 + j // 2) % 3, j % 2]
                    sp.dma_start(dst.rearrange("o h (i q) -> o (h i) q", i=TH),
                                 mparts[:, j % 2, c, :]).then_inc(S["shift_in"], 16)
                until(S["shift_in"], (g + 1) * 16 * PARTS)

            params(0)
            write_parts(0)
            load_stack(0, 0)
            load_stack(0, 1)
            params(1)
            shift_rows(0, 0)

            def each(u, last):
                shift_rows(u, 1)
                if not last:
                    write_parts(u + 1)
                    until(S["st_filled"], u * NU)
                    load_stack(u + 1, 0)
                shift_rows(u, 2)
                if not last:
                    until(S["st_filled"], units_upto(u, 1))
                    load_stack(u + 1, 1)
                shift_rows(u, 3)
                if not last:
                    shift_rows(u + 1, 0)

            each(0, False)
            params(2)
            with sp.Fori(1, NPAIR - 2) as u:
                each(u, False)
                params(u + 2)
            each(NPAIR - 2, False)
            each(NPAIR - 1, True)

        @block.tensor
        def _(pe):
            pe.wait_ge(S["shift_ones"], 1)
            pe.wait_ge(S["ones_ready"], 1)

            def bank_item(part, u, pos, x):
                _, kind, arg, who = x
                bank = plan.bank_of(part, pos)
                free = plan.bank_free(part, pos, u)
                if free is not None:
                    pe.wait_ge(S[free[0] + "_read"], free[1])
                o = ps_m[:, bank, :]
                if kind == "project":
                    qk, half = arg
                    up = 0 if part == "start" else u + 1
                    if half == 0 and qk == 0:
                        pe.wait_ge(S["loaded"], up * 32 + 32)
                    for k in range(KD):
                        mm = nc.tensor.matmul(o, w[:, qk, k, :], ht[:, k, half * HALF:(half + 1) * HALF],
                                              start=(k == 0), stop=(k == KD - 1))
                elif kind == "values":
                    for i in range(TH):
                        t = arg * TH + i
                        for k in range(KD):
                            mm = nc.tensor.matmul(o[:, i * P:(i + 1) * P], ht[:, k, t * P:(t + 1) * P],
                                                  w[:, 2, k, :], start=(k == 0), stop=(k == KD - 1))
                elif kind == "smax":
                    js, h, i, c = arg
                    jabs = js if part == "start" else (j_of(part, pos) + 2)
                    q = u * 2 + jabs // 2
                    if (h, i, c) == (0, 0, 0) and js % 2 == 0:
                        pe.wait_ge(S["stack_in"], (q + 1) * 2 * 16 * len(PRODUCTS))
                    t = (js % 2) * TH + i
                    keys = min(HALF, (t + 1) * P - c * HALF) if causal else HALF
                    diagonal = causal and t // TH == c
                    b3 = q % 3
                    mm = nc.tensor.matmul(o[:, 0:keys], qst[0:KS, b3, t // TH, h, i * P:(i + 1) * P],
                                          kst[0:KS, b3, h, c * HALF:c * HALF + keys], start=True, stop=not diagonal)
                    if diagonal:
                        mm = nc.tensor.matmul(o[:, keys - P:keys], C.identb[:], C.block_qk[:], start=False, stop=True)
                elif kind == "shift":
                    g = (0 if part == "start" else u * 4 + j_of(part, pos) + 1)
                    pe.wait_ge(S["maxima"], g + 1)
                    mm = nc.tensor.transpose(ps_m[0:QH * TH, bank, 0:P],
                                             nmax[:, arg % 2].rearrange("p h i -> p (h i)"), C.ident[:])
                elif kind == "ctx":
                    g = u * 4 + j_of(part, pos) - 1
                    pe.wait_ge(S["evacuated"], g + 1)
                    for i in range(TH):
                        mm = nc.tensor.transpose(o[:, i * P:(i + 1) * P], ctxs[:, arg % 2, i * P:(i + 1) * P],
                                                 C.ident[:])
                elif kind == "masked":
                    up = u * 4 + j_of(part, pos) - 1
                    pe.wait_ge(S["vsum_ready"], (up - arg) // 4 * 2 + arg // 2 + 1 if isinstance(up, int)
                               else (u if arg < 3 else u - 1) * 2 + arg // 2 + 1)
                    for i in range(TH):
                        t = (arg % 2) * TH + i
                        flat = lambda a: a[:, arg // 2, t].rearrange("p h c -> p (h c)")
                        nc.tensor.matmul(o[:, i * P:(i + 1) * P], C.tri[:], flat(v), start=True, stop=False)
                        mm = nc.tensor.matmul(o[:, i * P:(i + 1) * P], C.ones[:], flat(vsum), start=False, stop=True)
                elif kind == "turn":
                    n = plan.base(part, u, "ctx") + plan.count(part, "ctx", pos)
                    pe.wait_ge(S["ctok_ready"], n)
                    for i in range(TH):
                        mm = nc.tensor.transpose(o[:, i * P:(i + 1) * P], ctok[:, arg, i, :], C.ident[:])
                elif kind == "out":
                    half, c = arg
                    n = plan.base(part, u, "act bank") + plan.count(part, "act bank", pos)
                    pe.wait_ge(S["act_read"], n)
                    m = (u - 1) % 2 if half == 1 else u % 2
                    for ii in range(2):
                        i = 2 * c + ii
                        mm = nc.tensor.matmul(o[:, ii * D:(ii + 1) * D], cts[:, i * P:(i + 1) * P], C.woT[:, m, :],
                                              start=True, stop=True)
                mm.then_inc(S["filled"], 1)

            def each(part, u):
                for pos, x in items(part):
                    j = j_of(part, pos)
                    if x[0] == "bank":
                        bank_item(part, u, pos, x)
                    elif x[0] == "unit":
                        _, kt, hp = x
                        b3 = quad_buffer(part, u, j)
                        n = plan.base(part, u, "unit") + plan.count(part, "unit", pos)
                        if kt == 0 and hp == 0:
                            pe.wait_ge(S["shift_in"], (u * 4 + j + 1) * 16 * PARTS)
                        if not (isinstance(n, int) and n < 2):
                            pe.wait_ge(S["exp_done"], n - 1)
                        lo = first_col(j, kt)
                        diagonal = causal and kt * P >= (j % 2) * HALF
                        for hh in range(2):
                            h = 2 * hp + hh
                            o = ps_s[:, hp, hh, :]
                            mm = nc.tensor.matmul(o[:, lo:HALF], kst[:, b3, h, kt * P:(kt + 1) * P],
                                                  qst[:, b3, j % 2, h, lo:HALF], start=True, stop=not diagonal)
                            if diagonal:
                                mm = nc.tensor.matmul(o[:, lo:lo + P], C.identb[:], C.block_kq[:],
                                                      start=False, stop=True)
                        mm.then_inc(S["st_filled"], 1)
                    elif x[0] == "values_in":
                        kt = x[1]
                        n = plan.base(part, u, "values_in") + plan.count(part, "values_in", pos)
                        if kt == 0:
                            g = u * 4 + j
                            if not (isinstance(g, int) and g < 2):
                                pe.wait_ge(S["evacuated"], g - 1)
                            if j % 2 == 0:
                                pe.wait_ge(S["v_ready"], u * 2 + j // 2 + 1)
                        pe.wait_ge(S["exp_done"], n * 2 + 2)
                        lo = first_col(j, kt)
                        for h in range(QH):
                            mm = nc.tensor.matmul(ps_c[SLOT * h:SLOT * (h + 1), j % 2, lo:HALF],
                                                  v[:, j // 2, kt, h, :], pt[:, kt % 2, h, lo:HALF],
                                                  start=(kt == 0), stop=(kt == key_tiles(causal, j) - 1))
                        mm.then_inc(S["pv_done"], 1)
            over_parts(pe, each)

        @block.scalar
        def _(act):
            def each(part, u):
                for pos, x in items(part):
                    j = j_of(part, pos)
                    if x[0] == "unit":
                        _, kt, hp = x
                        n = plan.base(part, u, "unit") + plan.count(part, "unit", pos)
                        act.wait_ge(S["st_filled"], n + 1)
                        if hp == 0:
                            m = plan.base(part, u, "values_in") + sum(key_tiles(causal, i) for i in range(j)) + kt
                            if not (isinstance(m, int) and m < 2):
                                act.wait_ge(S["pv_done"], m - 1)
                        lo = first_col(j, kt)
                        nc.scalar.activation(pt[:, kt % 2, 2 * hp:2 * hp + 2, lo:HALF], ps_s[:, hp, :, lo:HALF],
                                             ACT.Exp).then_inc(S["exp_done"], 1)
                    elif x[0] == "bank" and x[3] == "act":
                        bank = plan.bank_of(part, pos)
                        n = plan.base(part, u, "bank") + plan.count(part, "bank", pos)
                        act.wait_ge(S["filled"], n + 1)
                        if x[1] == "project":
                            qk, half = x[2]
                            up = 0 if part == "start" else u + 1
                            if half == 0 and not (isinstance(up, int) and up == 0):
                                act.wait_ge(S["split_lo"], up * 2 - 1 + qk)
                            sc, bi = 1.0, 0.0
                            col = bass.ts(up, 1)
                            if causal:
                                bi = (G.qbias if qk == 0 else G.kbias)[:, col]
                                if qk == 0:
                                    sc = G.qscale[:, col]
                            elif qk == 0:
                                sc = 1.0 / 16.0
                            nc.scalar.activation(q32[:, qk, half * HALF:(half + 1) * HALF], ps_m[:, bank, :],
                                                 ACT.Identity, scale=sc, bias=bi).then_inc(S["act_read"], 1)
                        else:
                            nc.scalar.copy(cts[:], ps_m[:, bank, :]).then_inc(S["act_read"], 1)
                    elif x[1] == "weight":
                        g = 0 if part == "start" else u * 4 + j + 1
                        act.wait_ge(S["maxima"], g + 1)
                        nc.scalar.activation(wexp[:, x[2]], wlog[:, x[2]], ACT.Exp).then_inc(S["weights"], 1)
                    elif x[1] == "evacuate":
                        g = u * 4 + j
                        n = plan.base(part, u, "values_in") + plan.count(part, "values_in", pos)
                        act.wait_ge(S["pv_done"], n)
                        if not (isinstance(g, int) and g < 2):
                            act.wait_ge(S["ctx_ready"], g - 1)
                        nc.scalar.copy(ctxs[:, j % 2, :], ps_c[:, j % 2, :]).then_inc(S["evacuated"], 1)
            over_parts(act, each)

        def dve_program(dve, part, u, link):
            for pos, x in items(part):
                j = j_of(part, pos)
                kind, arg = x[1], x[2] if len(x) > 2 else None
                if x[0] not in ("bank", "step") or x[3] != "dve":
                    continue
                if x[0] == "bank":
                    bank = plan.bank_of(part, pos)
                    n = plan.base(part, u, "bank") + plan.count(part, "bank", pos)
                    dve.wait_ge(S["filled"], n + 1)
                    o = ps_m[:, bank, :]
                done = S["dve_read"]
                if kind == "smax":
                    js, h, i, c = arg
                    t = (js % 2) * TH + i
                    keys = min(HALF, (t + 1) * P - c * HALF) if causal else HALF
                    nc.vector.tensor_reduce(part_max[:, js % 2, h, i, c:c + 1], o[:, 0:keys], AX_X,
                                            ALU.max).then_inc(done, 1)
                elif kind == "combine":
                    g = 0 if part == "start" else u * 4 + j + 1
                    n = plan.base(part, u, "dve bank") + plan.count(part, "dve bank", pos)
                    dve.wait_ge(done, n)
                    pm = part_max[:, arg % 2]
                    if not causal:
                        link(nc.vector.tensor_tensor(mx[:], pm[:, :, :, 0], pm[:, :, :, 1], ALU.max))
                        nc.vector.tensor_scalar(nmax[:, arg % 2], mx[:], -1.0, None, ALU.mult).then_inc(S["maxima"], 1)
                        continue
                    up = (0 if part == "start" else u + 1 if j == 3 else u)
                    heads = G.gneg[:, bass.ds(up * HP + (arg // 2) * QH, QH)]
                    tiles = C.lastrow[:, (arg % 2) * TH:(arg % 2 + 1) * TH]
                    link(nc.vector.tensor_tensor(cneg[:], heads.unsqueeze(2).broadcast_to([P, QH, TH]),
                                                 tiles.unsqueeze(1).broadcast_to([P, QH, TH]), ALU.mult))
                    if arg % 2 == 1:
                        link(nc.vector.tensor_tensor(mx[:], pm[:, :, :, 0], pm[:, :, :, 1], ALU.max))
                        link(nc.vector.tensor_tensor(mx[:], mx[:], cneg[:], ALU.max))
                    else:
                        link(nc.vector.tensor_tensor(mx[:], pm[:, :, :, 0], cneg[:], ALU.max))
                    nc.vector.tensor_scalar(nmax[:, arg % 2], mx[:], -1.0, None, ALU.mult)
                    nc.vector.tensor_tensor(wlog[:, arg], cneg[:], mx[:], ALU.subtract).then_inc(S["maxima"], 1)
                elif kind == "shift":
                    g = 0 if part == "start" else u * 4 + j + 1
                    if not (isinstance(g, int) and g < 2):
                        dve.wait_ge(S["shift_in"], (g - 1) * 16 * PARTS)
                    mp = mparts[:, arg % 2]
                    src = ps_m[0:QH * TH, bank, 0:P]
                    link(nc.vector.tensor_copy(mp[:, 0, :], src))
                    nc.vector.tensor_tensor(mrest[:], src, mp[:, 0, :], ALU.subtract).then_inc(done, 1)
                    dve.wait_ge(done, plan.base(part, u, "dve bank") + plan.count(part, "dve bank", pos) + 1)
                    link(nc.vector.tensor_copy(mp[:, 1, :], mrest[:]))
                    nc.vector.tensor_tensor(mp[:, 2, :], mrest[:], mp[:, 1, :], ALU.subtract).then_inc(S["parts_ready"], 1)
                elif kind == "split":
                    up = 0 if part == "start" else u + 1
                    n = plan.base(part, u, "act bank") + plan.count(part, "act bank", pos)
                    dve.wait_ge(S["act_read"], n)
                    if not (isinstance(up, int) and up == 0):
                        dve.wait_ge(S["scratch_out"], up * WRITES * 16)
                    nc.vector.tensor_copy(parts[:, arg, 0, :], q32[:, arg, :]).then_inc(S["split_hi"], 1)
                    dve.wait_ge(S["rest_1"], up * 2 + arg + 1)
                    nc.vector.tensor_copy(parts[:, arg, 1, :], q32[:, arg, :]).then_inc(S["split_mid"], 1)
                elif kind == "values":
                    up = 0 if part == "start" else u + 1
                    if arg == 0 and not (isinstance(up, int) and up == 0):
                        dve.wait_ge(S["v_ready"], up * 2)
                    dst = vnew[:, arg * TH:(arg + 1) * TH, :]
                    src = o.rearrange("p (i c) -> p i c", i=TH)
                    if causal:
                        bv = C.bv[:, bass.ts(up % 2, P)].unsqueeze(1).broadcast_to([P, TH, P])
                        nc.vector.tensor_tensor(dst, src, bv, ALU.add).then_inc(done, 1)
                    else:
                        nc.vector.tensor_copy(dst, src).then_inc(done, 1)
                elif kind == "masked":
                    g = u * 4 + j - 1
                    dve.wait_ge(S["weights"], g + 1)
                    src = o.rearrange("p (i h c) -> p i h c", i=TH, h=QH)[:, :, :, 0:HD + 1]
                    wt = wexp[:, arg].rearrange("p h i -> p i h").unsqueeze(3).broadcast_to([P, TH, QH, HD + 1])
                    nc.vector.tensor_tensor(wsum[:], src, wt, ALU.mult).then_inc(done, 1)
                    dve.wait_ge(done, plan.base(part, u, "dve bank") + plan.count(part, "dve bank", pos) + 1)
                elif kind == "ctx":
                    src = o.rearrange("p (i h c) -> p i h c", i=TH, h=QH)
                    if causal:
                        link(nc.vector.tensor_tensor(num[:], src[:, :, :, 0:HD + 1], wsum[:], ALU.add))
                        src = num
                    link(nc.vector.reciprocal(rden[:], src[:, :, :, ONE]))
                    rb = rden[:].unsqueeze(3).broadcast_to([P, TH, QH, HD])
                    if causal:
                        dst = ctok[:, arg % 2, :, (arg // 2) * 64:(arg // 2 + 1) * 64].rearrange(
                            "p i (h c) -> p i h c", h=QH)
                        nc.vector.tensor_tensor(dst, num[:, :, :, 0:HD], rb, ALU.mult).then_inc(S["ctok_ready"], 1)
                        n = plan.base(part, u, "ctx") + plan.count(part, "ctx", pos) + 1
                        dve.wait_ge(S["ctok_ready"], n)
                        dve.sem_inc(done, 1)
                        dve.sem_inc(S["ctx_ready"], 1)
                    else:
                        g = u * 4 + j - 1
                        if not (isinstance(g, int) and g < 2):
                            dve.wait_ge(S["added"], g - 1)
                        nc.vector.tensor_tensor(tmp[:, arg % 2], src[:, :, :, 0:HD], rb, ALU.mult).then_inc(
                            S["ctx_ready"], 1)
                        dve.wait_ge(S["ctx_ready"], g + 1)
                        dve.sem_inc(done, 1)
                elif kind == "out":
                    half, c = arg
                    up = u - 1 if half == 1 else u
                    rows = xs[:, bass.ds(up // 2 * T + half * TH + 2 * c, 2), :]
                    nc.vector.tensor_tensor(rows, o.rearrange("p (i d) -> p i d", i=2), rows, ALU.add).then_inc(done, 1)

        @block.vector
        def _(dve):
            def links_in(part):
                n = 0
                for _, x in items(part):
                    if x[0] in ("bank", "step") and x[1] == "combine":
                        n += 2 + x[2] % 2 if causal else 1
                    elif x[0] == "bank" and x[1] == "shift":
                        n += 2
                    elif x[0] == "bank" and x[1] == "ctx":
                        n += 2 if causal else 1
                return n
            per = {k: links_in(k) for k in plan.parts}

            def each(part, u):
                base = {"start": 0, "first": per["start"],
                        "loop": per["start"] + per["first"] + (u - 1) * per["loop"],
                        "last": per["start"] + per["first"] + (NPAIR - 2) * per["loop"],
                        "end": per["start"] + per["first"] + (NPAIR - 2) * per["loop"] + per["last"]}[part]
                link = Links(dve, S["linked"], base)
                dve_program(dve, part, u, link)
                assert link.n == per[part], (part, link.n, per[part])
            nc.vector.memset(kst[KS:KS + PARTS], 1.0).then_inc(S["shift_ones"], 1)
            over_parts(dve, each)

        @block.gpsimd
        def _(pool):
            nc.gpsimd.memset(v[:], 0.0).then_inc(S["pool_linked"], 1)
            pool.wait_ge(S["pool_linked"], 1)
            ins = nc.gpsimd.memset(v[:, :, :, :, ONE:ONE + 1], 1.0)
            if causal:
                ins.then_inc(S["pool_linked"], 1)
                pool.wait_ge(S["pool_linked"], 2)
                ins = nc.gpsimd.memset(vsum[:, :, T - 1], 0.0)
            ins.then_inc(S["ones_ready"], 1)
            pool.wait_ge(S["ones_ready"], 1)

            def split(up):
                for qk in range(2):
                    pool.wait_ge(S["split_hi"], up * 2 + qk + 1)
                    nc.gpsimd.tensor_tensor(q32[:, qk, :], q32[:, qk, :], parts[:, qk, 0, :],
                                            ALU.subtract).then_inc(S["rest_1"], 1)
                    pool.wait_ge(S["split_mid"], up * 2 + qk + 1)
                    nc.gpsimd.tensor_tensor(parts[:, qk, 2, :], q32[:, qk, :], parts[:, qk, 1, :],
                                            ALU.subtract).then_inc(S["split_lo"], 1)

            def copy_v(up, n, vals, free):
                pool.wait_ge(S["dve_read"], vals)
                if free is not None:
                    pool.wait_ge(S["pv_done"], free[0])
                    pool.wait_ge(S["filled"], free[1])
                pool.sem_inc(S["pool_passed"], 1)
                src = vnew[:].rearrange("p t (n h c) -> p n t h c", n=2, h=QH)[:, n]
                nc.gpsimd.tensor_copy(v[:, n, :, :, 0:HD], src).then_inc(S["v_ready"], 1)
                if causal:
                    pool.wait_ge(S["v_ready"], up * 2 + n + 1)
                    for i in range(T - 2, -1, -1):
                        ins = nc.gpsimd.tensor_tensor(vsum[:, n, i], vsum[:, n, i + 1], v[:, n, i + 1], ALU.add)
                        if i:
                            ins.then_inc(S["pool_linked"], 1)
                            pool.wait_ge(S["pool_linked"], 2 + (up * 2 + n) * (T - 2) + (T - 1 - i))
                        else:
                            ins.then_inc(S["vsum_ready"], 1)

            def vals_in(part, u):
                pos = max(i for i, x in enumerate(plan.flat[part]) if x[1] == "values")
                return plan.base(part, u, "dve bank") + plan.count(part, "dve bank", pos + 1)

            def turned(part, u, j):
                kind = "masked" if causal else "ctx"
                pos = [i for i, x in enumerate(plan.flat[part]) if x[0] == "bank" and x[1] == kind and x[2] == j][0]
                return plan.base(part, u, "bank") + plan.count(part, "bank", pos + 1)

            def add(part, u, j):
                up = u - 1 if j == 3 else u
                g = up * 4 + j
                pool.wait_ge(S["ctx_ready"], g + 1)
                rows = xs[:, bass.ds(up // 2 * T + (j % 2) * TH, TH), bass.ds(up % 2 * P + (j // 2) * 64, 64)]
                nc.gpsimd.tensor_tensor(rows, rows, tmp[:, j % 2].rearrange("p i h c -> p i (h c)"),
                                        ALU.add).then_inc(S["added"], 1)

            split(0)
            copy_v(0, 0, vals_in("start", 0), None)
            copy_v(0, 1, vals_in("start", 0), None)

            def each(part, u):
                if part in ("start", "end"):
                    if part == "end" and not causal:
                        add(part, u, 3)
                    return
                if part != "first":
                    if not causal:
                        add(part, u, 3)
                    vals = plan.base("loop", u - 1, "dve bank") + plan.count(
                        "loop", "dve bank", max(i for i, x in enumerate(plan.flat["loop"]) if x[1] == "values") + 1)
                    copy_v(u, 1, vals, (u * NV, turned(part, u, 3)))
                if part != "last":
                    split(u + 1)
                for j in range(3):
                    if not causal:
                        add(part, u, j)
                    if j == 1 and part != "last":
                        done = u * NV + sum(key_tiles(causal, i) for i in range(2))
                        copy_v(u + 1, 0, vals_in(part, u), (done, turned(part, u, 1)))
            over_parts(pool, each)


def ffn_phase(nc, sem, C, dram, tag, out=None):
    xs = C.xs
    names = ["loaded", "linked", "stats", "logged", "rstd", "h_ready", "turned", "ht_read", "scored", "spread",
             "row_filled", "ranked", "sigmoid", "coef_ready", "h_added", "hidden", "gelu", "product", "updated",
             "sent", "counted", "biased", "zeroed"]
    S = {n: sem(tag + n) for n in names}
    with ExitStack() as ctx:
        def sb(name, shape, dt=F32):
            return ctx.enter_context(nc.sbuf_tensor(tag + name, shape, dt))
        W1 = sb("W1", [P, KD, F])
        W2 = sb("W2", [P, FT, D])
        h = sb("h", [P, T, D])
        ht = sb("ht", [P, 2, KD, L])
        gt = sb("gt", [P, 2, FT, HALF])
        st = sb("st", [P, T, 6])
        var, msum, r0, lnv, t1, rs, nmr = (sb(n, [P, T]) for n in ("var", "msum", "r0", "lnv", "t1", "rs", "nmr"))
        score = sb("score", [P, T])
        spread = sb("spread", [P, T, P])
        hw = sb("hw", [P, T, D])
        above = sb("above", [P, T, L], BF16)
        equal = sb("equal", [P, T, P], BF16)
        cnt = sb("cnt", [P, T, 3])
        rank = sb("rank", [P, T])
        sig = sb("sig", [P, T])
        coef = sb("coef", [P, 2, T])
        biased = sb("biased", [P, 2, D])
        ps_h = ctx.enter_context(nc.psum_tensor(tag + "ps_h", [P, 2, HALF], F32))
        ps_o = ctx.enter_context(nc.psum_tensor(tag + "ps_o", [P, 2, HALF], F32))
        ps_t = ctx.enter_context(nc.psum_tensor(tag + "ps_t", [P, 2, HALF], F32))
        ps_r = ctx.enter_context(nc.psum_tensor(tag + "ps_r", [P, L], F32))
        block = ctx.enter_context(nc.Block())

        def over_batches(eng, prepare, use):
            prepare(0)
            prepare(1)
            use(0)
            with eng.Fori(1, B - 1) as b:
                prepare(b + 1)
                use(b)
            use(B - 1)

        @block.sync
        def _(sp):
            sp.dma_start(W1[:], dram["W1"].rearrange("(k p) f -> p k f", p=P)).then_inc(S["loaded"], 16)
            sp.dma_start(W2[:], dram["W2"].rearrange("(f p) d -> p f d", p=P)).then_inc(S["loaded"], 16)
            sp.wait_ge(S["loaded"], 32)
            if out is not None:
                for b in range(B):
                    sp.wait_ge(S["updated"], (b + 1) * T)
                    sp.dma_start(out[b].rearrange("(t p) d -> p t d", p=P),
                                 xs[:, b * T:(b + 1) * T, :]).then_inc(S["sent"], 16)
                sp.wait_ge(S["sent"], 16 * B)

        @block.vector
        def _(dve):
            LINKS = 9

            def prepare(b):
                link = Links(dve, S["linked"], b * LINKS)
                for t in range(T):
                    ins = nc.vector.bn_stats(st[:, t, :], xs[:, b * T + t, :])
                link(ins)
                nc.vector.tensor_tensor(msum[:], st[:, :, 1], st[:, :, 4], ALU.add)
                nc.vector.tensor_tensor(t1[:], st[:, :, 1], st[:, :, 4], ALU.subtract)
                link(nc.vector.tensor_tensor(var[:], st[:, :, 2], st[:, :, 5], ALU.add))
                link(nc.vector.scalar_tensor_tensor(t1[:], t1[:], 0.25, t1[:], ALU.mult, ALU.mult))
                nc.vector.scalar_tensor_tensor(var[:], var[:], 1.0 / D, t1[:], ALU.mult, ALU.add).then_inc(
                    S["stats"], 1)
                dve.wait_ge(S["rstd"], b + 1)
                dve.wait_ge(S["stats"], b + 1)
                link(nc.vector.scalar_tensor_tensor(t1[:], r0[:], -0.5, r0[:], ALU.mult, ALU.mult))
                link(nc.vector.scalar_tensor_tensor(t1[:], var[:], EPS, t1[:], ALU.add, ALU.mult))
                link(nc.vector.scalar_tensor_tensor(rs[:], t1[:], 1.5, r0[:], ALU.add, ALU.mult))
                link(nc.vector.scalar_tensor_tensor(nmr[:], msum[:], -0.5, rs[:], ALU.mult, ALU.mult))
                wait_past(dve, S["turned"], b * 4)
                wait_past(dve, S["h_added"], b)
                for t in range(T):
                    nc.vector.tensor_scalar(h[:, t, :], xs[:, b * T + t, :], rs[:, t:t + 1], nmr[:, t:t + 1],
                                            ALU.mult, ALU.add).then_inc(S["h_ready"], 1)
                dve.wait_ge(S["h_ready"], (b + 1) * T)
                for t in range(T):
                    ins = nc.vector.tensor_tensor_reduce(hw[:, t, :], h[:, t, :], C.wr[:], 1.0, 0.0, ALU.mult,
                                                         ALU.add, score[:, t:t + 1])
                ins.then_inc(S["scored"], 1)
                dve.wait_ge(S["scored"], b + 1)
                nc.vector.tensor_copy(spread[:], score[:].unsqueeze(2).broadcast_to([P, T, P])).then_inc(
                    S["spread"], 1)
                dve.wait_ge(S["row_filled"], b + 1)
                for t in range(T):
                    s = score[:, t:t + 1]
                    if t:
                        nc.vector.tensor_scalar(above[:, t, 0:t * P], ps_r[:, 0:t * P], s, None, ALU.is_ge, ALU.add,
                                                accum_out=cnt[:, t, 0:1])
                    nc.vector.tensor_scalar(above[:, t, t * P:L], ps_r[:, t * P:L], s, None, ALU.is_gt, ALU.add,
                                            accum_out=cnt[:, t, 1:2])
                    ins = nc.vector.scalar_tensor_tensor(equal[:, t, :], ps_r[:, t * P:(t + 1) * P], s, C.tri[:],
                                                         ALU.is_equal, ALU.mult, accum_out=cnt[:, t, 2:3])
                ins.then_inc(S["counted"], 1)
                dve.wait_ge(S["counted"], b + 1)
                link(nc.vector.tensor_tensor(rank[:], cnt[:, :, 0], cnt[:, :, 1], ALU.add))
                link(nc.vector.tensor_tensor(rank[:], rank[:], cnt[:, :, 2], ALU.add))
                dve.wait_ge(S["sigmoid"], b + 1)
                nc.vector.scalar_tensor_tensor(coef[:, b % 2, :], rank[:], KEEP - 0.5, sig[:], ALU.is_lt,
                                               ALU.mult).then_inc(S["coef_ready"], 1)
                assert link.n == LINKS

            def use(b):
                dve.wait_ge(S["coef_ready"], b + 1)
                dve.wait_ge(S["h_added"], b + 1)
                for t in range(T):
                    n = b * T + t
                    dve.wait_ge(S["product"], n + 1)
                    nc.vector.tensor_tensor(biased[:, t % 2, :], ps_o[:, t % 2, 0:D], C.b2[:], ALU.add).then_inc(
                        S["biased"], 1)
                    dve.wait_ge(S["biased"], n + 1)
                    rows = xs[:, n, :]
                    nc.vector.scalar_tensor_tensor(rows, biased[:, t % 2, :], coef[:, b % 2, t:t + 1], rows,
                                                   ALU.mult, ALU.add).then_inc(S["updated"], 1)

            nc.vector.memset(cnt[:, 0, 0:1], 0.0)
            over_batches(dve, prepare, use)

        @block.scalar
        def _(act):
            def prepare(b):
                act.wait_ge(S["stats"], b + 1)
                nc.scalar.activation(lnv[:], var[:], ACT.Ln, bias=C.eps[:]).then_inc(S["logged"], 1)
                act.wait_ge(S["logged"], b + 1)
                nc.scalar.activation(r0[:], lnv[:], ACT.Exp, scale=-0.5).then_inc(S["rstd"], 1)
                for g in range(4):
                    act.wait_ge(S["turned"], b * 4 + g + 1)
                    k, half = g // 2, g % 2
                    nc.scalar.copy(ht[:, b % 2, k, half * HALF:(half + 1) * HALF], ps_t[:, g % 2, :]).then_inc(
                        S["ht_read"], 1)
                act.wait_ge(S["scored"], b + 1)
                nc.scalar.activation(sig[:], score[:], ACT.Sigmoid).then_inc(S["sigmoid"], 1)

            def use(b):
                for half in range(2):
                    for f in range(FT):
                        n = b * 2 * FT + half * FT + f
                        act.wait_ge(S["hidden"], n + 1)
                        nc.scalar.activation(gt[:, half, f, :], ps_h[:, f % 2, :], ACT.Gelu_apprx_tanh,
                                             bias=C.b1[:, f:f + 1]).then_inc(S["gelu"], 1)
            over_batches(act, prepare, use)

        @block.tensor
        def _(pe):
            pe.wait_ge(S["loaded"], 32)

            def prepare(b):
                for g in range(4):
                    k, half = g // 2, g % 2
                    pe.wait_ge(S["h_ready"], b * T + (half + 1) * TH)
                    if g >= 2:
                        pe.wait_ge(S["ht_read"], b * 4 + g - 1)
                    else:
                        wait_past(pe, S["ht_read"], b * 4)
                    for i in range(TH):
                        t = half * TH + i
                        mm = nc.tensor.transpose(ps_t[:, g % 2, i * P:(i + 1) * P], h[:, t, k * P:(k + 1) * P],
                                                 C.ident[:])
                    mm.then_inc(S["turned"], 1)
                pe.wait_ge(S["spread"], b + 1)
                wait_past(pe, S["coef_ready"], b)
                for t in range(T):
                    mm = nc.tensor.transpose(ps_r[:, t * P:(t + 1) * P], spread[:, t, :], C.ident[:])
                mm.then_inc(S["row_filled"], 1)

            def use(b):
                pe.wait_ge(S["ht_read"], (b + 1) * 4)
                for half in range(2):
                    for f in range(FT):
                        n = half * FT + f
                        if n >= 2:
                            pe.wait_ge(S["gelu"], b * 2 * FT + n - 1)
                        else:
                            wait_past(pe, S["gelu"], b * 2 * FT)
                        for k in range(KD):
                            mm = nc.tensor.matmul(ps_h[:, f % 2, :], W1[:, k, f * P:(f + 1) * P],
                                                  ht[:, b % 2, k, half * HALF:(half + 1) * HALF],
                                                  start=(k == 0), stop=(k == KD - 1))
                        mm.then_inc(S["hidden"], 1)
                for t in range(T):
                    if t % TH == 0:
                        pe.wait_ge(S["gelu"], b * 2 * FT + (t // TH + 1) * FT)
                    if t >= 2:
                        pe.wait_ge(S["biased"], b * T + t - 1)
                    else:
                        wait_past(pe, S["biased"], b * T)
                    for f in range(FT):
                        mm = nc.tensor.matmul(ps_o[:, t % 2, 0:D], gt[:, t // TH, f, (t % TH) * P:(t % TH + 1) * P],
                                              W2[:, f, :], start=(f == 0), stop=(f == FT - 1))
                    mm.then_inc(S["product"], 1)
            over_batches(pe, prepare, use)

        @block.gpsimd
        def _(pool):
            with pool.Fori(0, B) as b:
                pool.wait_ge(S["h_ready"], b * T + T)
                rows = xs[:, bass.ts(b, T), :]
                nc.gpsimd.tensor_tensor(rows, rows, h[:], ALU.add).then_inc(S["h_added"], 1)



class Shared:
    pass


def program(nc, dram, out):
    nc.disable_value_cache = True
    with ExitStack() as ctx:
        def sb(name, shape, dt=F32):
            return ctx.enter_context(nc.sbuf_tensor(name, shape, dt))

        def sem(name):
            return ctx.enter_context(nc.semaphore(name))

        C, G = Shared(), Shared()
        C.xs = sb("xs", [P, B * T, D])
        C.ident = sb("ident", [P, P])
        C.identb = sb("identb", [P, P], BF16)
        C.ones = sb("ones", [P, P])
        C.zerosb = sb("zerosb", [P, P], BF16)
        C.tri = sb("tri", [P, P])
        C.block_qk = sb("block_qk", [P, P], BF16)
        C.block_kq = sb("block_kq", [P, P], BF16)
        C.lastrow = sb("lastrow", [P, T])
        C.eps = sb("eps", [P, 1])
        C.bo = sb("bo", [P, D])
        C.bv = sb("bv", [P, D])
        C.woT = sb("woT", [P, KD, D])
        C.wr = sb("wr", [P, D])
        C.b1 = sb("b1", [P, FT])
        C.b2 = sb("b2", [P, D])
        G.xsum = sb("xsum", [P, KD, B])
        G.gneg = sb("gneg", [P, B * H])
        G.qscale = sb("qscale", [P, NPAIR])
        G.qbias = sb("qbias", [P, NPAIR])
        G.kbias = sb("kbias", [P, NPAIR])
        C.ht_dram = nc.dram_tensor("ht_scratch", (B, P, KD, L), F32, kind="Internal").ap()
        C.g_dram = nc.dram_tensor("g_scratch", (B, H), F32, kind="Internal").ap()

        constants_phase(nc, sem, C, dram)
        norm_phase(nc, sem, C, "n0_", x_in=dram["x"], gates=G)
        gates_phase(nc, sem, C, G, dram)
        attention_phase(nc, sem, C, G, dram, True)
        ffn_phase(nc, sem, C, dram, "f1_")
        norm_phase(nc, sem, C, "n1_")
        attention_phase(nc, sem, C, G, dram, False)
        ffn_phase(nc, sem, C, dram, "f2_", out)


def layout(inputs):
    import numpy as np
    a = {k: np.asarray(v) for k, v in inputs.items()}
    at = lambda n: a["L0_attn_a_" + n]
    c = np.ascontiguousarray

    def per_pair(ws):
        w = np.stack([x.reshape(KD, P, KD, P) for x in ws])
        return c(w.transpose(3, 2, 0, 1, 4))
    wqkv = a["L0_attn_b_w_qkv"]
    return {
        "x": c(at("x")), "bo": at("bo"), "bv": at("bv"), "bq": at("bq"), "bk": at("bk"),
        "woT": c(at("wo").T),
        "wpairA": per_pair([at("wq").T, at("wk").T, at("wv").T]),
        "wpairB": per_pair([wqkv[:, 0:D], wqkv[:, D:2 * D], wqkv[:, 2 * D:3 * D]]),
        "gw1": c(np.concatenate([at("pw1"), at("sw1")[None]]).transpose(2, 0, 1)),
        "gb1": c(np.concatenate([at("pb1"), at("sb1")[None]])),
        "gw2": c(np.concatenate([at("pw2").reshape(NE * H, DH), at("sw2")]).T),
        "gb2": c(np.concatenate([at("pb2").reshape(NE * H), at("sb2")])),
        "wr": a["L0_ffn_w_router"], "W1": a["L0_ffn_W1"], "b1": a["L0_ffn_b1"],
        "W2": a["L0_ffn_W2"], "b2": a["L0_ffn_b2"],
    }


def kernel(**inputs):
    import concourse.bacc as bacc
    from concourse.bass_utils import run_bass_kernel_spmd

    nc = bacc.Bacc("TRN2", target_bir_lowering=False, num_devices=1)
    arrays = {f"in_{k}": v for k, v in layout(inputs).items()}
    dram = {k[3:]: nc.dram_tensor(k, v.shape, mybir.dt.from_np(v.dtype), kind="ExternalInput").ap()
            for k, v in arrays.items()}
    out = nc.dram_tensor("out_dram", (B, L, D), F32, kind="ExternalOutput").ap()
    program(nc, dram, out)
    return run_bass_kernel_spmd(nc, [arrays], core_ids=[0]).results[0]["out_dram"]
```

```python
from contextlib import ExitStack

import concourse.bass as bass
from concourse import mybir

P = 128
F32 = mybir.dt.float32
BF16 = mybir.dt.bfloat16
ALU = mybir.AluOpType
ACT = mybir.ActivationFunctionType
AX_X = mybir.AxisListType.X

B, L, D = 8, 1024, 256
H, HD = 16, 16
T = L // P
KD = D // P
HALF = L // 2
TH = T // 2
NE, DH = 3, 128
F = 1024
FT = F // P
KEEP = L // 2
EPS = 1e-5
MASKED = -1.0e9
BLOCKED = -1.0e30
HP = 8
QH = 4
NPAIR = B * H // HP
SLOT = 32
ONE = HD
PARTS = 3
PRODUCTS = [(0, 0), (0, 1), (1, 0), (1, 1), (0, 2), (2, 0)]
KS = HD * len(PRODUCTS)


class Links:

    def __init__(self, eng, sem, base=0):
        self.eng, self.sem, self.base, self.n = eng, sem, base, 0

    def __call__(self, ins):
        self.n += 1
        ins.then_inc(self.sem, 1)
        self.eng.wait_ge(self.sem, self.base + self.n)


def wait_past(eng, sem, value):
    if not (isinstance(value, int) and value == 0):
        eng.wait_ge(sem, value)


def peel_first(eng, count, each):
    each(0)
    with eng.Fori(1, count) as b:
        each(b)


def norm_phase(nc, sem, C, tag, x_in=None, gates=None):
    xs = C.xs
    x_here, linked, stats, rstd, h_ready, filled, ht_ready, stored, ht_sent, bo_added = (
        sem(tag + n) for n in ("x_here", "linked", "stats", "rstd", "h_ready", "filled", "ht_ready",
                               "stored", "ht_sent", "bo_added"))
    with ExitStack() as ctx:
        def sb(name, shape, dt=F32):
            return ctx.enter_context(nc.sbuf_tensor(tag + name, shape, dt))
        h = sb("h", [P, T, D])
        st = sb("st", [P, T, 6])
        var = sb("var", [P, T])
        msum = sb("msum", [P, T])
        r0 = sb("r0", [P, T])
        lnv = sb("lnv", [P, T])
        t1 = sb("t1", [P, T])
        rs = sb("rs", [P, T])
        nmr = sb("nmr", [P, T])
        hts = sb("hts", [P, 2, KD, L])
        psT = ctx.enter_context(nc.psum_tensor(tag + "psT", [P, KD, L], F32))
        block = ctx.enter_context(nc.Block())

        @block.sync
        def _(sp):
            if x_in is not None:
                for b in range(B):
                    sp.dma_start(xs[:, b * T:(b + 1) * T, :],
                                 x_in[b].rearrange("(t p) d -> p t d", p=P)).then_inc(x_here, 16)
                    sp.wait_ge(x_here, b * 16 + 16)
            sp.sem_inc(ht_sent, 16)
            for b in range(B):
                sp.wait_ge(ht_ready, b * 2 + 2)
                sp.dma_start(C.ht_dram[b], hts[:, b % 2]).then_inc(ht_sent, 16)
                sp.wait_ge(ht_sent, b * 16 + 32)

        @block.vector
        def _(dve):
            def each(b):
                link = Links(dve, linked, b * 7)
                if x_in is not None:
                    dve.wait_ge(x_here, b * 16 + 16)
                for t in range(T):
                    ins = nc.vector.bn_stats(st[:, t, :], xs[:, b * T + t, :])
                link(ins)
                nc.vector.tensor_tensor(msum[:], st[:, :, 1], st[:, :, 4], ALU.add)
                nc.vector.tensor_tensor(t1[:], st[:, :, 1], st[:, :, 4], ALU.subtract)
                link(nc.vector.tensor_tensor(var[:], st[:, :, 2], st[:, :, 5], ALU.add))
                link(nc.vector.scalar_tensor_tensor(t1[:], t1[:], 0.25, t1[:], ALU.mult, ALU.mult))
                nc.vector.scalar_tensor_tensor(var[:], var[:], 1.0 / D, t1[:], ALU.mult, ALU.add).then_inc(stats, 1)
                dve.wait_ge(rstd, b + 1)
                dve.wait_ge(stats, b + 1)
                link(nc.vector.scalar_tensor_tensor(t1[:], r0[:], -0.5, r0[:], ALU.mult, ALU.mult))
                link(nc.vector.scalar_tensor_tensor(t1[:], var[:], EPS, t1[:], ALU.add, ALU.mult))
                link(nc.vector.scalar_tensor_tensor(rs[:], t1[:], 1.5, r0[:], ALU.add, ALU.mult))
                link(nc.vector.scalar_tensor_tensor(nmr[:], msum[:], -0.5, rs[:], ALU.mult, ALU.mult))
                wait_past(dve, filled, b * 4)
                for t in range(T):
                    nc.vector.tensor_scalar(h[:, t, :], xs[:, b * T + t, :], rs[:, t:t + 1], nmr[:, t:t + 1],
                                            ALU.mult, ALU.add).then_inc(h_ready, 1)
            peel_first(dve, B, each)

        @block.scalar
        def _(act):
            def each(b):
                act.wait_ge(stats, b + 1)
                nc.scalar.activation(lnv[:], var[:], ACT.Ln, bias=C.eps[:]).then_inc(stored, 1)
                act.wait_ge(stored, b + 1)
                nc.scalar.activation(r0[:], lnv[:], ACT.Exp, scale=-0.5).then_inc(rstd, 1)
                wait_past(act, ht_sent, b * 16)
                for k in range(KD):
                    act.wait_ge(filled, b * 4 + 2 * k + 2)
                    accum = None if gates is None else gates.xsum[:, k, bass.ts(b, 1)]
                    nc.scalar.activation(hts[:, b % 2, k, :], psT[:, k, :], ACT.Identity,
                                         accum_out=accum).then_inc(ht_ready, 1)
            peel_first(act, B, each)

        @block.tensor
        def _(pe):
            def each(b):
                for k in range(KD):
                    for half in range(2):
                        pe.wait_ge(h_ready, b * T + (half + 1) * TH)
                        if half == 0:
                            wait_past(pe, ht_ready, b * 2)
                        for i in range(TH):
                            t = half * TH + i
                            mm = nc.tensor.transpose(psT[:, k, t * P:(t + 1) * P], h[:, t, k * P:(k + 1) * P],
                                                     C.ident[:])
                        mm.then_inc(filled, 1)
            peel_first(pe, B, each)

        if x_in is not None:
            @block.gpsimd
            def _(pool):
                def each(b):
                    pool.wait_ge(h_ready, b * T + T)
                    nc.gpsimd.tensor_tensor(xs[:, bass.ts(b, T), :], xs[:, bass.ts(b, T), :],
                                            C.bo[:].unsqueeze(1).broadcast_to([P, T, D]),
                                            ALU.add).then_inc(bo_added, 1)
                peel_first(pool, B, each)


def constants_phase(nc, sem, C, dram):
    loaded, made, step = sem("c_loaded"), sem("c_made"), sem("c_step")
    with nc.Block() as block:
        @block.sync
        def _(sp):
            loads = [
                (C.bo[:], dram["bo"].partition_broadcast(P)),
                (C.woT[:], dram["woT"].rearrange("(m p) n -> p m n", p=P)),
                (C.bv[:], dram["bv"].partition_broadcast(P)),
                (C.wr[:], dram["wr"].partition_broadcast(P)),
                (C.b2[:], dram["b2"].partition_broadcast(P)),
                (C.b1[:], dram["b1"].rearrange("(f p) -> p f", p=P)),
            ]
            for dst, src in loads:
                sp.dma_start(dst, src, allow_slow_non_contiguous=True).then_inc(loaded, 16)
            sp.wait_ge(loaded, 16 * len(loads))

        @block.vector
        def _(dve):
            nc.vector.memset(C.eps[:], EPS).then_inc(made, 1)
            nc.vector.memset(C.ones[:], 1.0).then_inc(made, 1)
            nc.vector.memset(C.zerosb[:], 0.0).then_inc(made, 1)

        @block.gpsimd
        def _(pool):
            pool.wait_ge(made, 3)
            def keep(out, in_, op, fill, pattern, base, ch):
                return nc.gpsimd.affine_select(out=out, in_=in_, compare_op=op, fill=fill, base=base,
                                               pattern=pattern, channel_multiplier=ch)
            keep(C.ident[:], C.ones[:], ALU.is_equal, 0.0, [[-1, P]], 0, 1).then_inc(step, 1)
            pool.wait_ge(step, 1)
            nc.gpsimd.tensor_copy(C.identb[:], C.ident[:]).then_inc(step, 1)
            keep(C.tri[:], C.ones[:], ALU.is_gt, 0.0, [[-1, P]], 0, 1).then_inc(step, 1)
            keep(C.block_qk[:], C.zerosb[:], ALU.is_ge, BLOCKED, [[-1, P]], 0, 1).then_inc(step, 1)
            keep(C.block_kq[:], C.zerosb[:], ALU.is_ge, BLOCKED, [[1, P]], 0, -1).then_inc(step, 1)
            keep(C.lastrow[:], C.ones[:, 0:T], ALU.not_equal, 3.0e29, [[P, T]], 1 - L, 1).then_inc(step, 1)


def gates_phase(nc, sem, C, G, dram):
    loaded, mm_done, act_done, linked, g_out, g_in, ready = (
        sem("g_" + n) for n in ("loaded", "mm", "act", "linked", "out", "in", "ready"))
    NG = NE + 1
    with ExitStack() as ctx:
        def sb(name, shape, dt=F32):
            return ctx.enter_context(nc.sbuf_tensor("g_" + name, shape, dt))
        w1 = sb("w1", [P, KD, NG, DH])
        bias1 = sb("bias1", [P, NG])
        w2 = sb("w2", [P, NE * H + NE])
        bias2 = sb("bias2", [B, NE * H + NE])
        hid = sb("hid", [P, NG, B])
        lg = sb("lg", [B, NE * H + NE])
        mx = sb("mx", [B, NG])
        ex = sb("ex", [B, NE * H + NE])
        sm = sb("sm", [B, NG])
        hg = sb("hg", [B, H])
        bqc = sb("bqc", [P, KD])
        bkc = sb("bkc", [P, KD])
        ps1 = ctx.enter_context(nc.psum_tensor("g_ps1", [P, NG, B], F32))
        ps2 = ctx.enter_context(nc.psum_tensor("g_ps2", [P, NE * H + NE], F32))
        block = ctx.enter_context(nc.Block())
        experts = lambda t: t[:, 0:NE * H].rearrange("b (e h) -> b e h", e=NE)
        policy = lambda t: t[:, NE * H:NE * H + NE]

        @block.sync
        def _(sp):
            loads = [(w1[:], dram["gw1"].rearrange("(k p) g c -> p k g c", p=P)),
                     (bias1[:], dram["gb1"].rearrange("g c -> c g")),
                     (w2[:], dram["gw2"]), (bias2[:], dram["gb2"].partition_broadcast(B)),
                     (bqc[:], dram["bq"].rearrange("(m p) -> p m", p=P)),
                     (bkc[:], dram["bk"].rearrange("(m p) -> p m", p=P))]
            for dst, src in loads:
                sp.dma_start(dst, src, allow_slow_non_contiguous=True).then_inc(loaded, 16)
            sp.wait_ge(loaded, 16 * len(loads))
            sp.wait_ge(linked, G_LINKS)
            sp.dma_start(C.g_dram, hg[:]).then_inc(g_out, 16)
            sp.wait_ge(g_out, 16)
            sp.dma_start(G.gneg[:], C.g_dram.rearrange("b h -> (b h)").partition_broadcast(P)).then_inc(g_in, 16)
            for hh in range(HP):
                src = C.g_dram.rearrange("b (m h) -> h (b m)", m=KD)[hh]
                sp.dma_start(G.qscale[hh * HD:(hh + 1) * HD, :], src.partition_broadcast(HD),
                             allow_slow_non_contiguous=True).then_inc(g_in, 16)
            sp.wait_ge(g_in, 16 * (HP + 1))

        @block.tensor
        def _(pe):
            pe.wait_ge(loaded, 16 * 6)
            for g in range(NG):
                for k in range(KD):
                    mm = nc.tensor.matmul(ps1[:, g, :], w1[:, k, g, :], G.xsum[:, k, :],
                                          start=(k == 0), stop=(k == KD - 1))
            mm.then_inc(mm_done, 1)
            pe.wait_ge(act_done, NG)
            for e in range(NE):
                nc.tensor.matmul(ps2[0:B, e * H:(e + 1) * H], hid[:, e, :], w2[:, e * H:(e + 1) * H],
                                 start=True, stop=True)
            nc.tensor.matmul(policy(ps2[0:B]), hid[:, NE, :], policy(w2), start=True, stop=True).then_inc(mm_done, 1)

        @block.scalar
        def _(act):
            act.wait_ge(loaded, 16 * 6)
            act.wait_ge(mm_done, 1)
            for g in range(NG):
                nc.scalar.activation(hid[:, g, :], ps1[:, g, :], ACT.Gelu, bias=bias1[:, g:g + 1],
                                     scale=1.0 / L).then_inc(act_done, 1)
            act.wait_ge(linked, 3)
            nc.scalar.activation(ex[:], lg[:], ACT.Exp).then_inc(act_done, 1)

        @block.vector
        def _(dve):
            link = Links(dve, linked)
            dve.wait_ge(mm_done, 2)
            link(nc.vector.tensor_tensor(lg[:], ps2[0:B, :], bias2[:], ALU.add))
            nc.vector.tensor_reduce(mx[:, 0:NE], experts(lg), AX_X, ALU.max)
            link(nc.vector.tensor_reduce(mx[:, NE:NG], policy(lg), AX_X, ALU.max))
            nc.vector.tensor_tensor(experts(lg), experts(lg), mx[:, 0:NE].unsqueeze(2).broadcast_to([B, NE, H]),
                                    ALU.subtract)
            link(nc.vector.tensor_scalar(policy(lg), policy(lg), mx[:, NE:NG], None, ALU.subtract))
            dve.wait_ge(act_done, NG + 1)
            nc.vector.tensor_reduce(sm[:, 0:NE], experts(ex), AX_X, ALU.add)
            link(nc.vector.tensor_reduce(sm[:, NE:NG], policy(ex), AX_X, ALU.add))
            link(nc.vector.reciprocal(sm[:], sm[:]))
            link(nc.vector.tensor_scalar(policy(ex), policy(ex), sm[:, NE:NG], None, ALU.mult))
            link(nc.vector.tensor_tensor(sm[:, 0:NE], sm[:, 0:NE], policy(ex), ALU.mult))
            link(nc.vector.tensor_scalar(hg[:], ex[:, 0:H], sm[:, 0:1], None, ALU.mult))
            for e in range(1, NE):
                link(nc.vector.scalar_tensor_tensor(hg[:], ex[:, e * H:(e + 1) * H], sm[:, e:e + 1], hg[:],
                                                    ALU.mult, ALU.add))
            assert link.n == G_LINKS
            dve.wait_ge(g_in, 16 * (HP + 1))
            link(nc.vector.tensor_scalar(G.qscale[:], G.qscale[:], 0.25, None, ALU.mult))
            per_pair = lambda t: t[:].rearrange("p (b m) -> p b m", m=KD)
            over_b = lambda t: t[:].unsqueeze(1).broadcast_to([P, B, KD])
            nc.vector.tensor_tensor(per_pair(G.qbias), per_pair(G.qscale), over_b(bqc), ALU.mult)
            nc.vector.tensor_copy(per_pair(G.kbias), over_b(bkc))
            nc.vector.tensor_scalar(G.gneg[:], G.gneg[:], MASKED, None, ALU.mult).then_inc(ready, 1)


G_LINKS = 10



NB = 3
BUFS = 3
STEP = 3
TAIL = 3
SHIFT_AT = 4
LEFT = 3
COST = {"smax": 3, "project": 6, "values": 4, "ctx": 4, "masked": 3, "turn": 3, "out": 3, "shift": 3,
        "split_hi": 3, "split_mid": 3, "combine": 1}


def key_tiles(causal, j):
    return TH if causal and j % 2 == 0 else T


def halfstep(causal, j, first, last):
    smax_j = j + 2
    ev = []
    if not (last and j == 3):
        ev.append(("step", "combine", (j + 1) % 4, "dve"))
        if causal:
            ev.append(("step", "weight", (j + 1) % 4, "act"))
    before = []
    if not (last and j >= 2):
        for h in range(QH):
            for i in range(TH):
                pieces = 1 if causal and smax_j % 2 == 0 else 2
                before += [("bank", "smax", (smax_j % 4, h, i, c), "dve") for c in range(pieces)]
    extra = []
    if not (first and j == 0):
        if causal:
            extra.append(("bank", "masked", (j - 1) % 4, "dve"))
        extra.append(("bank", "ctx", (j - 1) % 4, "dve"))
    if not last and j == 0:
        for qk in range(2):
            extra += [("bank", "project", (qk, 0), "act"), ("bank", "project", (qk, 1), "act"),
                      ("step", "split_hi", qk, "dve"), ("step", "split_mid", qk, "dve")]
    if not last and j == 1:
        extra += [("bank", "values", 0, "dve"), ("bank", "values", 1, "dve")]
    if causal and (j == 3 or (j == 0 and not first)):
        half = 0 if j == 3 else 1
        extra += [("bank", "turn", half, "act"), ("bank", "out", (half, 0), "dve"), ("bank", "out", (half, 1), "dve")]
    if not (last and j == 3):
        before.insert(min(SHIFT_AT, len(before)), ("bank", "shift", (j + 1) % 4, "dve"))
    n, m = len(before), len(extra)
    at = {min(n, 4 + (n - 4) * i // m) if n else 0: [] for i in range(m)} if m else {}
    for i, e in enumerate(extra):
        at[min(n, 4 + (n - 4) * i // m) if n else 0].append(e)
    for i in range(n + 1):
        ev += at.get(i, [])
        if i < n:
            ev.append(before[i])
    units = [(kt, hp) for kt in range(key_tiles(causal, j)) for hp in range(2)]
    main = []
    for kt, hp in units:
        main.append((2, ("unit", kt, hp)))
        if hp == 1 and kt > 0:
            main.append((4, ("values_in", kt - 1)))
    main.append((4, ("values_in", key_tiles(causal, j) - 1)))
    cost = lambda x: COST.get(x[1], 0)
    whole, rest = sum(c for c, _ in main[:-1]), sum(map(cost, ev))
    left = min(rest, LEFT * COST["smax"])
    order, spent, at_main = [], 0, 0
    for c, x in main:
        now = rest if x == main[-1][1] else (rest - left) * at_main / whole
        while ev and (spent < now or x == main[-1][1]):
            spent += cost(ev[0])
            order.append(ev.pop(0))
        order.append(x)
        at_main += c
    order.append(("step", "evacuate", j, "act"))
    return order


class Plan:

    def __init__(self, causal):
        self.causal = causal
        proj = [("bank", "project", (qk, h), "act") if h < 2 else
                ("step", "split_hi" if h == 2 else "split_mid", qk, "dve") for qk in range(2) for h in range(4)]
        vals = [("bank", "values", 0, "dve"), ("bank", "values", 1, "dve")]
        smax = [("bank", "smax", (j, h, i, c), "dve") for j in range(2) for h in range(QH) for i in range(TH)
                for c in range(1 if causal and j == 0 else 2)]
        shift = [("step", "combine", 0, "dve")] + ([("step", "weight", 0, "act")] if causal else []) + [
            ("bank", "shift", 0, "dve")]
        self.parts = {"start": [proj + vals + smax + shift]}
        pairs = {"first": [(True, False)], "loop": [(False, False)] * STEP,
                 "last": [(False, False)] * (TAIL - 1) + [(False, True)]}
        for name, kinds in pairs.items():
            self.parts[name] = [halfstep(causal, j, *k) for k in kinds for j in range(4)]
        tail = [("bank", "masked", 3, "dve")] if causal else []
        tail.append(("bank", "ctx", 3, "dve"))
        if causal:
            tail += [("bank", "turn", 1, "act"), ("bank", "out", (1, 0), "dve"), ("bank", "out", (1, 1), "dve")]
        self.parts["end"] = [tail]
        self.flat = {k: [x for seq in v for x in seq] for k, v in self.parts.items()}

    @staticmethod
    def matches(x, what):
        if what == "bank":
            return x[0] == "bank"
        if what.endswith(" bank"):
            return x[0] == "bank" and x[3] == what.split()[0]
        if what in ("unit", "values_in"):
            return x[0] == what
        return x[0] in ("bank", "step") and x[1] == what

    def count(self, part, what, upto=None):
        return sum(self.matches(x, what) for x in self.flat[part][:upto])

    def base(self, part, u, what):
        n = 0 if part == "start" else self.count("start", what)
        if part in ("loop", "last", "end"):
            n += self.count("first", what)
        per = self.count("loop", what) // STEP
        assert per * STEP == self.count("loop", what)
        if part == "loop":
            return (u - 1) * per + n
        if part in ("last", "end"):
            n += (NPAIR - 1 - TAIL) * per
        if part == "end":
            n += self.count("last", what)
        return n

    def bank_of(self, part, pos):
        return (self.count(part, "bank", pos) - self.count(part, "bank")) % NB

    PRIOR = {"first": "start", "loop": "loop", "last": "loop", "end": "last"}

    def read(self, part, pos, u, kind, arg):
        is_it = lambda x: x[0] == "bank" and x[1] == kind and x[2] == arg
        seen = [i for i in range(pos) if is_it(self.flat[part][i])]
        if seen:
            i = seen[-1]
            who = self.flat[part][i][3] + " bank"
            return self.base(part, u, who) + self.count(part, who, i + 1)
        prior = self.PRIOR[part]
        i = max(i for i, x in enumerate(self.flat[prior]) if is_it(x))
        who = self.flat[prior][i][3] + " bank"
        return self.base(part, u, who) - self.count(prior, who) + self.count(prior, who, i + 1)

    def bank_free(self, part, pos, u):
        bank = self.bank_of(part, pos)
        seen = [i for i in range(pos) if self.flat[part][i][0] == "bank" and self.bank_of(part, i) == bank]
        if seen:
            i = seen[-1]
            who = self.flat[part][i][3]
            return who, self.base(part, u, who + " bank") + self.count(part, who + " bank", i + 1)
        if part == "start":
            return None
        prior = self.PRIOR[part]
        i = max(i for i, x in enumerate(self.flat[prior]) if x[0] == "bank" and self.bank_of(prior, i) == bank)
        who = self.flat[prior][i][3]
        later = self.count(prior, who + " bank") - self.count(prior, who + " bank", i + 1)
        return who, self.base(part, u, who + " bank") - later


def attention_phase(nc, sem, C, G, dram, causal):
    tag = "a_" if causal else "b_"
    plan = Plan(causal)
    xs = C.xs
    names = ["loaded", "filled", "dve_read", "act_read", "st_filled", "exp_done", "pv_done", "evacuated", "maxima",
             "parts_ready", "shift_in", "split_hi", "split_mid", "rest_1", "split_lo", "scratch_out", "stack_in",
             "v_ready", "ones_ready", "linked", "pool_linked", "weights", "added", "vsum_ready",
             "shift_ones", "sp_passed", "pool_passed"]
    S = {n: sem(tag + n) for n in names}
    wpair = dram["wpairA" if causal else "wpairB"]
    with ExitStack() as ctx:
        def sb(name, shape, dt=F32):
            return ctx.enter_context(nc.sbuf_tensor(tag + name, shape, dt))
        ht = sb("ht", [P, KD, L])
        w = sb("w", [P, 3, KD, P])
        q32 = sb("q32", [P, 2, L])
        parts = sb("parts", [P, 2, PARTS, L], BF16)
        qst = sb("qst", [KS + PARTS, 3, 2, QH, HALF], BF16)
        kst = sb("kst", [KS + PARTS, 3, QH, L], BF16)
        pt = sb("pt", [P, 2, QH, HALF])
        vnew = sb("vnew", [P, T, P])
        v = sb("v", [P, 2, T, QH, SLOT])
        ctxs = sb("ctxs", [P, 2, HALF])
        tmp = sb("tmp", [P, 2, TH, QH, HD])
        rden = sb("rden", [P, TH, QH])
        part_max = sb("part_max", [P, 2, QH, TH, 2])
        mx = sb("mx", [P, QH, TH])
        nmax = sb("nmax", [P, 2, QH, TH])
        mrest = sb("mrest", [QH * TH, P])
        mparts = sb("mparts", [QH * TH, 2, PARTS, P], BF16)
        if causal:
            vsum = sb("vsum", [P, 2, T, QH, SLOT])
            cneg = sb("cneg", [P, QH, TH])
            wlog = sb("wlog", [P, 4, QH, TH])
            wexp = sb("wexp", [P, 4, QH, TH])
            num = sb("num", [P, TH, QH, HD + 1])
            wsum = sb("wsum", [P, TH, QH, HD + 1])
            ctok = sb("ctok", [P, 2, TH, P])
            cts = sb("cts", [P, HALF])
        ps_s = ctx.enter_context(nc.psum_tensor(tag + "ps_s", [P, 2, 2, HALF], F32))
        ps_c = ctx.enter_context(nc.psum_tensor(tag + "ps_c", [P, HALF], F32))
        ps_m = ctx.enter_context(nc.psum_tensor(tag + "ps_m", [P, NB, HALF], F32))
        q_dram = nc.dram_tensor(tag + "q_scratch", (NPAIR, PARTS, 2, 2, P // 2, HALF), BF16, kind="Internal").ap()
        k_dram = nc.dram_tensor(tag + "k_scratch", (NPAIR, PARTS, P, L), BF16, kind="Internal").ap()
        block = ctx.enter_context(nc.Block())

        WRITES = 2 * PARTS + 1
        NU, NV = (plan.count("loop", n) // STEP for n in ("unit", "values_in"))
        assert NU == 2 * NV

        def units_upto(u, j):
            return u * NU + 2 * sum(key_tiles(causal, i) for i in range(j + 1))

        def first_col(j, kt):
            return max(0, kt * P - (j % 2) * HALF) if causal else 0

        def over_parts(eng, each):
            each("start", 0)
            each("first", 0)
            with eng.Fori(1, NPAIR - TAIL, STEP) as u:
                each("loop", u)
            each("last", NPAIR - TAIL)
            each("end", NPAIR)

        def quad_buffer(u, j):
            first = u if isinstance(u, int) else 1
            return (2 * first + j // 2) % BUFS

        def items(part):
            pos = 0
            for seq in plan.parts[part]:
                for x in seq:
                    yield pos, x
                    pos += 1

        def j_of(part, pos):
            n = 0
            for j, seq in enumerate(plan.parts[part]):
                n += len(seq)
                if pos < n:
                    return j

        def upto_projection(u):
            if isinstance(u, int) and u == 1:
                pos = max(i for i, x in enumerate(plan.flat["start"]) if x[1] == "values")
                return plan.count("start", "bank", pos + 1)
            return in_pair(u - 2, "values", 1, "bank")

        def in_pair(p, kind, arg, what):
            part, u, nth = "loop", p, 0
            if isinstance(p, int) and p == 0:
                part = "first"
            elif isinstance(p, int) and p >= NPAIR - TAIL:
                part, u = "last", NPAIR - TAIL
                nth = p - u
            pos = [i for i, x in enumerate(plan.flat[part]) if x[0] == "bank" and x[1] == kind and x[2] == arg][nth]
            return plan.base(part, u, what) + plan.count(part, what, pos + 1)

        @block.sync
        def _(sp):
            def until(s, value):
                sp.wait_ge(s, value)
                if not isinstance(value, int):
                    sp.sem_inc(S["sp_passed"], 1)

            def params(u):
                if not (isinstance(u, int) and u == 0):
                    until(S["filled"], upto_projection(u))
                sp.dma_start(ht[:], C.ht_dram[u // 2]).then_inc(S["loaded"], 16)
                sp.dma_start(w[:], wpair[u % 2]).then_inc(S["loaded"], 16)
                until(S["loaded"], u * 32 + 32)

            def write_parts(u):
                until(S["split_lo"], u * 2 + 1)
                for n in range(2):
                    for c in range(PARTS):
                        sp.dma_start(q_dram[u, c, n].rearrange("f p q -> p f q"),
                                     parts[n * 64:(n + 1) * 64, 0, c, :].rearrange("p (f q) -> p f q", f=2)
                                     ).then_inc(S["scratch_out"], 16)
                until(S["split_lo"], u * 2 + 2)
                sp.dma_start(k_dram[u].rearrange("c p q -> p c q"), parts[:, 1]).then_inc(S["scratch_out"], 16)
                until(S["scratch_out"], (u + 1) * WRITES * 16)

            def load_stack(u, n):
                q = u * 2 + n
                buf = q % 3
                for r, (cq, ck) in enumerate(PRODUCTS):
                    rows = slice(r * HD, (r + 1) * HD)
                    sp.dma_start(qst[rows, buf].rearrange("d f h q -> d (f h) q"),
                                 q_dram[u, cq, n].rearrange("f (h d) q -> d (f h) q", h=QH)).then_inc(
                        S["stack_in"], 16)
                    sp.dma_start(kst[rows, buf], k_dram[u, ck, n * 64:(n + 1) * 64, :].rearrange(
                        "(h d) q -> d h q", h=QH)).then_inc(S["stack_in"], 16)
                until(S["stack_in"], (q + 1) * 2 * 16 * len(PRODUCTS))

            def shift_rows(u, j):
                g = u * 4 + j
                until(S["parts_ready"], g + 1)
                for c in range(PARTS):
                    dst = qst[KS + c:KS + c + 1, (u * 2 + j // 2) % 3, j % 2]
                    sp.dma_start(dst.rearrange("o h (i q) -> o (h i) q", i=TH),
                                 mparts[:, j % 2, c, :]).then_inc(S["shift_in"], 16)
                until(S["shift_in"], (g + 1) * 16 * PARTS)

            params(0)
            write_parts(0)
            load_stack(0, 0)
            load_stack(0, 1)
            params(1)
            shift_rows(0, 0)

            def each(u, last):
                shift_rows(u, 1)
                if not last:
                    write_parts(u + 1)
                    until(S["st_filled"], u * NU)
                    load_stack(u + 1, 0)
                shift_rows(u, 2)
                if not last:
                    until(S["st_filled"], units_upto(u, 1))
                    load_stack(u + 1, 1)
                shift_rows(u, 3)
                if not last:
                    shift_rows(u + 1, 0)

            each(0, False)
            params(2)
            with sp.Fori(1, NPAIR - 2) as u:
                each(u, False)
                params(u + 2)
            each(NPAIR - 2, False)
            each(NPAIR - 1, True)

        @block.tensor
        def _(pe):
            pe.wait_ge(S["shift_ones"], 1)
            pe.wait_ge(S["ones_ready"], 1)

            def bank_item(part, u, pos, x):
                _, kind, arg, who = x
                jj = j_of(part, pos)
                p = u + jj // 4
                bank = plan.bank_of(part, pos)
                free = plan.bank_free(part, pos, u)
                if free is not None:
                    pe.wait_ge(S[free[0] + "_read"], free[1])
                o = ps_m[:, bank, :]
                if kind == "project":
                    qk, half = arg
                    up = 0 if part == "start" else p + 1
                    if half == 0 and qk == 0:
                        pe.wait_ge(S["loaded"], up * 32 + 32)
                    for k in range(KD):
                        mm = nc.tensor.matmul(o, w[:, qk, k, :], ht[:, k, half * HALF:(half + 1) * HALF],
                                              start=(k == 0), stop=(k == KD - 1))
                elif kind == "values":
                    for i in range(TH):
                        t = arg * TH + i
                        for k in range(KD):
                            mm = nc.tensor.matmul(o[:, i * P:(i + 1) * P], ht[:, k, t * P:(t + 1) * P],
                                                  w[:, 2, k, :], start=(k == 0), stop=(k == KD - 1))
                elif kind == "smax":
                    js, h, i, c = arg
                    jabs = js if part == "start" else jj + 2
                    q = u * 2 + jabs // 2
                    if (h, i, c) == (0, 0, 0) and js % 2 == 0:
                        pe.wait_ge(S["stack_in"], (q + 1) * 2 * 16 * len(PRODUCTS))
                    t = (js % 2) * TH + i
                    keys = min(HALF, (t + 1) * P - c * HALF) if causal else HALF
                    diagonal = causal and t // TH == c
                    b3 = quad_buffer(u, jabs)
                    mm = nc.tensor.matmul(o[:, 0:keys], qst[0:KS, b3, t // TH, h, i * P:(i + 1) * P],
                                          kst[0:KS, b3, h, c * HALF:c * HALF + keys], start=True, stop=not diagonal)
                    if diagonal:
                        mm = nc.tensor.matmul(o[:, keys - P:keys], C.identb[:], C.block_qk[:], start=False, stop=True)
                elif kind == "shift":
                    g = 0 if part == "start" else u * 4 + jj + 1
                    pe.wait_ge(S["maxima"], g + 1)
                    mm = nc.tensor.transpose(ps_m[0:QH * TH, bank, 0:P],
                                             nmax[:, arg % 2].rearrange("p h i -> p (h i)"), C.ident[:])
                elif kind == "ctx":
                    g = u * 4 + jj - 1
                    pe.wait_ge(S["evacuated"], g + 1)
                    for i in range(TH):
                        mm = nc.tensor.transpose(o[:, i * P:(i + 1) * P], ctxs[:, arg % 2, i * P:(i + 1) * P],
                                                 C.ident[:])
                elif kind == "masked":
                    pe.wait_ge(S["vsum_ready"], (p - 1 if arg == 3 else p) * 2 + arg // 2 + 1)
                    for i in range(TH):
                        t = (arg % 2) * TH + i
                        flat = lambda a: a[:, arg // 2, t].rearrange("p h c -> p (h c)")
                        nc.tensor.matmul(o[:, i * P:(i + 1) * P], C.tri[:], flat(v), start=True, stop=False)
                        mm = nc.tensor.matmul(o[:, i * P:(i + 1) * P], C.ones[:], flat(vsum), start=False, stop=True)
                elif kind == "turn":
                    pe.wait_ge(S["dve_read"], plan.read(part, pos, u, "ctx", 2 + arg))
                    for i in range(TH):
                        mm = nc.tensor.transpose(o[:, i * P:(i + 1) * P], ctok[:, arg, i, :], C.ident[:])
                elif kind == "out":
                    half, c = arg
                    n = plan.base(part, u, "act bank") + plan.count(part, "act bank", pos)
                    pe.wait_ge(S["act_read"], n)
                    m = (p - 1) % 2 if half == 1 else p % 2
                    for ii in range(2):
                        i = 2 * c + ii
                        mm = nc.tensor.matmul(o[:, ii * D:(ii + 1) * D], cts[:, i * P:(i + 1) * P], C.woT[:, m, :],
                                              start=True, stop=True)
                mm.then_inc(S["filled"], 1)

            def each(part, u):
                for pos, x in items(part):
                    jj = j_of(part, pos)
                    p, j = u + jj // 4, jj % 4
                    if x[0] == "bank":
                        bank_item(part, u, pos, x)
                    elif x[0] == "unit":
                        _, kt, hp = x
                        b3 = quad_buffer(u, jj)
                        n = plan.base(part, u, "unit") + plan.count(part, "unit", pos)
                        if kt == 0 and hp == 0:
                            pe.wait_ge(S["shift_in"], (p * 4 + j + 1) * 16 * PARTS)
                        if not (isinstance(n, int) and n < 2):
                            pe.wait_ge(S["exp_done"], n - 1)
                        lo = first_col(j, kt)
                        diagonal = causal and kt * P >= (j % 2) * HALF
                        for hh in range(2):
                            h = 2 * hp + hh
                            o = ps_s[:, hp, hh, :]
                            mm = nc.tensor.matmul(o[:, lo:HALF], kst[:, b3, h, kt * P:(kt + 1) * P],
                                                  qst[:, b3, j % 2, h, lo:HALF], start=True, stop=not diagonal)
                            if diagonal:
                                mm = nc.tensor.matmul(o[:, lo:lo + P], C.identb[:], C.block_kq[:],
                                                      start=False, stop=True)
                        mm.then_inc(S["st_filled"], 1)
                    elif x[0] == "values_in":
                        kt = x[1]
                        n = plan.base(part, u, "values_in") + plan.count(part, "values_in", pos)
                        if kt == 0:
                            g = p * 4 + j
                            wait_past(pe, S["evacuated"], g)
                            if j % 2 == 0:
                                pe.wait_ge(S["v_ready"], p * 2 + j // 2 + 1)
                        pe.wait_ge(S["exp_done"], n * 2 + 2)
                        lo = first_col(j, kt)
                        for h in range(QH):
                            mm = nc.tensor.matmul(ps_c[SLOT * h:SLOT * (h + 1), lo:HALF],
                                                  v[:, j // 2, kt, h, :], pt[:, kt % 2, h, lo:HALF],
                                                  start=(kt == 0), stop=(kt == key_tiles(causal, j) - 1))
                        mm.then_inc(S["pv_done"], 1)
            over_parts(pe, each)

        @block.scalar
        def _(act):
            def each(part, u):
                for pos, x in items(part):
                    jj = j_of(part, pos)
                    p, j = u + jj // 4, jj % 4
                    if x[0] == "unit":
                        _, kt, hp = x
                        n = plan.base(part, u, "unit") + plan.count(part, "unit", pos)
                        act.wait_ge(S["st_filled"], n + 1)
                        if hp == 0:
                            m = plan.base(part, u, "values_in") + sum(key_tiles(causal, i) for i in range(jj)) + kt
                            if not (isinstance(m, int) and m < 2):
                                act.wait_ge(S["pv_done"], m - 1)
                        lo = first_col(j, kt)
                        nc.scalar.activation(pt[:, kt % 2, 2 * hp:2 * hp + 2, lo:HALF], ps_s[:, hp, :, lo:HALF],
                                             ACT.Exp).then_inc(S["exp_done"], 1)
                    elif x[0] == "bank" and x[3] == "act":
                        bank = plan.bank_of(part, pos)
                        n = plan.base(part, u, "bank") + plan.count(part, "bank", pos)
                        act.wait_ge(S["filled"], n + 1)
                        if x[1] == "project":
                            qk, half = x[2]
                            up = 0 if part == "start" else p + 1
                            if half == 0 and not (isinstance(up, int) and up == 0):
                                act.wait_ge(S["split_lo"], up * 2 - 1 + qk)
                            sc, bi = 1.0, 0.0
                            col = bass.ts(up, 1)
                            if causal:
                                bi = (G.qbias if qk == 0 else G.kbias)[:, col]
                                if qk == 0:
                                    sc = G.qscale[:, col]
                            elif qk == 0:
                                sc = 1.0 / 16.0
                            nc.scalar.activation(q32[:, qk, half * HALF:(half + 1) * HALF], ps_m[:, bank, :],
                                                 ACT.Identity, scale=sc, bias=bi).then_inc(S["act_read"], 1)
                        else:
                            nc.scalar.copy(cts[:], ps_m[:, bank, :]).then_inc(S["act_read"], 1)
                    elif x[1] == "weight":
                        g = 0 if part == "start" else p * 4 + j + 1
                        act.wait_ge(S["maxima"], g + 1)
                        nc.scalar.activation(wexp[:, x[2]], wlog[:, x[2]], ACT.Exp).then_inc(S["weights"], 1)
                    elif x[1] == "evacuate":
                        g = p * 4 + j
                        n = plan.base(part, u, "values_in") + plan.count(part, "values_in", pos)
                        act.wait_ge(S["pv_done"], n)
                        if not (isinstance(g, int) and g < 2):
                            act.wait_ge(S["dve_read"], plan.read(part, pos, u, "ctx", (j - 2) % 4))
                        nc.scalar.copy(ctxs[:, j % 2, :], ps_c[:]).then_inc(S["evacuated"], 1)
            over_parts(act, each)

        def dve_program(dve, part, u, link):
            for pos, x in items(part):
                jj = j_of(part, pos)
                p, j = u + jj // 4, jj % 4
                kind, arg = x[1], x[2] if len(x) > 2 else None
                if x[0] not in ("bank", "step") or x[3] != "dve":
                    continue
                if x[0] == "bank":
                    bank = plan.bank_of(part, pos)
                    n = plan.base(part, u, "bank") + plan.count(part, "bank", pos)
                    dve.wait_ge(S["filled"], n + 1)
                    o = ps_m[:, bank, :]
                done = S["dve_read"]
                if kind == "smax":
                    js, h, i, c = arg
                    t = (js % 2) * TH + i
                    keys = min(HALF, (t + 1) * P - c * HALF) if causal else HALF
                    nc.vector.tensor_reduce(part_max[:, js % 2, h, i, c:c + 1], o[:, 0:keys], AX_X,
                                            ALU.max).then_inc(done, 1)
                elif kind == "combine":
                    g = 0 if part == "start" else p * 4 + j + 1
                    n = plan.base(part, u, "dve bank") + plan.count(part, "dve bank", pos)
                    dve.wait_ge(done, n)
                    pm = part_max[:, arg % 2]
                    if not causal:
                        link(nc.vector.tensor_tensor(mx[:], pm[:, :, :, 0], pm[:, :, :, 1], ALU.max))
                        nc.vector.tensor_scalar(nmax[:, arg % 2], mx[:], -1.0, None, ALU.mult).then_inc(S["maxima"], 1)
                        continue
                    up = 0 if part == "start" else p + 1 if j == 3 else p
                    heads = G.gneg[:, bass.ds(up * HP + (arg // 2) * QH, QH)]
                    tiles = C.lastrow[:, (arg % 2) * TH:(arg % 2 + 1) * TH]
                    link(nc.vector.tensor_tensor(cneg[:], heads.unsqueeze(2).broadcast_to([P, QH, TH]),
                                                 tiles.unsqueeze(1).broadcast_to([P, QH, TH]), ALU.mult))
                    if arg % 2 == 1:
                        link(nc.vector.tensor_tensor(mx[:], pm[:, :, :, 0], pm[:, :, :, 1], ALU.max))
                        link(nc.vector.tensor_tensor(mx[:], mx[:], cneg[:], ALU.max))
                    else:
                        link(nc.vector.tensor_tensor(mx[:], pm[:, :, :, 0], cneg[:], ALU.max))
                    nc.vector.tensor_scalar(nmax[:, arg % 2], mx[:], -1.0, None, ALU.mult)
                    nc.vector.tensor_tensor(wlog[:, arg], cneg[:], mx[:], ALU.subtract).then_inc(S["maxima"], 1)
                elif kind == "shift":
                    g = 0 if part == "start" else p * 4 + j + 1
                    if not (isinstance(g, int) and g < 2):
                        dve.wait_ge(S["shift_in"], (g - 1) * 16 * PARTS)
                    mp = mparts[:, arg % 2]
                    src = ps_m[0:QH * TH, bank, 0:P]
                    link(nc.vector.tensor_copy(mp[:, 0, :], src))
                    nc.vector.tensor_tensor(mrest[:], src, mp[:, 0, :], ALU.subtract).then_inc(done, 1)
                    dve.wait_ge(done, plan.base(part, u, "dve bank") + plan.count(part, "dve bank", pos) + 1)
                    link(nc.vector.tensor_copy(mp[:, 1, :], mrest[:]))
                    nc.vector.tensor_tensor(mp[:, 2, :], mrest[:], mp[:, 1, :], ALU.subtract).then_inc(S["parts_ready"], 1)
                elif kind == "split_hi":
                    up = 0 if part == "start" else p + 1
                    n = plan.base(part, u, "act bank") + plan.count(part, "act bank", pos)
                    dve.wait_ge(S["act_read"], n)
                    if not (isinstance(up, int) and up == 0):
                        dve.wait_ge(S["scratch_out"], up * WRITES * 16)
                    nc.vector.tensor_copy(parts[:, arg, 0, :], q32[:, arg, :]).then_inc(S["split_hi"], 1)
                elif kind == "split_mid":
                    up = 0 if part == "start" else p + 1
                    dve.wait_ge(S["rest_1"], up * 2 + arg + 1)
                    nc.vector.tensor_copy(parts[:, arg, 1, :], q32[:, arg, :]).then_inc(S["split_mid"], 1)
                elif kind == "values":
                    up = 0 if part == "start" else p + 1
                    if arg == 0 and not (isinstance(up, int) and up == 0):
                        dve.wait_ge(S["v_ready"], up * 2)
                    dst = vnew[:, arg * TH:(arg + 1) * TH, :]
                    src = o.rearrange("p (i c) -> p i c", i=TH)
                    if causal:
                        bv = C.bv[:, bass.ts(up % 2, P)].unsqueeze(1).broadcast_to([P, TH, P])
                        nc.vector.tensor_tensor(dst, src, bv, ALU.add).then_inc(done, 1)
                    else:
                        nc.vector.tensor_copy(dst, src).then_inc(done, 1)
                elif kind == "masked":
                    g = p * 4 + j - 1
                    dve.wait_ge(S["weights"], g + 1)
                    src = o.rearrange("p (i h c) -> p i h c", i=TH, h=QH)[:, :, :, 0:HD + 1]
                    wt = wexp[:, arg].rearrange("p h i -> p i h").unsqueeze(3).broadcast_to([P, TH, QH, HD + 1])
                    nc.vector.tensor_tensor(wsum[:], src, wt, ALU.mult).then_inc(done, 1)
                    dve.wait_ge(done, plan.base(part, u, "dve bank") + plan.count(part, "dve bank", pos) + 1)
                elif kind == "ctx":
                    src = o.rearrange("p (i h c) -> p i h c", i=TH, h=QH)
                    if not (part == "first" and arg == 0):
                        dve.wait_ge(done, plan.read(part, pos, u, "ctx", (arg - 1) % 4))
                    if causal:
                        link(nc.vector.tensor_tensor(num[:], src[:, :, :, 0:HD + 1], wsum[:], ALU.add))
                        src = num
                    link(nc.vector.reciprocal(rden[:], src[:, :, :, ONE]))
                    rb = rden[:].unsqueeze(3).broadcast_to([P, TH, QH, HD])
                    if causal:
                        dst = ctok[:, arg % 2, :, (arg // 2) * 64:(arg // 2 + 1) * 64].rearrange(
                            "p i (h c) -> p i h c", h=QH)
                        nc.vector.tensor_tensor(dst, num[:, :, :, 0:HD], rb, ALU.mult).then_inc(done, 1)
                    else:
                        g = p * 4 + j - 1
                        if not (isinstance(g, int) and g < 2):
                            dve.wait_ge(S["added"], g - 1)
                        nc.vector.tensor_tensor(tmp[:, arg % 2], src[:, :, :, 0:HD], rb, ALU.mult).then_inc(done, 1)
                elif kind == "out":
                    half, c = arg
                    up = p - 1 if half == 1 else p
                    rows = xs[:, bass.ds(up // 2 * T + half * TH + 2 * c, 2), :]
                    nc.vector.tensor_tensor(rows, o.rearrange("p (i d) -> p i d", i=2), rows, ALU.add).then_inc(done, 1)

        @block.vector
        def _(dve):
            def links_in(part):
                n = 0
                for _, x in items(part):
                    if x[0] in ("bank", "step") and x[1] == "combine":
                        n += 2 + x[2] % 2 if causal else 1
                    elif x[0] == "bank" and x[1] == "shift":
                        n += 2
                    elif x[0] == "bank" and x[1] == "ctx":
                        n += 2 if causal else 1
                return n
            per = {k: links_in(k) for k in plan.parts}
            in_loop = (NPAIR - 1 - TAIL) // STEP * per["loop"]

            def each(part, u):
                base = {"start": 0, "first": per["start"],
                        "loop": per["start"] + per["first"] + (u - 1) * (per["loop"] // STEP),
                        "last": per["start"] + per["first"] + in_loop,
                        "end": per["start"] + per["first"] + in_loop + per["last"]}[part]
                link = Links(dve, S["linked"], base)
                dve_program(dve, part, u, link)
                assert link.n == per[part], (part, link.n, per[part])
            nc.vector.memset(kst[KS:KS + PARTS], 1.0).then_inc(S["shift_ones"], 1)
            over_parts(dve, each)

        @block.gpsimd
        def _(pool):
            nc.gpsimd.memset(v[:], 0.0).then_inc(S["pool_linked"], 1)
            pool.wait_ge(S["pool_linked"], 1)
            ins = nc.gpsimd.memset(v[:, :, :, :, ONE:ONE + 1], 1.0)
            if causal:
                ins.then_inc(S["pool_linked"], 1)
                pool.wait_ge(S["pool_linked"], 2)
                ins = nc.gpsimd.memset(vsum[:, :, T - 1], 0.0)
            ins.then_inc(S["ones_ready"], 1)
            pool.wait_ge(S["ones_ready"], 1)

            def split(up):
                for qk in range(2):
                    pool.wait_ge(S["split_hi"], up * 2 + qk + 1)
                    nc.gpsimd.tensor_tensor(q32[:, qk, :], q32[:, qk, :], parts[:, qk, 0, :],
                                            ALU.subtract).then_inc(S["rest_1"], 1)
                    pool.wait_ge(S["split_mid"], up * 2 + qk + 1)
                    nc.gpsimd.tensor_tensor(parts[:, qk, 2, :], q32[:, qk, :], parts[:, qk, 1, :],
                                            ALU.subtract).then_inc(S["split_lo"], 1)

            def copy_v(up, n, vals, free):
                pool.wait_ge(S["dve_read"], vals)
                if free is not None:
                    pool.wait_ge(S["pv_done"], free[0])
                    pool.wait_ge(S["filled"], free[1])
                pool.sem_inc(S["pool_passed"], 1)
                src = vnew[:].rearrange("p t (n h c) -> p n t h c", n=2, h=QH)[:, n]
                nc.gpsimd.tensor_copy(v[:, n, :, :, 0:HD], src).then_inc(S["v_ready"], 1)
                if causal:
                    pool.wait_ge(S["v_ready"], up * 2 + n + 1)
                    for i in range(T - 2, -1, -1):
                        ins = nc.gpsimd.tensor_tensor(vsum[:, n, i], vsum[:, n, i + 1], v[:, n, i + 1], ALU.add)
                        if i:
                            ins.then_inc(S["pool_linked"], 1)
                            pool.wait_ge(S["pool_linked"], 2 + (up * 2 + n) * (T - 2) + (T - 1 - i))
                        else:
                            ins.then_inc(S["vsum_ready"], 1)

            def turned(p, j):
                return in_pair(p + 1 if j == 3 else p, "masked" if causal else "ctx", j, "bank")

            def add(p, j):
                if isinstance(p, int) and p == NPAIR - 1 and j == 3:
                    n = plan.base("end", NPAIR, "dve bank") + plan.count("end", "dve bank")
                else:
                    n = in_pair(p + 1 if j == 3 else p, "ctx", j, "dve bank")
                pool.wait_ge(S["dve_read"], n)
                rows = xs[:, bass.ds(p // 2 * T + (j % 2) * TH, TH), bass.ds(p % 2 * P + (j // 2) * 64, 64)]
                nc.gpsimd.tensor_tensor(rows, rows, tmp[:, j % 2].rearrange("p i h c -> p i (h c)"),
                                        ALU.add).then_inc(S["added"], 1)

            vals = plan.count("start", "dve bank", 1 + max(
                i for i, x in enumerate(plan.flat["start"]) if x[1] == "values"))
            split(0)
            copy_v(0, 0, vals, None)
            copy_v(0, 1, vals, None)

            def each(p, last=False):
                if not (isinstance(p, int) and p == 0):
                    if not causal:
                        add(p - 1, 3)
                    copy_v(p, 1, in_pair(p - 1, "values", 1, "dve bank"), (p * NV, turned(p - 1, 3)))
                if not last:
                    split(p + 1)
                for j in range(3):
                    if not causal:
                        add(p, j)
                    if j == 1 and not last:
                        done = p * NV + sum(key_tiles(causal, i) for i in range(2))
                        copy_v(p + 1, 0, in_pair(p, "values", 1, "dve bank"), (done, turned(p, 1)))

            each(0)
            with pool.Fori(1, NPAIR - 1) as u:
                each(u)
            each(NPAIR - 1, True)
            if not causal:
                add(NPAIR - 1, 3)


def ffn_phase(nc, sem, C, dram, tag, out=None):
    xs = C.xs
    names = ["loaded", "linked", "stats", "logged", "rstd", "h_ready", "turned", "ht_read", "scored", "spread",
             "row_filled", "ranked", "sigmoid", "coef_ready", "h_added", "hidden", "gelu", "product", "updated",
             "sent", "counted", "biased", "zeroed"]
    S = {n: sem(tag + n) for n in names}
    with ExitStack() as ctx:
        def sb(name, shape, dt=F32):
            return ctx.enter_context(nc.sbuf_tensor(tag + name, shape, dt))
        W1 = sb("W1", [P, KD, F])
        W2 = sb("W2", [P, FT, D])
        h = sb("h", [P, T, D])
        ht = sb("ht", [P, 2, KD, L])
        gt = sb("gt", [P, 2, FT, HALF])
        st = sb("st", [P, T, 6])
        var, msum, r0, lnv, t1, rs, nmr = (sb(n, [P, T]) for n in ("var", "msum", "r0", "lnv", "t1", "rs", "nmr"))
        score = sb("score", [P, T])
        spread = sb("spread", [P, T, P])
        hw = sb("hw", [P, T, D])
        above = sb("above", [P, T, L], BF16)
        equal = sb("equal", [P, T, P], BF16)
        cnt = sb("cnt", [P, T, 3])
        rank = sb("rank", [P, T])
        sig = sb("sig", [P, T])
        coef = sb("coef", [P, 2, T])
        biased = sb("biased", [P, 2, D])
        ps_h = ctx.enter_context(nc.psum_tensor(tag + "ps_h", [P, 2, HALF], F32))
        ps_o = ctx.enter_context(nc.psum_tensor(tag + "ps_o", [P, 2, HALF], F32))
        ps_t = ctx.enter_context(nc.psum_tensor(tag + "ps_t", [P, 2, HALF], F32))
        ps_r = ctx.enter_context(nc.psum_tensor(tag + "ps_r", [P, L], F32))
        block = ctx.enter_context(nc.Block())

        def over_batches(eng, prepare, use):
            prepare(0)
            prepare(1)
            use(0)
            with eng.Fori(1, B - 1) as b:
                prepare(b + 1)
                use(b)
            use(B - 1)

        @block.sync
        def _(sp):
            sp.dma_start(W1[:], dram["W1"].rearrange("(k p) f -> p k f", p=P)).then_inc(S["loaded"], 16)
            sp.dma_start(W2[:], dram["W2"].rearrange("(f p) d -> p f d", p=P)).then_inc(S["loaded"], 16)
            sp.wait_ge(S["loaded"], 32)
            if out is not None:
                for b in range(B):
                    sp.wait_ge(S["updated"], (b + 1) * T)
                    sp.dma_start(out[b].rearrange("(t p) d -> p t d", p=P),
                                 xs[:, b * T:(b + 1) * T, :]).then_inc(S["sent"], 16)
                sp.wait_ge(S["sent"], 16 * B)

        @block.vector
        def _(dve):
            LINKS = 9

            def prepare(b):
                link = Links(dve, S["linked"], b * LINKS)
                for t in range(T):
                    ins = nc.vector.bn_stats(st[:, t, :], xs[:, b * T + t, :])
                link(ins)
                nc.vector.tensor_tensor(msum[:], st[:, :, 1], st[:, :, 4], ALU.add)
                nc.vector.tensor_tensor(t1[:], st[:, :, 1], st[:, :, 4], ALU.subtract)
                link(nc.vector.tensor_tensor(var[:], st[:, :, 2], st[:, :, 5], ALU.add))
                link(nc.vector.scalar_tensor_tensor(t1[:], t1[:], 0.25, t1[:], ALU.mult, ALU.mult))
                nc.vector.scalar_tensor_tensor(var[:], var[:], 1.0 / D, t1[:], ALU.mult, ALU.add).then_inc(
                    S["stats"], 1)
                dve.wait_ge(S["rstd"], b + 1)
                dve.wait_ge(S["stats"], b + 1)
                link(nc.vector.scalar_tensor_tensor(t1[:], r0[:], -0.5, r0[:], ALU.mult, ALU.mult))
                link(nc.vector.scalar_tensor_tensor(t1[:], var[:], EPS, t1[:], ALU.add, ALU.mult))
                link(nc.vector.scalar_tensor_tensor(rs[:], t1[:], 1.5, r0[:], ALU.add, ALU.mult))
                link(nc.vector.scalar_tensor_tensor(nmr[:], msum[:], -0.5, rs[:], ALU.mult, ALU.mult))
                wait_past(dve, S["turned"], b * 4)
                wait_past(dve, S["h_added"], b)
                for t in range(T):
                    nc.vector.tensor_scalar(h[:, t, :], xs[:, b * T + t, :], rs[:, t:t + 1], nmr[:, t:t + 1],
                                            ALU.mult, ALU.add).then_inc(S["h_ready"], 1)
                dve.wait_ge(S["h_ready"], (b + 1) * T)
                for t in range(T):
                    ins = nc.vector.tensor_tensor_reduce(hw[:, t, :], h[:, t, :], C.wr[:], 1.0, 0.0, ALU.mult,
                                                         ALU.add, score[:, t:t + 1])
                ins.then_inc(S["scored"], 1)
                dve.wait_ge(S["scored"], b + 1)
                nc.vector.tensor_copy(spread[:], score[:].unsqueeze(2).broadcast_to([P, T, P])).then_inc(
                    S["spread"], 1)
                dve.wait_ge(S["row_filled"], b + 1)
                for t in range(T):
                    s = score[:, t:t + 1]
                    if t:
                        nc.vector.tensor_scalar(above[:, t, 0:t * P], ps_r[:, 0:t * P], s, None, ALU.is_ge, ALU.add,
                                                accum_out=cnt[:, t, 0:1])
                    nc.vector.tensor_scalar(above[:, t, t * P:L], ps_r[:, t * P:L], s, None, ALU.is_gt, ALU.add,
                                            accum_out=cnt[:, t, 1:2])
                    ins = nc.vector.scalar_tensor_tensor(equal[:, t, :], ps_r[:, t * P:(t + 1) * P], s, C.tri[:],
                                                         ALU.is_equal, ALU.mult, accum_out=cnt[:, t, 2:3])
                ins.then_inc(S["counted"], 1)
                dve.wait_ge(S["counted"], b + 1)
                link(nc.vector.tensor_tensor(rank[:], cnt[:, :, 0], cnt[:, :, 1], ALU.add))
                link(nc.vector.tensor_tensor(rank[:], rank[:], cnt[:, :, 2], ALU.add))
                dve.wait_ge(S["sigmoid"], b + 1)
                nc.vector.scalar_tensor_tensor(coef[:, b % 2, :], rank[:], KEEP - 0.5, sig[:], ALU.is_lt,
                                               ALU.mult).then_inc(S["coef_ready"], 1)
                assert link.n == LINKS

            def use(b):
                dve.wait_ge(S["coef_ready"], b + 1)
                dve.wait_ge(S["h_added"], b + 1)
                for t in range(T):
                    n = b * T + t
                    dve.wait_ge(S["product"], n + 1)
                    nc.vector.tensor_tensor(biased[:, t % 2, :], ps_o[:, t % 2, 0:D], C.b2[:], ALU.add).then_inc(
                        S["biased"], 1)
                    dve.wait_ge(S["biased"], n + 1)
                    rows = xs[:, n, :]
                    nc.vector.scalar_tensor_tensor(rows, biased[:, t % 2, :], coef[:, b % 2, t:t + 1], rows,
                                                   ALU.mult, ALU.add).then_inc(S["updated"], 1)

            nc.vector.memset(cnt[:, 0, 0:1], 0.0)
            over_batches(dve, prepare, use)

        @block.scalar
        def _(act):
            def prepare(b):
                act.wait_ge(S["stats"], b + 1)
                nc.scalar.activation(lnv[:], var[:], ACT.Ln, bias=C.eps[:]).then_inc(S["logged"], 1)
                act.wait_ge(S["logged"], b + 1)
                nc.scalar.activation(r0[:], lnv[:], ACT.Exp, scale=-0.5).then_inc(S["rstd"], 1)
                for g in range(4):
                    act.wait_ge(S["turned"], b * 4 + g + 1)
                    k, half = g // 2, g % 2
                    nc.scalar.copy(ht[:, b % 2, k, half * HALF:(half + 1) * HALF], ps_t[:, g % 2, :]).then_inc(
                        S["ht_read"], 1)
                act.wait_ge(S["scored"], b + 1)
                nc.scalar.activation(sig[:], score[:], ACT.Sigmoid).then_inc(S["sigmoid"], 1)

            def use(b):
                for half in range(2):
                    for f in range(FT):
                        n = b * 2 * FT + half * FT + f
                        act.wait_ge(S["hidden"], n + 1)
                        nc.scalar.activation(gt[:, half, f, :], ps_h[:, f % 2, :], ACT.Gelu_apprx_tanh,
                                             bias=C.b1[:, f:f + 1]).then_inc(S["gelu"], 1)
            over_batches(act, prepare, use)

        @block.tensor
        def _(pe):
            pe.wait_ge(S["loaded"], 32)

            def prepare(b):
                for g in range(4):
                    k, half = g // 2, g % 2
                    pe.wait_ge(S["h_ready"], b * T + (half + 1) * TH)
                    if g >= 2:
                        pe.wait_ge(S["ht_read"], b * 4 + g - 1)
                    else:
                        wait_past(pe, S["ht_read"], b * 4)
                    for i in range(TH):
                        t = half * TH + i
                        mm = nc.tensor.transpose(ps_t[:, g % 2, i * P:(i + 1) * P], h[:, t, k * P:(k + 1) * P],
                                                 C.ident[:])
                    mm.then_inc(S["turned"], 1)
                pe.wait_ge(S["spread"], b + 1)
                wait_past(pe, S["coef_ready"], b)
                for t in range(T):
                    mm = nc.tensor.transpose(ps_r[:, t * P:(t + 1) * P], spread[:, t, :], C.ident[:])
                mm.then_inc(S["row_filled"], 1)

            def use(b):
                pe.wait_ge(S["ht_read"], (b + 1) * 4)
                for half in range(2):
                    for f in range(FT):
                        n = half * FT + f
                        if n >= 2:
                            pe.wait_ge(S["gelu"], b * 2 * FT + n - 1)
                        else:
                            wait_past(pe, S["gelu"], b * 2 * FT)
                        for k in range(KD):
                            mm = nc.tensor.matmul(ps_h[:, f % 2, :], W1[:, k, f * P:(f + 1) * P],
                                                  ht[:, b % 2, k, half * HALF:(half + 1) * HALF],
                                                  start=(k == 0), stop=(k == KD - 1))
                        mm.then_inc(S["hidden"], 1)
                for t in range(T):
                    if t % TH == 0:
                        pe.wait_ge(S["gelu"], b * 2 * FT + (t // TH + 1) * FT)
                    if t >= 2:
                        pe.wait_ge(S["biased"], b * T + t - 1)
                    else:
                        wait_past(pe, S["biased"], b * T)
                    for f in range(FT):
                        mm = nc.tensor.matmul(ps_o[:, t % 2, 0:D], gt[:, t // TH, f, (t % TH) * P:(t % TH + 1) * P],
                                              W2[:, f, :], start=(f == 0), stop=(f == FT - 1))
                    mm.then_inc(S["product"], 1)
            over_batches(pe, prepare, use)

        @block.gpsimd
        def _(pool):
            with pool.Fori(0, B) as b:
                pool.wait_ge(S["h_ready"], b * T + T)
                rows = xs[:, bass.ts(b, T), :]
                nc.gpsimd.tensor_tensor(rows, rows, h[:], ALU.add).then_inc(S["h_added"], 1)



class Shared:
    pass


def program(nc, dram, out):
    nc.disable_value_cache = True
    with ExitStack() as ctx:
        def sb(name, shape, dt=F32):
            return ctx.enter_context(nc.sbuf_tensor(name, shape, dt))

        def sem(name):
            return ctx.enter_context(nc.semaphore(name))

        C, G = Shared(), Shared()
        C.xs = sb("xs", [P, B * T, D])
        C.ident = sb("ident", [P, P])
        C.identb = sb("identb", [P, P], BF16)
        C.ones = sb("ones", [P, P])
        C.zerosb = sb("zerosb", [P, P], BF16)
        C.tri = sb("tri", [P, P])
        C.block_qk = sb("block_qk", [P, P], BF16)
        C.block_kq = sb("block_kq", [P, P], BF16)
        C.lastrow = sb("lastrow", [P, T])
        C.eps = sb("eps", [P, 1])
        C.bo = sb("bo", [P, D])
        C.bv = sb("bv", [P, D])
        C.woT = sb("woT", [P, KD, D])
        C.wr = sb("wr", [P, D])
        C.b1 = sb("b1", [P, FT])
        C.b2 = sb("b2", [P, D])
        G.xsum = sb("xsum", [P, KD, B])
        G.gneg = sb("gneg", [P, B * H])
        G.qscale = sb("qscale", [P, NPAIR])
        G.qbias = sb("qbias", [P, NPAIR])
        G.kbias = sb("kbias", [P, NPAIR])
        C.ht_dram = nc.dram_tensor("ht_scratch", (B, P, KD, L), F32, kind="Internal").ap()
        C.g_dram = nc.dram_tensor("g_scratch", (B, H), F32, kind="Internal").ap()

        constants_phase(nc, sem, C, dram)
        norm_phase(nc, sem, C, "n0_", x_in=dram["x"], gates=G)
        gates_phase(nc, sem, C, G, dram)
        attention_phase(nc, sem, C, G, dram, True)
        ffn_phase(nc, sem, C, dram, "f1_")
        norm_phase(nc, sem, C, "n1_")
        attention_phase(nc, sem, C, G, dram, False)
        ffn_phase(nc, sem, C, dram, "f2_", out)


def layout(inputs):
    import numpy as np
    a = {k: np.asarray(v) for k, v in inputs.items()}
    at = lambda n: a["L0_attn_a_" + n]
    c = np.ascontiguousarray

    def per_pair(ws):
        w = np.stack([x.reshape(KD, P, KD, P) for x in ws])
        return c(w.transpose(3, 2, 0, 1, 4))
    wqkv = a["L0_attn_b_w_qkv"]
    return {
        "x": c(at("x")), "bo": at("bo"), "bv": at("bv"), "bq": at("bq"), "bk": at("bk"),
        "woT": c(at("wo").T),
        "wpairA": per_pair([at("wq").T, at("wk").T, at("wv").T]),
        "wpairB": per_pair([wqkv[:, 0:D], wqkv[:, D:2 * D], wqkv[:, 2 * D:3 * D]]),
        "gw1": c(np.concatenate([at("pw1"), at("sw1")[None]]).transpose(2, 0, 1)),
        "gb1": c(np.concatenate([at("pb1"), at("sb1")[None]])),
        "gw2": c(np.concatenate([at("pw2").reshape(NE * H, DH), at("sw2")]).T),
        "gb2": c(np.concatenate([at("pb2").reshape(NE * H), at("sb2")])),
        "wr": a["L0_ffn_w_router"], "W1": a["L0_ffn_W1"], "b1": a["L0_ffn_b1"],
        "W2": a["L0_ffn_W2"], "b2": a["L0_ffn_b2"],
    }


def kernel(**inputs):
    import concourse.bacc as bacc
    from concourse.bass_utils import run_bass_kernel_spmd

    nc = bacc.Bacc("TRN2", target_bir_lowering=False, num_devices=1)
    arrays = {f"in_{k}": v for k, v in layout(inputs).items()}
    dram = {k[3:]: nc.dram_tensor(k, v.shape, mybir.dt.from_np(v.dtype), kind="ExternalInput").ap()
            for k, v in arrays.items()}
    out = nc.dram_tensor("out_dram", (B, L, D), F32, kind="ExternalOutput").ap()
    program(nc, dram, out)
    return run_bass_kernel_spmd(nc, [arrays], core_ids=[0]).results[0]["out_dram"]
```

```python
from contextlib import ExitStack

import concourse.bass as bass
from concourse import mybir

P = 128
F32 = mybir.dt.float32
BF16 = mybir.dt.bfloat16
U32 = mybir.dt.uint32
ALU = mybir.AluOpType
ACT = mybir.ActivationFunctionType
AX_X = mybir.AxisListType.X

B, L, D = 8, 1024, 256
H, HD = 16, 16
T = L // P
KD = D // P
HALF = L // 2
TH = T // 2
NE, DH = 3, 128
F = 1024
FT = F // P
KEEP = L // 2
TK = KEEP // P
EPS = 1e-5
MASKED = -1.0e9
BLOCKED = -1.0e30
HP = 8
QH = 4
NPAIR = B * H // HP
SLOT = 32
ONE = HD
PARTS = 3
PRODUCTS = [(0, 0), (0, 1), (1, 0), (1, 1), (0, 2), (2, 0)]
KS = HD * len(PRODUCTS)


class Links:

    def __init__(self, eng, sem, base=0):
        self.eng, self.sem, self.base, self.n = eng, sem, base, 0

    def __call__(self, ins):
        self.n += 1
        ins.then_inc(self.sem, 1)
        self.eng.wait_ge(self.sem, self.base + self.n)


def wait_past(eng, sem, value):
    if not (isinstance(value, int) and value <= 0):
        eng.wait_ge(sem, value)


def peel_first(eng, count, each):
    each(0)
    with eng.Fori(1, count) as b:
        each(b)


def norm_phase(nc, sem, C, tag, x_in=None, gates=None):
    xs = C.xs
    x_here, linked, stats, rstd, h_ready, filled, ht_ready, stored, ht_sent, bo_added = (
        sem(tag + n) for n in ("x_here", "linked", "stats", "rstd", "h_ready", "filled", "ht_ready",
                               "stored", "ht_sent", "bo_added"))
    with ExitStack() as ctx:
        def sb(name, shape, dt=F32):
            return ctx.enter_context(nc.sbuf_tensor(tag + name, shape, dt))
        h = sb("h", [P, T, D])
        st = sb("st", [P, T, 6])
        var = sb("var", [P, T])
        msum = sb("msum", [P, T])
        r0 = sb("r0", [P, T])
        lnv = sb("lnv", [P, T])
        t1 = sb("t1", [P, T])
        rs = sb("rs", [P, T])
        nmr = sb("nmr", [P, T])
        hts = sb("hts", [P, 2, KD, L])
        psT = ctx.enter_context(nc.psum_tensor(tag + "psT", [P, KD, L], F32))
        block = ctx.enter_context(nc.Block())

        @block.sync
        def _(sp):
            if x_in is not None:
                for b in range(B):
                    sp.dma_start(xs[:, b * T:(b + 1) * T, :],
                                 x_in[b].rearrange("(t p) d -> p t d", p=P)).then_inc(x_here, 16)
                    sp.wait_ge(x_here, b * 16 + 16)
            sp.sem_inc(ht_sent, 16)
            for b in range(B):
                sp.wait_ge(ht_ready, b * 2 + 2)
                sp.dma_start(C.ht_dram[b], hts[:, b % 2]).then_inc(ht_sent, 16)
                sp.wait_ge(ht_sent, b * 16 + 32)

        @block.vector
        def _(dve):
            def variances(b):
                link = Links(dve, linked, b * 7)
                if x_in is not None:
                    dve.wait_ge(x_here, b * 16 + 16)
                for t in range(T):
                    ins = nc.vector.bn_stats(st[:, t, :], xs[:, b * T + t, :])
                link(ins)
                nc.vector.tensor_tensor(msum[:], st[:, :, 1], st[:, :, 4], ALU.add)
                nc.vector.tensor_tensor(t1[:], st[:, :, 1], st[:, :, 4], ALU.subtract)
                link(nc.vector.tensor_tensor(var[:], st[:, :, 2], st[:, :, 5], ALU.add))
                link(nc.vector.scalar_tensor_tensor(t1[:], t1[:], 0.25, t1[:], ALU.mult, ALU.mult))
                nc.vector.scalar_tensor_tensor(var[:], var[:], 1.0 / D, t1[:], ALU.mult, ALU.add).then_inc(stats, 1)

            def normalise(b):
                link = Links(dve, linked, b * 7 + 3)
                dve.wait_ge(rstd, b + 1)
                dve.wait_ge(stats, b + 1)
                link(nc.vector.scalar_tensor_tensor(t1[:], r0[:], -0.5, r0[:], ALU.mult, ALU.mult))
                link(nc.vector.scalar_tensor_tensor(t1[:], var[:], EPS, t1[:], ALU.add, ALU.mult))
                link(nc.vector.scalar_tensor_tensor(rs[:], t1[:], 1.5, r0[:], ALU.add, ALU.mult))
                link(nc.vector.scalar_tensor_tensor(nmr[:], msum[:], -0.5, rs[:], ALU.mult, ALU.mult))
                wait_past(dve, filled, b * 4)
                for t in range(T):
                    nc.vector.tensor_scalar(h[:, t, :], xs[:, b * T + t, :], rs[:, t:t + 1], nmr[:, t:t + 1],
                                            ALU.mult, ALU.add).then_inc(h_ready, 1)

            def each(b):
                normalise(b)
                variances(b + 1)
            variances(0)
            peel_first(dve, B - 1, each)
            normalise(B - 1)

        @block.scalar
        def _(act):
            def inverse_roots(b):
                act.wait_ge(stats, b + 1)
                nc.scalar.activation(lnv[:], var[:], ACT.Ln, bias=C.eps[:]).then_inc(stored, 1)
                act.wait_ge(stored, b + 1)
                nc.scalar.activation(r0[:], lnv[:], ACT.Exp, scale=-0.5).then_inc(rstd, 1)

            def read_turned(b):
                wait_past(act, ht_sent, b * 16)
                for k in range(KD):
                    act.wait_ge(filled, b * 4 + 2 * k + 2)
                    accum = None if gates is None else gates.xsum[:, k, bass.ts(b, 1)]
                    nc.scalar.activation(hts[:, b % 2, k, :], psT[:, k, :], ACT.Identity,
                                         accum_out=accum).then_inc(ht_ready, 1)

            def each(b):
                read_turned(b)
                inverse_roots(b + 1)
            inverse_roots(0)
            peel_first(act, B - 1, each)
            read_turned(B - 1)

        @block.tensor
        def _(pe):
            def each(b):
                for k in range(KD):
                    for half in range(2):
                        pe.wait_ge(h_ready, b * T + (half + 1) * TH)
                        if half == 0:
                            wait_past(pe, ht_ready, b * 2)
                        for i in range(TH):
                            t = half * TH + i
                            mm = nc.tensor.transpose(psT[:, k, t * P:(t + 1) * P], h[:, t, k * P:(k + 1) * P],
                                                     C.ident[:])
                        mm.then_inc(filled, 1)
            peel_first(pe, B, each)

        if x_in is not None:
            @block.gpsimd
            def _(pool):
                def each(b):
                    pool.wait_ge(h_ready, b * T + T)
                    nc.gpsimd.tensor_tensor(xs[:, bass.ts(b, T), :], xs[:, bass.ts(b, T), :],
                                            C.bo[:].unsqueeze(1).broadcast_to([P, T, D]),
                                            ALU.add).then_inc(bo_added, 1)
                peel_first(pool, B, each)


def constants_phase(nc, sem, C, dram):
    loaded, made, step = sem("c_loaded"), sem("c_made"), sem("c_step")
    with nc.Block() as block:
        @block.sync
        def _(sp):
            loads = [
                (C.bo[:], dram["bo"].partition_broadcast(P)),
                (C.woT[:], dram["woT"].rearrange("(m p) n -> p m n", p=P)),
                (C.bv[:], dram["bv"].partition_broadcast(P)),
                (C.wr[:], dram["wr"].partition_broadcast(P)),
                (C.b2[:], dram["b2"].partition_broadcast(P)),
                (C.b1[:], dram["b1"].rearrange("(f p) -> p f", p=P)),
            ]
            for dst, src in loads:
                sp.dma_start(dst, src, allow_slow_non_contiguous=True).then_inc(loaded, 16)
            sp.wait_ge(loaded, 16 * len(loads))

        @block.vector
        def _(dve):
            nc.vector.memset(C.eps[:], EPS).then_inc(made, 1)
            nc.vector.memset(C.ones[:], 1.0).then_inc(made, 1)
            nc.vector.memset(C.zerosb[:], 0.0).then_inc(made, 1)

        @block.gpsimd
        def _(pool):
            pool.wait_ge(made, 3)
            def keep(out, in_, op, fill, pattern, base, ch):
                return nc.gpsimd.affine_select(out=out, in_=in_, compare_op=op, fill=fill, base=base,
                                               pattern=pattern, channel_multiplier=ch)
            keep(C.ident[:], C.ones[:], ALU.is_equal, 0.0, [[-1, P]], 0, 1).then_inc(step, 1)
            pool.wait_ge(step, 1)
            nc.gpsimd.tensor_copy(C.identb[:], C.ident[:]).then_inc(step, 1)
            keep(C.tri[:], C.ones[:], ALU.is_gt, 0.0, [[-1, P]], 0, 1).then_inc(step, 1)
            keep(C.block_qk[:], C.zerosb[:], ALU.is_ge, BLOCKED, [[-1, P]], 0, 1).then_inc(step, 1)
            keep(C.block_kq[:], C.zerosb[:], ALU.is_ge, BLOCKED, [[1, P]], 0, -1).then_inc(step, 1)
            keep(C.lastrow[:], C.ones[:, 0:T], ALU.not_equal, 3.0e29, [[P, T]], 1 - L, 1).then_inc(step, 1)


def gates_phase(nc, sem, C, G, dram):
    loaded, mm_done, act_done, linked, g_out, g_in, ready = (
        sem("g_" + n) for n in ("loaded", "mm", "act", "linked", "out", "in", "ready"))
    NG = NE + 1
    with ExitStack() as ctx:
        def sb(name, shape, dt=F32):
            return ctx.enter_context(nc.sbuf_tensor("g_" + name, shape, dt))
        w1 = sb("w1", [P, KD, NG, DH])
        bias1 = sb("bias1", [P, NG])
        w2 = sb("w2", [P, NE * H + NE])
        bias2 = sb("bias2", [B, NE * H + NE])
        hid = sb("hid", [P, NG, B])
        lg = sb("lg", [B, NE * H + NE])
        mx = sb("mx", [B, NG])
        ex = sb("ex", [B, NE * H + NE])
        sm = sb("sm", [B, NG])
        hg = sb("hg", [B, H])
        bqc = sb("bqc", [P, KD])
        bkc = sb("bkc", [P, KD])
        ps1 = ctx.enter_context(nc.psum_tensor("g_ps1", [P, NG, B], F32))
        ps2 = ctx.enter_context(nc.psum_tensor("g_ps2", [P, NE * H + NE], F32))
        block = ctx.enter_context(nc.Block())
        experts = lambda t: t[:, 0:NE * H].rearrange("b (e h) -> b e h", e=NE)
        policy = lambda t: t[:, NE * H:NE * H + NE]

        @block.sync
        def _(sp):
            loads = [(w1[:], dram["gw1"].rearrange("(k p) g c -> p k g c", p=P)),
                     (bias1[:], dram["gb1"].rearrange("g c -> c g")),
                     (w2[:], dram["gw2"]), (bias2[:], dram["gb2"].partition_broadcast(B)),
                     (bqc[:], dram["bq"].rearrange("(m p) -> p m", p=P)),
                     (bkc[:], dram["bk"].rearrange("(m p) -> p m", p=P))]
            for dst, src in loads:
                sp.dma_start(dst, src, allow_slow_non_contiguous=True).then_inc(loaded, 16)
            sp.wait_ge(loaded, 16 * len(loads))
            sp.wait_ge(linked, G_LINKS)
            sp.dma_start(C.g_dram, hg[:]).then_inc(g_out, 16)
            sp.wait_ge(g_out, 16)
            sp.dma_start(G.gneg[:], C.g_dram.rearrange("b h -> (b h)").partition_broadcast(P)).then_inc(g_in, 16)
            for hh in range(HP):
                src = C.g_dram.rearrange("b (m h) -> h (b m)", m=KD)[hh]
                sp.dma_start(G.qscale[hh * HD:(hh + 1) * HD, :], src.partition_broadcast(HD),
                             allow_slow_non_contiguous=True).then_inc(g_in, 16)
            sp.wait_ge(g_in, 16 * (HP + 1))

        @block.tensor
        def _(pe):
            pe.wait_ge(loaded, 16 * 6)
            for g in range(NG):
                for k in range(KD):
                    mm = nc.tensor.matmul(ps1[:, g, :], w1[:, k, g, :], G.xsum[:, k, :],
                                          start=(k == 0), stop=(k == KD - 1))
            mm.then_inc(mm_done, 1)
            pe.wait_ge(act_done, NG)
            for e in range(NE):
                nc.tensor.matmul(ps2[0:B, e * H:(e + 1) * H], hid[:, e, :], w2[:, e * H:(e + 1) * H],
                                 start=True, stop=True)
            nc.tensor.matmul(policy(ps2[0:B]), hid[:, NE, :], policy(w2), start=True, stop=True).then_inc(mm_done, 1)

        @block.scalar
        def _(act):
            act.wait_ge(loaded, 16 * 6)
            act.wait_ge(mm_done, 1)
            for g in range(NG):
                nc.scalar.activation(hid[:, g, :], ps1[:, g, :], ACT.Gelu, bias=bias1[:, g:g + 1],
                                     scale=1.0 / L).then_inc(act_done, 1)
            act.wait_ge(linked, 3)
            nc.scalar.activation(ex[:], lg[:], ACT.Exp).then_inc(act_done, 1)

        @block.vector
        def _(dve):
            link = Links(dve, linked)
            dve.wait_ge(mm_done, 2)
            link(nc.vector.tensor_tensor(lg[:], ps2[0:B, :], bias2[:], ALU.add))
            nc.vector.tensor_reduce(mx[:, 0:NE], experts(lg), AX_X, ALU.max)
            link(nc.vector.tensor_reduce(mx[:, NE:NG], policy(lg), AX_X, ALU.max))
            nc.vector.tensor_tensor(experts(lg), experts(lg), mx[:, 0:NE].unsqueeze(2).broadcast_to([B, NE, H]),
                                    ALU.subtract)
            link(nc.vector.tensor_scalar(policy(lg), policy(lg), mx[:, NE:NG], None, ALU.subtract))
            dve.wait_ge(act_done, NG + 1)
            nc.vector.tensor_reduce(sm[:, 0:NE], experts(ex), AX_X, ALU.add)
            link(nc.vector.tensor_reduce(sm[:, NE:NG], policy(ex), AX_X, ALU.add))
            link(nc.vector.reciprocal(sm[:], sm[:]))
            link(nc.vector.tensor_scalar(policy(ex), policy(ex), sm[:, NE:NG], None, ALU.mult))
            link(nc.vector.tensor_tensor(sm[:, 0:NE], sm[:, 0:NE], policy(ex), ALU.mult))
            link(nc.vector.tensor_scalar(hg[:], ex[:, 0:H], sm[:, 0:1], None, ALU.mult))
            for e in range(1, NE):
                link(nc.vector.scalar_tensor_tensor(hg[:], ex[:, e * H:(e + 1) * H], sm[:, e:e + 1], hg[:],
                                                    ALU.mult, ALU.add))
            assert link.n == G_LINKS
            dve.wait_ge(g_in, 16 * (HP + 1))
            link(nc.vector.tensor_scalar(G.qscale[:], G.qscale[:], 0.25, None, ALU.mult))
            per_pair = lambda t: t[:].rearrange("p (b m) -> p b m", m=KD)
            over_b = lambda t: t[:].unsqueeze(1).broadcast_to([P, B, KD])
            nc.vector.tensor_tensor(per_pair(G.qbias), per_pair(G.qscale), over_b(bqc), ALU.mult)
            nc.vector.tensor_copy(per_pair(G.kbias), over_b(bkc))
            nc.vector.tensor_scalar(G.gneg[:], G.gneg[:], MASKED, None, ALU.mult).then_inc(ready, 1)


G_LINKS = 10



NB = 3
BUFS = 3
STEP = 3
TAIL = 3
SHIFT_AT = 6
LEFT = 1
COST = {"smax": 3, "project": 6, "values": 4, "ctx": 4, "masked": 3, "turn": 3, "out": 3, "shift": 3,
        "split_hi": 3, "split_mid": 3, "combine": 1}


def key_tiles(causal, j):
    return TH if causal and j % 2 == 0 else T


def halfstep(causal, j, first, last):
    smax_j = j + 2
    ev = []
    if not (last and j == 3):
        ev.append(("step", "combine", (j + 1) % 4, "dve"))
        if causal:
            ev.append(("step", "weight", (j + 1) % 4, "act"))
    before = []
    if not (last and j >= 2):
        for h in range(QH):
            for i in range(TH):
                pieces = 1 if causal and smax_j % 2 == 0 else 2
                before += [("bank", "smax", (smax_j % 4, h, i, c), "dve") for c in range(pieces)]
    extra = []
    if not (first and j == 0):
        if causal:
            extra.append(("bank", "masked", (j - 1) % 4, "dve"))
        extra.append(("bank", "ctx", (j - 1) % 4, "dve"))
    if not last and j == 0:
        for qk in range(2):
            extra += [("bank", "project", (qk, 0), "act"), ("bank", "project", (qk, 1), "act"),
                      ("step", "split_hi", qk, "dve"), ("step", "split_mid", qk, "dve")]
    if not last and j == 1:
        extra += [("bank", "values", 0, "dve"), ("bank", "values", 1, "dve")]
    if causal and (j == 3 or (j == 0 and not first)):
        half = 0 if j == 3 else 1
        extra += [("bank", "turn", half, "act"), ("bank", "out", (half, 0), "dve"), ("bank", "out", (half, 1), "dve")]
    if not (last and j == 3):
        before.insert(min(SHIFT_AT, len(before)), ("bank", "shift", (j + 1) % 4, "dve"))
    n, m = len(before), len(extra)
    at = {min(n, 4 + (n - 4) * i // m) if n else 0: [] for i in range(m)} if m else {}
    for i, e in enumerate(extra):
        at[min(n, 4 + (n - 4) * i // m) if n else 0].append(e)
    for i in range(n + 1):
        ev += at.get(i, [])
        if i < n:
            ev.append(before[i])
    units = [(kt, hp) for kt in range(key_tiles(causal, j)) for hp in range(2)]
    main = []
    for kt, hp in units:
        main.append((2, ("unit", kt, hp)))
        if hp == 1 and kt > 0:
            main.append((4, ("values_in", kt - 1)))
    main.append((4, ("values_in", key_tiles(causal, j) - 1)))
    cost = lambda x: COST.get(x[1], 0)
    whole, rest = sum(c for c, _ in main[:-1]), sum(map(cost, ev))
    left = min(rest, LEFT * COST["smax"])
    order, spent, at_main = [], 0, 0
    for c, x in main:
        now = rest if x == main[-1][1] else (rest - left) * at_main / whole
        while ev and (spent < now or x == main[-1][1]):
            spent += cost(ev[0])
            order.append(ev.pop(0))
        order.append(x)
        at_main += c
    order.append(("step", "evacuate", j, "act"))
    return order


class Plan:

    def __init__(self, causal):
        self.causal = causal
        proj = [("bank", "project", (qk, h), "act") if h < 2 else
                ("step", "split_hi" if h == 2 else "split_mid", qk, "dve") for qk in range(2) for h in range(4)]
        vals = [("bank", "values", 0, "dve"), ("bank", "values", 1, "dve")]
        smax = [("bank", "smax", (j, h, i, c), "dve") for j in range(2) for h in range(QH) for i in range(TH)
                for c in range(1 if causal and j == 0 else 2)]
        shift = [("step", "combine", 0, "dve")] + ([("step", "weight", 0, "act")] if causal else []) + [
            ("bank", "shift", 0, "dve")]
        self.parts = {"start": [proj + vals + smax + shift]}
        pairs = {"first": [(True, False)], "loop": [(False, False)] * STEP,
                 "last": [(False, False)] * (TAIL - 1) + [(False, True)]}
        for name, kinds in pairs.items():
            self.parts[name] = [halfstep(causal, j, *k) for k in kinds for j in range(4)]
        tail = [("bank", "masked", 3, "dve")] if causal else []
        tail.append(("bank", "ctx", 3, "dve"))
        if causal:
            tail += [("bank", "turn", 1, "act"), ("bank", "out", (1, 0), "dve"), ("bank", "out", (1, 1), "dve")]
        self.parts["end"] = [tail]
        self.flat = {k: [x for seq in v for x in seq] for k, v in self.parts.items()}

    @staticmethod
    def matches(x, what):
        if what == "bank":
            return x[0] == "bank"
        if what.endswith(" bank"):
            return x[0] == "bank" and x[3] == what.split()[0]
        if what in ("unit", "values_in"):
            return x[0] == what
        return x[0] in ("bank", "step") and x[1] == what

    def count(self, part, what, upto=None):
        return sum(self.matches(x, what) for x in self.flat[part][:upto])

    def base(self, part, u, what):
        n = 0 if part == "start" else self.count("start", what)
        if part in ("loop", "last", "end"):
            n += self.count("first", what)
        per = self.count("loop", what) // STEP
        assert per * STEP == self.count("loop", what)
        if part == "loop":
            return (u - 1) * per + n
        if part in ("last", "end"):
            n += (NPAIR - 1 - TAIL) * per
        if part == "end":
            n += self.count("last", what)
        return n

    def bank_of(self, part, pos):
        return (self.count(part, "bank", pos) - self.count(part, "bank")) % NB

    PRIOR = {"first": "start", "loop": "loop", "last": "loop", "end": "last"}

    def read(self, part, pos, u, kind, arg):
        is_it = lambda x: x[0] == "bank" and x[1] == kind and x[2] == arg
        seen = [i for i in range(pos) if is_it(self.flat[part][i])]
        if seen:
            i = seen[-1]
            who = self.flat[part][i][3] + " bank"
            return self.base(part, u, who) + self.count(part, who, i + 1)
        prior = self.PRIOR[part]
        i = max(i for i, x in enumerate(self.flat[prior]) if is_it(x))
        who = self.flat[prior][i][3] + " bank"
        return self.base(part, u, who) - self.count(prior, who) + self.count(prior, who, i + 1)

    def bank_free(self, part, pos, u):
        bank = self.bank_of(part, pos)
        seen = [i for i in range(pos) if self.flat[part][i][0] == "bank" and self.bank_of(part, i) == bank]
        if seen:
            i = seen[-1]
            who = self.flat[part][i][3]
            return who, self.base(part, u, who + " bank") + self.count(part, who + " bank", i + 1)
        if part == "start":
            return None
        prior = self.PRIOR[part]
        i = max(i for i, x in enumerate(self.flat[prior]) if x[0] == "bank" and self.bank_of(prior, i) == bank)
        who = self.flat[prior][i][3]
        later = self.count(prior, who + " bank") - self.count(prior, who + " bank", i + 1)
        return who, self.base(part, u, who + " bank") - later


def attention_phase(nc, sem, C, G, dram, causal):
    tag = "a_" if causal else "b_"
    plan = Plan(causal)
    xs = C.xs
    names = ["loaded", "filled", "dve_read", "act_read", "st_filled", "exp_done", "pv_done", "evacuated", "maxima",
             "parts_ready", "shift_in", "split_hi", "split_mid", "rest_1", "split_lo", "scratch_out", "stack_in",
             "v_ready", "ones_ready", "linked", "pool_linked", "weights", "added", "vsum_ready",
             "shift_ones", "sp_passed", "pool_passed"]
    S = {n: sem(tag + n) for n in names}
    wpair = dram["wpairA" if causal else "wpairB"]
    with ExitStack() as ctx:
        def sb(name, shape, dt=F32):
            return ctx.enter_context(nc.sbuf_tensor(tag + name, shape, dt))
        ht = sb("ht", [P, KD, L])
        w = sb("w", [P, 3, KD, P])
        q32 = sb("q32", [P, 2, L])
        parts = sb("parts", [P, 2, PARTS, L], BF16)
        qst = sb("qst", [KS + PARTS, 3, 2, QH, HALF], BF16)
        kst = sb("kst", [KS + PARTS, 3, QH, L], BF16)
        pt = sb("pt", [P, 2, QH, HALF])
        vnew = sb("vnew", [P, T, P])
        v = sb("v", [P, 2, T, QH, SLOT])
        ctxs = sb("ctxs", [P, 2, HALF])
        tmp = sb("tmp", [P, 2, TH, QH, HD])
        rden = sb("rden", [P, TH, QH])
        part_max = sb("part_max", [P, 2, QH, TH, 2])
        mx = sb("mx", [P, QH, TH])
        nmax = sb("nmax", [P, 2, QH, TH])
        mrest = sb("mrest", [QH * TH, P])
        mparts = sb("mparts", [QH * TH, 2, PARTS, P], BF16)
        if causal:
            vsum = sb("vsum", [P, 2, T, QH, SLOT])
            cneg = sb("cneg", [P, QH, TH])
            wlog = sb("wlog", [P, 4, QH, TH])
            wexp = sb("wexp", [P, 4, QH, TH])
            num = sb("num", [P, TH, QH, HD + 1])
            wsum = sb("wsum", [P, TH, QH, HD + 1])
            ctok = sb("ctok", [P, 2, TH, P])
            cts = sb("cts", [P, HALF])
        ps_s = ctx.enter_context(nc.psum_tensor(tag + "ps_s", [P, 2, 2, HALF], F32))
        ps_c = ctx.enter_context(nc.psum_tensor(tag + "ps_c", [P, HALF], F32))
        ps_m = ctx.enter_context(nc.psum_tensor(tag + "ps_m", [P, NB, HALF], F32))
        q_dram = nc.dram_tensor(tag + "q_scratch", (NPAIR, PARTS, 2, 2, P // 2, HALF), BF16, kind="Internal").ap()
        k_dram = nc.dram_tensor(tag + "k_scratch", (NPAIR, PARTS, P, L), BF16, kind="Internal").ap()
        block = ctx.enter_context(nc.Block())

        WRITES = 2 * PARTS + 1
        NU, NV = (plan.count("loop", n) // STEP for n in ("unit", "values_in"))
        assert NU == 2 * NV

        def units_upto(u, j):
            return u * NU + 2 * sum(key_tiles(causal, i) for i in range(j + 1))

        def first_col(j, kt):
            return max(0, kt * P - (j % 2) * HALF) if causal else 0

        def over_parts(eng, each):
            each("start", 0)
            each("first", 0)
            with eng.Fori(1, NPAIR - TAIL, STEP) as u:
                each("loop", u)
            each("last", NPAIR - TAIL)
            each("end", NPAIR)

        def quad_buffer(u, j):
            first = u if isinstance(u, int) else 1
            return (2 * first + j // 2) % BUFS

        def items(part):
            pos = 0
            for seq in plan.parts[part]:
                for x in seq:
                    yield pos, x
                    pos += 1

        def j_of(part, pos):
            n = 0
            for j, seq in enumerate(plan.parts[part]):
                n += len(seq)
                if pos < n:
                    return j

        def upto_projection(u):
            if isinstance(u, int) and u == 1:
                pos = max(i for i, x in enumerate(plan.flat["start"]) if x[1] == "values")
                return plan.count("start", "bank", pos + 1)
            return in_pair(u - 2, "values", 1, "bank")

        def in_pair(p, kind, arg, what):
            part, u, nth = "loop", p, 0
            if isinstance(p, int) and p == 0:
                part = "first"
            elif isinstance(p, int) and p >= NPAIR - TAIL:
                part, u = "last", NPAIR - TAIL
                nth = p - u
            pos = [i for i, x in enumerate(plan.flat[part]) if x[0] == "bank" and x[1] == kind and x[2] == arg][nth]
            return plan.base(part, u, what) + plan.count(part, what, pos + 1)

        @block.sync
        def _(sp):
            def until(s, value):
                sp.wait_ge(s, value)
                if not isinstance(value, int):
                    sp.sem_inc(S["sp_passed"], 1)

            def params(u):
                if not (isinstance(u, int) and u == 0):
                    until(S["filled"], upto_projection(u))
                sp.dma_start(ht[:], C.ht_dram[u // 2]).then_inc(S["loaded"], 16)
                sp.dma_start(w[:], wpair[u % 2]).then_inc(S["loaded"], 16)
                until(S["loaded"], u * 32 + 32)

            def write_parts(u):
                until(S["split_lo"], u * 2 + 1)
                for n in range(2):
                    for c in range(PARTS):
                        sp.dma_start(q_dram[u, c, n].rearrange("f p q -> p f q"),
                                     parts[n * 64:(n + 1) * 64, 0, c, :].rearrange("p (f q) -> p f q", f=2)
                                     ).then_inc(S["scratch_out"], 16)
                until(S["split_lo"], u * 2 + 2)
                sp.dma_start(k_dram[u].rearrange("c p q -> p c q"), parts[:, 1]).then_inc(S["scratch_out"], 16)
                until(S["scratch_out"], (u + 1) * WRITES * 16)

            def load_stack(u, n):
                q = u * 2 + n
                buf = q % 3
                for r, (cq, ck) in enumerate(PRODUCTS):
                    rows = slice(r * HD, (r + 1) * HD)
                    sp.dma_start(qst[rows, buf].rearrange("d f h q -> d (f h) q"),
                                 q_dram[u, cq, n].rearrange("f (h d) q -> d (f h) q", h=QH)).then_inc(
                        S["stack_in"], 16)
                    sp.dma_start(kst[rows, buf], k_dram[u, ck, n * 64:(n + 1) * 64, :].rearrange(
                        "(h d) q -> d h q", h=QH)).then_inc(S["stack_in"], 16)
                until(S["stack_in"], (q + 1) * 2 * 16 * len(PRODUCTS))

            def shift_rows(u, j):
                g = u * 4 + j
                until(S["parts_ready"], g + 1)
                for c in range(PARTS):
                    dst = qst[KS + c:KS + c + 1, (u * 2 + j // 2) % 3, j % 2]
                    sp.dma_start(dst.rearrange("o h (i q) -> o (h i) q", i=TH),
                                 mparts[:, j % 2, c, :]).then_inc(S["shift_in"], 16)
                until(S["shift_in"], (g + 1) * 16 * PARTS)

            params(0)
            write_parts(0)
            load_stack(0, 0)
            load_stack(0, 1)
            params(1)
            shift_rows(0, 0)

            def each(u, last):
                shift_rows(u, 1)
                if not last:
                    write_parts(u + 1)
                    until(S["st_filled"], u * NU)
                    load_stack(u + 1, 0)
                shift_rows(u, 2)
                if not last:
                    until(S["st_filled"], units_upto(u, 1))
                    load_stack(u + 1, 1)
                shift_rows(u, 3)
                if not last:
                    shift_rows(u + 1, 0)

            each(0, False)
            params(2)
            with sp.Fori(1, NPAIR - 2) as u:
                each(u, False)
                params(u + 2)
            each(NPAIR - 2, False)
            each(NPAIR - 1, True)

        @block.tensor
        def _(pe):
            pe.wait_ge(S["shift_ones"], 1)
            pe.wait_ge(S["ones_ready"], 1)

            def bank_item(part, u, pos, x):
                _, kind, arg, who = x
                jj = j_of(part, pos)
                p = u + jj // 4
                bank = plan.bank_of(part, pos)
                free = plan.bank_free(part, pos, u)
                if free is not None:
                    pe.wait_ge(S[free[0] + "_read"], free[1])
                o = ps_m[:, bank, :]
                if kind == "project":
                    qk, half = arg
                    up = 0 if part == "start" else p + 1
                    if half == 0 and qk == 0:
                        pe.wait_ge(S["loaded"], up * 32 + 32)
                    for k in range(KD):
                        mm = nc.tensor.matmul(o, w[:, qk, k, :], ht[:, k, half * HALF:(half + 1) * HALF],
                                              start=(k == 0), stop=(k == KD - 1))
                elif kind == "values":
                    for i in range(TH):
                        t = arg * TH + i
                        for k in range(KD):
                            mm = nc.tensor.matmul(o[:, i * P:(i + 1) * P], ht[:, k, t * P:(t + 1) * P],
                                                  w[:, 2, k, :], start=(k == 0), stop=(k == KD - 1))
                elif kind == "smax":
                    js, h, i, c = arg
                    jabs = js if part == "start" else jj + 2
                    q = u * 2 + jabs // 2
                    if (h, i, c) == (0, 0, 0) and js % 2 == 0:
                        pe.wait_ge(S["stack_in"], (q + 1) * 2 * 16 * len(PRODUCTS))
                    t = (js % 2) * TH + i
                    keys = min(HALF, (t + 1) * P - c * HALF) if causal else HALF
                    diagonal = causal and t // TH == c
                    b3 = quad_buffer(u, jabs)
                    mm = nc.tensor.matmul(o[:, 0:keys], qst[0:KS, b3, t // TH, h, i * P:(i + 1) * P],
                                          kst[0:KS, b3, h, c * HALF:c * HALF + keys], start=True, stop=not diagonal)
                    if diagonal:
                        mm = nc.tensor.matmul(o[:, keys - P:keys], C.identb[:], C.block_qk[:], start=False, stop=True)
                elif kind == "shift":
                    g = 0 if part == "start" else u * 4 + jj + 1
                    pe.wait_ge(S["maxima"], g + 1)
                    mm = nc.tensor.transpose(ps_m[0:QH * TH, bank, 0:P],
                                             nmax[:, arg % 2].rearrange("p h i -> p (h i)"), C.ident[:])
                elif kind == "ctx":
                    g = u * 4 + jj - 1
                    pe.wait_ge(S["evacuated"], g + 1)
                    for i in range(TH):
                        mm = nc.tensor.transpose(o[:, i * P:(i + 1) * P], ctxs[:, arg % 2, i * P:(i + 1) * P],
                                                 C.ident[:])
                elif kind == "masked":
                    pe.wait_ge(S["vsum_ready"], (p - 1 if arg == 3 else p) * 2 + arg // 2 + 1)
                    for i in range(TH):
                        t = (arg % 2) * TH + i
                        flat = lambda a: a[:, arg // 2, t].rearrange("p h c -> p (h c)")
                        nc.tensor.matmul(o[:, i * P:(i + 1) * P], C.tri[:], flat(v), start=True, stop=False)
                        mm = nc.tensor.matmul(o[:, i * P:(i + 1) * P], C.ones[:], flat(vsum), start=False, stop=True)
                elif kind == "turn":
                    pe.wait_ge(S["dve_read"], plan.read(part, pos, u, "ctx", 2 + arg))
                    for i in range(TH):
                        mm = nc.tensor.transpose(o[:, i * P:(i + 1) * P], ctok[:, arg, i, :], C.ident[:])
                elif kind == "out":
                    half, c = arg
                    n = plan.base(part, u, "act bank") + plan.count(part, "act bank", pos)
                    pe.wait_ge(S["act_read"], n)
                    m = (p - 1) % 2 if half == 1 else p % 2
                    for ii in range(2):
                        i = 2 * c + ii
                        mm = nc.tensor.matmul(o[:, ii * D:(ii + 1) * D], cts[:, i * P:(i + 1) * P], C.woT[:, m, :],
                                              start=True, stop=True)
                mm.then_inc(S["filled"], 1)

            def each(part, u):
                for pos, x in items(part):
                    jj = j_of(part, pos)
                    p, j = u + jj // 4, jj % 4
                    if x[0] == "bank":
                        bank_item(part, u, pos, x)
                    elif x[0] == "unit":
                        _, kt, hp = x
                        b3 = quad_buffer(u, jj)
                        n = plan.base(part, u, "unit") + plan.count(part, "unit", pos)
                        if kt == 0 and hp == 0:
                            pe.wait_ge(S["shift_in"], (p * 4 + j + 1) * 16 * PARTS)
                        if not (isinstance(n, int) and n < 2):
                            pe.wait_ge(S["exp_done"], n - 1)
                        lo = first_col(j, kt)
                        diagonal = causal and kt * P >= (j % 2) * HALF
                        for hh in range(2):
                            h = 2 * hp + hh
                            o = ps_s[:, hp, hh, :]
                            mm = nc.tensor.matmul(o[:, lo:HALF], kst[:, b3, h, kt * P:(kt + 1) * P],
                                                  qst[:, b3, j % 2, h, lo:HALF], start=True, stop=not diagonal)
                            if diagonal:
                                mm = nc.tensor.matmul(o[:, lo:lo + P], C.identb[:], C.block_kq[:],
                                                      start=False, stop=True)
                        mm.then_inc(S["st_filled"], 1)
                    elif x[0] == "values_in":
                        kt = x[1]
                        n = plan.base(part, u, "values_in") + plan.count(part, "values_in", pos)
                        if kt == 0:
                            g = p * 4 + j
                            wait_past(pe, S["evacuated"], g)
                            if j % 2 == 0:
                                pe.wait_ge(S["v_ready"], p * 2 + j // 2 + 1)
                        pe.wait_ge(S["exp_done"], n * 2 + 2)
                        lo = first_col(j, kt)
                        for h in range(QH):
                            mm = nc.tensor.matmul(ps_c[SLOT * h:SLOT * (h + 1), lo:HALF],
                                                  v[:, j // 2, kt, h, :], pt[:, kt % 2, h, lo:HALF],
                                                  start=(kt == 0), stop=(kt == key_tiles(causal, j) - 1))
                        mm.then_inc(S["pv_done"], 1)
            over_parts(pe, each)

        @block.scalar
        def _(act):
            def each(part, u):
                for pos, x in items(part):
                    jj = j_of(part, pos)
                    p, j = u + jj // 4, jj % 4
                    if x[0] == "unit":
                        _, kt, hp = x
                        n = plan.base(part, u, "unit") + plan.count(part, "unit", pos)
                        act.wait_ge(S["st_filled"], n + 1)
                        if hp == 0:
                            m = plan.base(part, u, "values_in") + sum(key_tiles(causal, i) for i in range(jj)) + kt
                            if not (isinstance(m, int) and m < 2):
                                act.wait_ge(S["pv_done"], m - 1)
                        lo = first_col(j, kt)
                        nc.scalar.activation(pt[:, kt % 2, 2 * hp:2 * hp + 2, lo:HALF], ps_s[:, hp, :, lo:HALF],
                                             ACT.Exp).then_inc(S["exp_done"], 1)
                    elif x[0] == "bank" and x[3] == "act":
                        bank = plan.bank_of(part, pos)
                        n = plan.base(part, u, "bank") + plan.count(part, "bank", pos)
                        act.wait_ge(S["filled"], n + 1)
                        if x[1] == "project":
                            qk, half = x[2]
                            up = 0 if part == "start" else p + 1
                            if half == 0 and not (isinstance(up, int) and up == 0):
                                act.wait_ge(S["split_lo"], up * 2 - 1 + qk)
                            sc, bi = 1.0, 0.0
                            col = bass.ts(up, 1)
                            if causal:
                                bi = (G.qbias if qk == 0 else G.kbias)[:, col]
                                if qk == 0:
                                    sc = G.qscale[:, col]
                            elif qk == 0:
                                sc = 1.0 / 16.0
                            nc.scalar.activation(q32[:, qk, half * HALF:(half + 1) * HALF], ps_m[:, bank, :],
                                                 ACT.Identity, scale=sc, bias=bi).then_inc(S["act_read"], 1)
                        else:
                            nc.scalar.copy(cts[:], ps_m[:, bank, :]).then_inc(S["act_read"], 1)
                    elif x[1] == "weight":
                        g = 0 if part == "start" else p * 4 + j + 1
                        act.wait_ge(S["maxima"], g + 1)
                        nc.scalar.activation(wexp[:, x[2]], wlog[:, x[2]], ACT.Exp).then_inc(S["weights"], 1)
                    elif x[1] == "evacuate":
                        g = p * 4 + j
                        n = plan.base(part, u, "values_in") + plan.count(part, "values_in", pos)
                        act.wait_ge(S["pv_done"], n)
                        if not (isinstance(g, int) and g < 2):
                            act.wait_ge(S["dve_read"], plan.read(part, pos, u, "ctx", (j - 2) % 4))
                        nc.scalar.copy(ctxs[:, j % 2, :], ps_c[:]).then_inc(S["evacuated"], 1)
            over_parts(act, each)

        def dve_program(dve, part, u, link):
            for pos, x in items(part):
                jj = j_of(part, pos)
                p, j = u + jj // 4, jj % 4
                kind, arg = x[1], x[2] if len(x) > 2 else None
                if x[0] not in ("bank", "step") or x[3] != "dve":
                    continue
                if x[0] == "bank":
                    bank = plan.bank_of(part, pos)
                    n = plan.base(part, u, "bank") + plan.count(part, "bank", pos)
                    dve.wait_ge(S["filled"], n + 1)
                    o = ps_m[:, bank, :]
                done = S["dve_read"]
                if kind == "smax":
                    js, h, i, c = arg
                    t = (js % 2) * TH + i
                    keys = min(HALF, (t + 1) * P - c * HALF) if causal else HALF
                    nc.vector.tensor_reduce(part_max[:, js % 2, h, i, c:c + 1], o[:, 0:keys], AX_X,
                                            ALU.max).then_inc(done, 1)
                elif kind == "combine":
                    g = 0 if part == "start" else p * 4 + j + 1
                    n = plan.base(part, u, "dve bank") + plan.count(part, "dve bank", pos)
                    dve.wait_ge(done, n)
                    pm = part_max[:, arg % 2]
                    if not causal:
                        link(nc.vector.tensor_tensor(mx[:], pm[:, :, :, 0], pm[:, :, :, 1], ALU.max))
                        nc.vector.tensor_scalar(nmax[:, arg % 2], mx[:], -1.0, None, ALU.mult).then_inc(S["maxima"], 1)
                        continue
                    up = 0 if part == "start" else p + 1 if j == 3 else p
                    heads = G.gneg[:, bass.ds(up * HP + (arg // 2) * QH, QH)]
                    tiles = C.lastrow[:, (arg % 2) * TH:(arg % 2 + 1) * TH]
                    link(nc.vector.tensor_tensor(cneg[:], heads.unsqueeze(2).broadcast_to([P, QH, TH]),
                                                 tiles.unsqueeze(1).broadcast_to([P, QH, TH]), ALU.mult))
                    if arg % 2 == 1:
                        link(nc.vector.tensor_tensor(mx[:], pm[:, :, :, 0], pm[:, :, :, 1], ALU.max))
                        link(nc.vector.tensor_tensor(mx[:], mx[:], cneg[:], ALU.max))
                    else:
                        link(nc.vector.tensor_tensor(mx[:], pm[:, :, :, 0], cneg[:], ALU.max))
                    nc.vector.tensor_scalar(nmax[:, arg % 2], mx[:], -1.0, None, ALU.mult)
                    nc.vector.tensor_tensor(wlog[:, arg], cneg[:], mx[:], ALU.subtract).then_inc(S["maxima"], 1)
                elif kind == "shift":
                    g = 0 if part == "start" else p * 4 + j + 1
                    if not (isinstance(g, int) and g < 2):
                        dve.wait_ge(S["shift_in"], (g - 1) * 16 * PARTS)
                    mp = mparts[:, arg % 2]
                    src = ps_m[0:QH * TH, bank, 0:P]
                    link(nc.vector.tensor_copy(mp[:, 0, :], src))
                    nc.vector.tensor_tensor(mrest[:], src, mp[:, 0, :], ALU.subtract).then_inc(done, 1)
                    dve.wait_ge(done, plan.base(part, u, "dve bank") + plan.count(part, "dve bank", pos) + 1)
                    link(nc.vector.tensor_copy(mp[:, 1, :], mrest[:]))
                    nc.vector.tensor_tensor(mp[:, 2, :], mrest[:], mp[:, 1, :], ALU.subtract).then_inc(S["parts_ready"], 1)
                elif kind == "split_hi":
                    up = 0 if part == "start" else p + 1
                    n = plan.base(part, u, "act bank") + plan.count(part, "act bank", pos)
                    dve.wait_ge(S["act_read"], n)
                    if not (isinstance(up, int) and up == 0):
                        dve.wait_ge(S["scratch_out"], up * WRITES * 16)
                    nc.vector.tensor_copy(parts[:, arg, 0, :], q32[:, arg, :]).then_inc(S["split_hi"], 1)
                elif kind == "split_mid":
                    up = 0 if part == "start" else p + 1
                    dve.wait_ge(S["rest_1"], up * 2 + arg + 1)
                    nc.vector.tensor_copy(parts[:, arg, 1, :], q32[:, arg, :]).then_inc(S["split_mid"], 1)
                elif kind == "values":
                    up = 0 if part == "start" else p + 1
                    if arg == 0 and not (isinstance(up, int) and up == 0):
                        dve.wait_ge(S["v_ready"], up * 2)
                    dst = vnew[:, arg * TH:(arg + 1) * TH, :]
                    src = o.rearrange("p (i c) -> p i c", i=TH)
                    if causal:
                        bv = C.bv[:, bass.ts(up % 2, P)].unsqueeze(1).broadcast_to([P, TH, P])
                        nc.vector.tensor_tensor(dst, src, bv, ALU.add).then_inc(done, 1)
                    else:
                        nc.vector.tensor_copy(dst, src).then_inc(done, 1)
                elif kind == "masked":
                    g = p * 4 + j - 1
                    dve.wait_ge(S["weights"], g + 1)
                    src = o.rearrange("p (i h c) -> p i h c", i=TH, h=QH)[:, :, :, 0:HD + 1]
                    wt = wexp[:, arg].rearrange("p h i -> p i h").unsqueeze(3).broadcast_to([P, TH, QH, HD + 1])
                    nc.vector.tensor_tensor(wsum[:], src, wt, ALU.mult).then_inc(done, 1)
                    dve.wait_ge(done, plan.base(part, u, "dve bank") + plan.count(part, "dve bank", pos) + 1)
                elif kind == "ctx":
                    src = o.rearrange("p (i h c) -> p i h c", i=TH, h=QH)
                    if not (part == "first" and arg == 0):
                        dve.wait_ge(done, plan.read(part, pos, u, "ctx", (arg - 1) % 4))
                    if causal:
                        link(nc.vector.tensor_tensor(num[:], src[:, :, :, 0:HD + 1], wsum[:], ALU.add))
                        src = num
                    link(nc.vector.reciprocal(rden[:], src[:, :, :, ONE]))
                    rb = rden[:].unsqueeze(3).broadcast_to([P, TH, QH, HD])
                    if causal:
                        dst = ctok[:, arg % 2, :, (arg // 2) * 64:(arg // 2 + 1) * 64].rearrange(
                            "p i (h c) -> p i h c", h=QH)
                        nc.vector.tensor_tensor(dst, num[:, :, :, 0:HD], rb, ALU.mult).then_inc(done, 1)
                    else:
                        g = p * 4 + j - 1
                        if not (isinstance(g, int) and g < 2):
                            dve.wait_ge(S["added"], g - 1)
                        nc.vector.tensor_tensor(tmp[:, arg % 2], src[:, :, :, 0:HD], rb, ALU.mult).then_inc(done, 1)
                elif kind == "out":
                    half, c = arg
                    up = p - 1 if half == 1 else p
                    rows = xs[:, bass.ds(up // 2 * T + half * TH + 2 * c, 2), :]
                    nc.vector.tensor_tensor(rows, o.rearrange("p (i d) -> p i d", i=2), rows, ALU.add).then_inc(done, 1)

        @block.vector
        def _(dve):
            def links_in(part):
                n = 0
                for _, x in items(part):
                    if x[0] in ("bank", "step") and x[1] == "combine":
                        n += 2 + x[2] % 2 if causal else 1
                    elif x[0] == "bank" and x[1] == "shift":
                        n += 2
                    elif x[0] == "bank" and x[1] == "ctx":
                        n += 2 if causal else 1
                return n
            per = {k: links_in(k) for k in plan.parts}
            in_loop = (NPAIR - 1 - TAIL) // STEP * per["loop"]

            def each(part, u):
                base = {"start": 0, "first": per["start"],
                        "loop": per["start"] + per["first"] + (u - 1) * (per["loop"] // STEP),
                        "last": per["start"] + per["first"] + in_loop,
                        "end": per["start"] + per["first"] + in_loop + per["last"]}[part]
                link = Links(dve, S["linked"], base)
                dve_program(dve, part, u, link)
                assert link.n == per[part], (part, link.n, per[part])
            nc.vector.memset(kst[KS:KS + PARTS], 1.0).then_inc(S["shift_ones"], 1)
            over_parts(dve, each)

        @block.gpsimd
        def _(pool):
            nc.gpsimd.memset(v[:], 0.0).then_inc(S["pool_linked"], 1)
            pool.wait_ge(S["pool_linked"], 1)
            ins = nc.gpsimd.memset(v[:, :, :, :, ONE:ONE + 1], 1.0)
            if causal:
                ins.then_inc(S["pool_linked"], 1)
                pool.wait_ge(S["pool_linked"], 2)
                ins = nc.gpsimd.memset(vsum[:, :, T - 1], 0.0)
            ins.then_inc(S["ones_ready"], 1)
            pool.wait_ge(S["ones_ready"], 1)

            def split(up):
                for qk in range(2):
                    pool.wait_ge(S["split_hi"], up * 2 + qk + 1)
                    nc.gpsimd.tensor_tensor(q32[:, qk, :], q32[:, qk, :], parts[:, qk, 0, :],
                                            ALU.subtract).then_inc(S["rest_1"], 1)
                    pool.wait_ge(S["split_mid"], up * 2 + qk + 1)
                    nc.gpsimd.tensor_tensor(parts[:, qk, 2, :], q32[:, qk, :], parts[:, qk, 1, :],
                                            ALU.subtract).then_inc(S["split_lo"], 1)

            def copy_v(up, n, vals, free):
                pool.wait_ge(S["dve_read"], vals)
                if free is not None:
                    pool.wait_ge(S["pv_done"], free[0])
                    pool.wait_ge(S["filled"], free[1])
                pool.sem_inc(S["pool_passed"], 1)
                src = vnew[:].rearrange("p t (n h c) -> p n t h c", n=2, h=QH)[:, n]
                nc.gpsimd.tensor_copy(v[:, n, :, :, 0:HD], src).then_inc(S["v_ready"], 1)
                if causal:
                    pool.wait_ge(S["v_ready"], up * 2 + n + 1)
                    for i in range(T - 2, -1, -1):
                        ins = nc.gpsimd.tensor_tensor(vsum[:, n, i], vsum[:, n, i + 1], v[:, n, i + 1], ALU.add)
                        if i:
                            ins.then_inc(S["pool_linked"], 1)
                            pool.wait_ge(S["pool_linked"], 2 + (up * 2 + n) * (T - 2) + (T - 1 - i))
                        else:
                            ins.then_inc(S["vsum_ready"], 1)

            def turned(p, j):
                return in_pair(p + 1 if j == 3 else p, "masked" if causal else "ctx", j, "bank")

            def add(p, j):
                if isinstance(p, int) and p == NPAIR - 1 and j == 3:
                    n = plan.base("end", NPAIR, "dve bank") + plan.count("end", "dve bank")
                else:
                    n = in_pair(p + 1 if j == 3 else p, "ctx", j, "dve bank")
                pool.wait_ge(S["dve_read"], n)
                rows = xs[:, bass.ds(p // 2 * T + (j % 2) * TH, TH), bass.ds(p % 2 * P + (j // 2) * 64, 64)]
                nc.gpsimd.tensor_tensor(rows, rows, tmp[:, j % 2].rearrange("p i h c -> p i (h c)"),
                                        ALU.add).then_inc(S["added"], 1)

            vals = plan.count("start", "dve bank", 1 + max(
                i for i, x in enumerate(plan.flat["start"]) if x[1] == "values"))
            split(0)
            copy_v(0, 0, vals, None)
            copy_v(0, 1, vals, None)

            def each(p, last=False):
                if not (isinstance(p, int) and p == 0):
                    if not causal:
                        add(p - 1, 3)
                    copy_v(p, 1, in_pair(p - 1, "values", 1, "dve bank"), (p * NV, turned(p - 1, 3)))
                if not last:
                    split(p + 1)
                for j in range(3):
                    if not causal:
                        add(p, j)
                    if j == 1 and not last:
                        done = p * NV + sum(key_tiles(causal, i) for i in range(2))
                        copy_v(p + 1, 0, in_pair(p, "values", 1, "dve bank"), (done, turned(p, 1)))

            each(0)
            with pool.Fori(1, NPAIR - 1) as u:
                each(u)
            each(NPAIR - 1, True)
            if not causal:
                add(NPAIR - 1, 3)


def ffn_phase(nc, sem, C, dram, tag, out=None):
    xs = C.xs

    def routed(scratch, b):
        return scratch[b % 2][0:KEEP, :].rearrange("(t p) d -> p t d", p=P)
    names = ["loaded", "stats_linked", "norm_linked", "rank_linked", "stats", "logged", "rstd", "scales", "h_ready", "h_added",
             "scored", "spread", "row_filled", "counted", "sigmoid", "places", "scattered", "routed_in", "turned",
             "ht_read", "hidden", "gelu", "product", "biased", "routed_out", "sources", "gathered", "updated", "sent",
             "zeroed", "pool_passed"]
    S = {n: sem(tag + n) for n in names}
    with ExitStack() as ctx:
        def sb(name, shape, dt=F32):
            return ctx.enter_context(nc.sbuf_tensor(tag + name, shape, dt))
        W1 = sb("W1", [P, KD, F])
        W2 = sb("W2", [P, FT, D])
        h = sb("h", [P, 2, T, D])
        hr = sb("hr", [P, TK, D])
        ht = sb("ht", [P, KD, KEEP])
        gt = sb("gt", [P, FT, KEEP])
        st = sb("st", [P, T, 6])
        var, msum, r0, lnv, t1, rs, nmr = (sb(n, [P, T]) for n in ("var", "msum", "r0", "lnv", "t1", "rs", "nmr"))
        score = sb("score", [P, T])
        spread = sb("spread", [P, T, P])
        hw = sb("hw", [P, T, D])
        above = sb("above", [P, T, L], BF16)
        equal = sb("equal", [P, T, P], BF16)
        cnt = sb("cnt", [P, T, 3])
        rank = sb("rank", [P, B, T])
        sig = sb("sig", [P, T])
        coef = sb("coef", [P, B, T])
        place = sb("place", [P, 2, T], U32)
        source = sb("source", [P, 2, T], U32)
        biased = sb("biased", [P, TK, D])
        back = sb("back", [P, T, D])
        zeros = sb("zeros", [1, D])
        ps_h = ctx.enter_context(nc.psum_tensor(tag + "ps_h", [P, 2, HALF], F32))
        ps_o = ctx.enter_context(nc.psum_tensor(tag + "ps_o", [P, 2, HALF], F32))
        ps_t = ctx.enter_context(nc.psum_tensor(tag + "ps_t", [P, 2, HALF], F32))
        ps_r = ctx.enter_context(nc.psum_tensor(tag + "ps_r", [P, L], F32))
        h_rows, y_rows = ([nc.dram_tensor(f"{tag}{name}{i}", (n, D), F32, kind="Internal").ap() for i in range(2)]
                          for name, n in (("h_rows", L), ("y_rows", KEEP + 1)))
        block = ctx.enter_context(nc.Block())

        def over_batches(eng, step, begin=None):
            if begin is not None:
                begin()
            step(0, 0)
            with eng.Fori(1, B - 4, 2) as b:
                step(b, 1)
                step(b + 1, 0)
            for b in range(B - 3, B):
                step(b, b % 2, B - 1 - b)

        @block.sync
        def _(sp):
            def load_routed(b):
                sp.wait_ge(S["scattered"], (b + 1) * 16 * T)
                wait_past(sp, S["turned"], b * KD)
                sp.dma_start(hr[:], routed(h_rows, b)).then_inc(S["routed_in"], 16)

            def begin():
                sp.dma_start(W1[:], dram["W1"].rearrange("(k p) f -> p k f", p=P)).then_inc(S["loaded"], 16)
                sp.dma_start(W2[:], dram["W2"].rearrange("(f p) d -> p f d", p=P)).then_inc(S["loaded"], 16)
                sp.wait_ge(S["zeroed"], 1)
                for rows in y_rows:
                    sp.dma_start(rows[KEEP:KEEP + 1, :], zeros[:]).then_inc(S["loaded"], 16)
                sp.wait_ge(S["loaded"], 64)
                load_routed(0)

            def send(b):
                sp.wait_ge(S["updated"], (b + 1) * T)
                sp.dma_start(out[b].rearrange("(t p) d -> p t d", p=P),
                             xs[:, b * T:(b + 1) * T, :]).then_inc(S["sent"], 16)

            begin()
            for b in range(B):
                if b + 1 < B:
                    load_routed(b + 1)
                sp.wait_ge(S["biased"], (b + 1) * TK)
                wait_past(sp, S["gathered"], (b - 1) * 16 * T)
                sp.dma_start(routed(y_rows, b), biased[:]).then_inc(S["routed_out"], 16)
                if out is not None and b:
                    send(b - 1)
            sp.wait_ge(S["routed_in"], B * 16)
            sp.wait_ge(S["routed_out"], B * 16)
            if out is not None:
                send(B - 1)
                sp.wait_ge(S["sent"], 16 * B)

        @block.vector
        def _(dve):
            def variances(b):
                link = Links(dve, S["stats_linked"], b * 3)
                for t in range(T):
                    ins = nc.vector.bn_stats(st[:, t, :], xs[:, b * T + t, :])
                link(ins)
                nc.vector.tensor_tensor(msum[:], st[:, :, 1], st[:, :, 4], ALU.add)
                nc.vector.tensor_tensor(t1[:], st[:, :, 1], st[:, :, 4], ALU.subtract)
                link(nc.vector.tensor_tensor(var[:], st[:, :, 2], st[:, :, 5], ALU.add))
                link(nc.vector.scalar_tensor_tensor(t1[:], t1[:], 0.25, t1[:], ALU.mult, ALU.mult))
                nc.vector.scalar_tensor_tensor(var[:], var[:], 1.0 / D, t1[:], ALU.mult, ALU.add).then_inc(
                    S["stats"], 1)

            def scales(b):
                link = Links(dve, S["norm_linked"], b * 3)
                dve.wait_ge(S["rstd"], b + 1)
                dve.wait_ge(S["stats"], b + 1)
                link(nc.vector.scalar_tensor_tensor(t1[:], r0[:], -0.5, r0[:], ALU.mult, ALU.mult))
                link(nc.vector.scalar_tensor_tensor(t1[:], var[:], EPS, t1[:], ALU.add, ALU.mult))
                link(nc.vector.scalar_tensor_tensor(rs[:], t1[:], 1.5, r0[:], ALU.add, ALU.mult))
                nc.vector.scalar_tensor_tensor(nmr[:], msum[:], -0.5, rs[:], ALU.mult, ALU.mult).then_inc(
                    S["scales"], 1)

            def score_tokens(b, par):
                for t in range(T):
                    dve.wait_ge(S["h_ready"], b * T + t + 1)
                    ins = nc.vector.tensor_tensor_reduce(hw[:, t, :], h[:, par, t, :], C.wr[:], 1.0, 0.0, ALU.mult,
                                                         ALU.add, score[:, t:t + 1])
                ins.then_inc(S["scored"], 1)
                dve.wait_ge(S["scored"], b + 1)
                nc.vector.tensor_copy(spread[:], score[:].unsqueeze(2).broadcast_to([P, T, P])).then_inc(
                    S["spread"], 1)

            def count_above(b, t):
                if t == 0:
                    dve.wait_ge(S["row_filled"], b + 1)
                s = score[:, t:t + 1]
                if t:
                    nc.vector.tensor_scalar(above[:, t, 0:t * P], ps_r[:, 0:t * P], s, None, ALU.is_ge, ALU.add,
                                            accum_out=cnt[:, t, 0:1])
                nc.vector.tensor_scalar(above[:, t, t * P:L], ps_r[:, t * P:L], s, None, ALU.is_gt, ALU.add,
                                        accum_out=cnt[:, t, 1:2])
                ins = nc.vector.scalar_tensor_tensor(equal[:, t, :], ps_r[:, t * P:(t + 1) * P], s, C.tri[:],
                                                     ALU.is_equal, ALU.mult, accum_out=cnt[:, t, 2:3])
                if t == T - 1:
                    ins.then_inc(S["counted"], 1)

            def coefficients(b, par):
                link = Links(dve, S["rank_linked"], b * 2)
                dve.wait_ge(S["counted"], b + 1)
                rk = rank[:, bass.ds(b, 1), :].rearrange("p o t -> p (o t)")
                link(nc.vector.tensor_tensor(rk, cnt[:, :, 0], cnt[:, :, 1], ALU.add))
                link(nc.vector.tensor_tensor(rk, rk, cnt[:, :, 2], ALU.add))
                wait_past(dve, S["scattered"], (b - 1) * 16 * T)
                nc.vector.tensor_scalar(place[:, par, :], rk, 1.0, None, ALU.mult)
                dve.wait_ge(S["sigmoid"], b + 1)
                nc.vector.scalar_tensor_tensor(coef[:, bass.ds(b, 1), :].rearrange("p o t -> p (o t)"), rk,
                                               KEEP - 0.5, sig[:], ALU.is_lt, ALU.mult).then_inc(S["places"], 1)

            def sources(b, par):
                rk = rank[:, bass.ds(b, 1), :].rearrange("p o t -> p (o t)")
                nc.vector.tensor_scalar(source[:, par, :], rk, float(KEEP), None, ALU.min).then_inc(S["sources"], 1)

            def add_bias(b, t):
                dve.wait_ge(S["product"], b * TK + t + 1)
                if t == 0:
                    wait_past(dve, S["routed_out"], b * 16)
                nc.vector.tensor_tensor(biased[:, t, :], ps_o[:, t % 2, 0:D], C.b2[:], ALU.add).then_inc(
                    S["biased"], 1)

            def update(b):
                dve.wait_ge(S["gathered"], (b + 1) * 16 * T)
                dve.wait_ge(S["h_added"], b + 1)
                dve.wait_ge(S["places"], b + 1)
                for t in range(T):
                    rows = xs[:, b * T + t, :]
                    nc.vector.scalar_tensor_tensor(
                        rows, back[:, t, :], coef[:, bass.ds(b, 1), t:t + 1].rearrange("p o t -> p (o t)"), rows,
                        ALU.mult, ALU.add).then_inc(S["updated"], 1)

            def begin():
                nc.vector.memset(cnt[:, 0, 0:1], 0.0)
                nc.vector.memset(zeros[:], 0.0).then_inc(S["zeroed"], 1)
                dve.wait_ge(S["zeroed"], 1)
                variances(0)
                for b in range(2):
                    scales(b)
                    score_tokens(b, b)
                    for t in range(T):
                        count_above(b, t)
                    variances(b + 1)
                    coefficients(b, b)
                scales(2)

            def step(b, par, ahead=3):
                sources(b, par)
                if ahead >= 2:
                    score_tokens(b + 2, par)
                if ahead >= 3:
                    variances(b + 3)
                for t in range(T):
                    if ahead >= 2:
                        count_above(b + 2, t)
                    if t % 2 == 1:
                        add_bias(b, t // 2)
                if ahead >= 2:
                    coefficients(b + 2, par)
                if ahead >= 3:
                    scales(b + 3)
                if not (isinstance(b, int) and b == 0):
                    update(b - 1)
            over_batches(dve, step, begin)
            update(B - 1)

        @block.scalar
        def _(act):
            def inverse_roots(b):
                act.wait_ge(S["stats"], b + 1)
                nc.scalar.activation(lnv[:], var[:], ACT.Ln, bias=C.eps[:]).then_inc(S["logged"], 1)
                act.wait_ge(S["logged"], b + 1)
                nc.scalar.activation(r0[:], lnv[:], ACT.Exp, scale=-0.5).then_inc(S["rstd"], 1)

            def normalise(b, par, t):
                if t == 0:
                    act.wait_ge(S["scales"], b + 1)
                    wait_past(act, S["scattered"], (b - 1) * 16 * T)
                    wait_past(act, S["h_added"], b - 1)
                nc.scalar.activation(h[:, par, t, :], xs[:, b * T + t, :], ACT.Identity, scale=rs[:, t:t + 1],
                                     bias=nmr[:, t:t + 1]).then_inc(S["h_ready"], 1)

            def read_turned(b):
                for k in range(KD):
                    act.wait_ge(S["turned"], b * KD + k + 1)
                    nc.scalar.copy(ht[:, k, :], ps_t[:, k, :]).then_inc(S["ht_read"], 1)

            def sigmoids(b):
                act.wait_ge(S["scored"], b + 1)
                wait_past(act, S["places"], b)
                nc.scalar.activation(sig[:], score[:], ACT.Sigmoid).then_inc(S["sigmoid"], 1)

            def begin():
                inverse_roots(0)
                for b in range(2):
                    for t in range(T):
                        normalise(b, b, t)
                    sigmoids(b)
                    inverse_roots(b + 1)
                read_turned(0)

            def step(b, par, ahead=3):
                for f in range(FT):
                    act.wait_ge(S["hidden"], b * FT + f + 1)
                    if f == 0:
                        wait_past(act, S["product"], b * TK)
                    nc.scalar.activation(gt[:, f, :], ps_h[:, f % 2, :], ACT.Gelu_apprx_tanh,
                                         bias=C.b1[:, f:f + 1]).then_inc(S["gelu"], 1)
                    if ahead >= 2:
                        normalise(b + 2, par, f)
                if ahead >= 2:
                    sigmoids(b + 2)
                if ahead >= 3:
                    inverse_roots(b + 3)
                if ahead >= 1:
                    read_turned(b + 1)
            over_batches(act, step, begin)

        @block.tensor
        def _(pe):
            pe.wait_ge(S["loaded"], 64)

            def turn(b):
                pe.wait_ge(S["routed_in"], (b + 1) * 16)
                wait_past(pe, S["ht_read"], b * KD)
                for k in range(KD):
                    for t in range(TK):
                        mm = nc.tensor.transpose(ps_t[:, k, t * P:(t + 1) * P], hr[:, t, k * P:(k + 1) * P],
                                                 C.ident[:])
                    mm.then_inc(S["turned"], 1)

            def score_rows(b):
                pe.wait_ge(S["spread"], b + 1)
                wait_past(pe, S["places"], b)
                for t in range(T):
                    mm = nc.tensor.transpose(ps_r[:, t * P:(t + 1) * P], spread[:, t, :], C.ident[:])
                mm.then_inc(S["row_filled"], 1)

            def begin():
                score_rows(0)
                score_rows(1)
                turn(0)

            def step(b, par, ahead=3):
                pe.wait_ge(S["ht_read"], (b + 1) * KD)
                for f in range(FT):
                    wait_past(pe, S["gelu"], b * FT + f - 1 if f >= 2 else b * FT)
                    for k in range(KD):
                        mm = nc.tensor.matmul(ps_h[:, f % 2, :], W1[:, k, f * P:(f + 1) * P], ht[:, k, :],
                                              start=(k == 0), stop=(k == KD - 1))
                    mm.then_inc(S["hidden"], 1)
                if ahead >= 2:
                    score_rows(b + 2)
                pe.wait_ge(S["gelu"], (b + 1) * FT)
                for t in range(TK):
                    if t == TK - 1 and ahead >= 1:
                        turn(b + 1)
                    wait_past(pe, S["biased"], b * TK + t - 1 if t >= 2 else b * TK)
                    for f in range(FT):
                        mm = nc.tensor.matmul(ps_o[:, t % 2, 0:D], gt[:, f, t * P:(t + 1) * P],
                                              W2[:, f, :], start=(f == 0), stop=(f == FT - 1))
                    mm.then_inc(S["product"], 1)
            over_batches(pe, step, begin)

        @block.gpsimd
        def _(pool):
            def scatter(b, par):
                pool.wait_ge(S["h_ready"], b * T + T)
                wait_past(pool, S["scattered"], b * 16 * T)
                pool.wait_ge(S["places"], b + 1)
                wait_past(pool, S["routed_in"], (b - 1) * 16)
                pool.sem_inc(S["pool_passed"], 1)
                for t in range(T):
                    nc.gpsimd.indirect_dma_start(h_rows[par], bass.IndirectOffsetOnAxis(place[:, par, t:t + 1], 0),
                                                 h[:, par, t, :], None).then_inc(S["scattered"], 16)

            def add_h(b, par):
                rows = xs[:, bass.ts(b, T), :]
                nc.gpsimd.tensor_tensor(rows, rows, h[:, par], ALU.add).then_inc(S["h_added"], 1)

            def gather(b, par):
                wait_past(pool, S["gathered"], b * 16 * T)
                pool.wait_ge(S["sources"], b + 1)
                wait_past(pool, S["updated"], b * T)
                pool.wait_ge(S["routed_out"], (b + 1) * 16)
                pool.sem_inc(S["pool_passed"], 1)
                for t in range(T):
                    nc.gpsimd.indirect_dma_start(back[:, t, :], None, y_rows[par],
                                                 bass.IndirectOffsetOnAxis(source[:, par, t:t + 1], 0)
                                                 ).then_inc(S["gathered"], 16)

            def begin():
                pool.wait_ge(S["loaded"], 64)
                for b in range(2):
                    scatter(b, b)
                    add_h(b, b)

            def step(b, par, ahead=3):
                if ahead >= 2:
                    scatter(b + 2, par)
                gather(b, par)
                if ahead >= 2:
                    add_h(b + 2, par)
            over_batches(pool, step, begin)


class Shared:
    pass


def program(nc, dram, out):
    nc.disable_value_cache = True
    with ExitStack() as ctx:
        def sb(name, shape, dt=F32):
            return ctx.enter_context(nc.sbuf_tensor(name, shape, dt))

        def sem(name):
            return ctx.enter_context(nc.semaphore(name))

        C, G = Shared(), Shared()
        C.xs = sb("xs", [P, B * T, D])
        C.ident = sb("ident", [P, P])
        C.identb = sb("identb", [P, P], BF16)
        C.ones = sb("ones", [P, P])
        C.zerosb = sb("zerosb", [P, P], BF16)
        C.tri = sb("tri", [P, P])
        C.block_qk = sb("block_qk", [P, P], BF16)
        C.block_kq = sb("block_kq", [P, P], BF16)
        C.lastrow = sb("lastrow", [P, T])
        C.eps = sb("eps", [P, 1])
        C.bo = sb("bo", [P, D])
        C.bv = sb("bv", [P, D])
        C.woT = sb("woT", [P, KD, D])
        C.wr = sb("wr", [P, D])
        C.b1 = sb("b1", [P, FT])
        C.b2 = sb("b2", [P, D])
        G.xsum = sb("xsum", [P, KD, B])
        G.gneg = sb("gneg", [P, B * H])
        G.qscale = sb("qscale", [P, NPAIR])
        G.qbias = sb("qbias", [P, NPAIR])
        G.kbias = sb("kbias", [P, NPAIR])
        C.ht_dram = nc.dram_tensor("ht_scratch", (B, P, KD, L), F32, kind="Internal").ap()
        C.g_dram = nc.dram_tensor("g_scratch", (B, H), F32, kind="Internal").ap()

        constants_phase(nc, sem, C, dram)
        norm_phase(nc, sem, C, "n0_", x_in=dram["x"], gates=G)
        gates_phase(nc, sem, C, G, dram)
        attention_phase(nc, sem, C, G, dram, True)
        ffn_phase(nc, sem, C, dram, "f1_")
        norm_phase(nc, sem, C, "n1_")
        attention_phase(nc, sem, C, G, dram, False)
        ffn_phase(nc, sem, C, dram, "f2_", out)


def layout(inputs):
    import numpy as np
    a = {k: np.asarray(v) for k, v in inputs.items()}
    at = lambda n: a["L0_attn_a_" + n]
    c = np.ascontiguousarray

    def per_pair(ws):
        w = np.stack([x.reshape(KD, P, KD, P) for x in ws])
        return c(w.transpose(3, 2, 0, 1, 4))
    wqkv = a["L0_attn_b_w_qkv"]
    return {
        "x": c(at("x")), "bo": at("bo"), "bv": at("bv"), "bq": at("bq"), "bk": at("bk"),
        "woT": c(at("wo").T),
        "wpairA": per_pair([at("wq").T, at("wk").T, at("wv").T]),
        "wpairB": per_pair([wqkv[:, 0:D], wqkv[:, D:2 * D], wqkv[:, 2 * D:3 * D]]),
        "gw1": c(np.concatenate([at("pw1"), at("sw1")[None]]).transpose(2, 0, 1)),
        "gb1": c(np.concatenate([at("pb1"), at("sb1")[None]])),
        "gw2": c(np.concatenate([at("pw2").reshape(NE * H, DH), at("sw2")]).T),
        "gb2": c(np.concatenate([at("pb2").reshape(NE * H), at("sb2")])),
        "wr": a["L0_ffn_w_router"], "W1": a["L0_ffn_W1"], "b1": a["L0_ffn_b1"],
        "W2": a["L0_ffn_W2"], "b2": a["L0_ffn_b2"],
    }


def kernel(**inputs):
    import concourse.bacc as bacc
    from concourse.bass_utils import run_bass_kernel_spmd

    nc = bacc.Bacc("TRN2", target_bir_lowering=False, num_devices=1)
    arrays = {f"in_{k}": v for k, v in layout(inputs).items()}
    dram = {k[3:]: nc.dram_tensor(k, v.shape, mybir.dt.from_np(v.dtype), kind="ExternalInput").ap()
            for k, v in arrays.items()}
    out = nc.dram_tensor("out_dram", (B, L, D), F32, kind="ExternalOutput").ap()
    program(nc, dram, out)
    return run_bass_kernel_spmd(nc, [arrays], core_ids=[0]).results[0]["out_dram"]
```
